# Optimizing a Trainium2 kernel written in Bass

```python
import numpy as np
import jax
import jax.numpy as jnp

def _softmax(x, axis=-1):
    return jax.nn.softmax(x, axis=axis)

def _gelu(x):
    return jax.nn.gelu(x, approximate=True)

def _silu(x):
    return jax.nn.silu(x)

def _sigmoid(x):
    return jax.nn.sigmoid(x)

def _layernorm(x, axis=-1, eps=1e-05):
    m = jnp.mean(x, axis=axis, keepdims=True)
    v = jnp.var(x, axis=axis, keepdims=True)
    return (x - m) / jnp.sqrt(v + eps)

def _scatter_add(tgt, idx, src, axis=0):
    return tgt.at[idx].add(src)

def _segment_sum(src, seg, n):
    return jax.ops.segment_sum(src, seg, n)
kernel_name = 'mk_lm_tower_d1_tok_ids2048_r4_61e352'

def setup_inputs(seed: int=0):
    np.random.seed(seed)
    _w = jnp.asarray

    def _rec_inputs():
        import jax
        import jax.numpy as jnp
        _rk = jax.random.key(seed)
        x = jax.random.randint(jax.random.fold_in(_rk, 1), (8, 1024), 0, 63993, jnp.int32)
        return x
    x = _rec_inputs()

    def _L0_tok_setup():
        import jax, jax.numpy as jnp
        import numpy as np
        VOCAB = 16000
        NGRAM_VOCAB = 25000
        DIM = 512
        MAX_NGRAM = 3
        B, S = (4, 512)
        EPS = 1e-06

        def _hash_ngram(windows):
            h = jnp.zeros(windows.shape[:-1], dtype=windows.dtype)
            for i in range(windows.shape[-1]):
                h = (h * 131 + windows[..., i]) % NGRAM_VOCAB
            return h
        key = jax.random.key(seed)
        k0, k1, k2, k3 = jax.random.split(key, 4)
        input_ids = jax.random.randint(k0, (B, S), 0, VOCAB)
        scale = 0.02
        unigram_table = jax.random.normal(k1, (VOCAB, DIM), jnp.float32) * scale
        ngram_table = jax.random.normal(k2, (NGRAM_VOCAB, DIM), jnp.float32) * scale
        W = jax.random.normal(k3, (DIM * MAX_NGRAM, DIM), jnp.float32) * (1.0 / np.sqrt(DIM * MAX_NGRAM))
        b = jnp.zeros((DIM,), jnp.float32)
        norm_w = jnp.ones((DIM,), jnp.float32)
        return {'input_ids': input_ids, 'unigram_table': unigram_table, 'ngram_table': ngram_table, 'W': W, 'b': b, 'norm_w': norm_w}
    _L0_tok_all = _L0_tok_setup()
    _L0_tok_in = {k: v for k, v in _L0_tok_all.items() if k in ('unigram_table', 'ngram_table', 'W', 'b', 'norm_w')}
    del _L0_tok_all

    def _L0_attn_setup():
        import jax, jax.numpy as jnp
        import numpy as np
        D = 512
        E = 128
        H = D // E
        C = 64
        EPS = 1e-06

        def _lightning_scalar_decay(q, k, v, ld):
            b, n, h, e = q.shape
            nc = n // C
            qc = q.reshape(b, nc, C, h, e)
            kc = k.reshape(b, nc, C, h, e)
            vc = v.reshape(b, nc, C, h, e)
            ldc = ld.reshape(b, nc, C, h)
            cum = jnp.cumsum(ldc, axis=2)
            tot = cum[:, :, -1, :]
            Lh = cum.transpose(0, 1, 3, 2)
            decay = jnp.exp(Lh[..., :, None] - Lh[..., None, :])
            mask = jnp.tril(jnp.ones((C, C), bool))
            scores = jnp.einsum('bmihe,bmjhe->bmhij', qc, kc) * decay
            scores = jnp.where(mask, scores, 0.0)
            o_intra = jnp.einsum('bmhij,bmjhe->bmihe', scores, vc)

            def step(S, inp):
                q_c, k_c, v_c, cum_c, tot_c = inp
                o = jnp.einsum('bihe,bhef->bihf', q_c * jnp.exp(cum_c)[..., None], S)
                kd = k_c * jnp.exp(tot_c[:, None, :] - cum_c)[..., None]
                S_new = S * jnp.exp(tot_c)[:, :, None, None] + jnp.einsum('bihe,bihf->bhef', kd, v_c)
                return (S_new, o)
            xs = (qc.transpose(1, 0, 2, 3, 4), kc.transpose(1, 0, 2, 3, 4), vc.transpose(1, 0, 2, 3, 4), cum.transpose(1, 0, 2, 3), tot.transpose(1, 0, 2))
            S0 = jnp.zeros((b, h, e, e), q.dtype)
            S_final, o_inter = jax.lax.scan(step, S0, xs)
            o_inter = o_inter.transpose(1, 0, 2, 3, 4)
            return ((o_intra + o_inter).reshape(b, n, h * e), S_final)
        key = jax.random.key(seed)
        ks = jax.random.split(key, 6)
        b, n = (2, 512)
        s = 0.02
        x = jax.random.normal(ks[0], (b, n, D), jnp.float32)
        Wq = jax.random.normal(ks[1], (D, D), jnp.float32) * s
        Wk = jax.random.normal(ks[2], (D, D), jnp.float32) * s
        Wv = jax.random.normal(ks[3], (D, D), jnp.float32) * s
        Wf = jax.random.normal(ks[4], (D, H), jnp.float32) * s
        Wo = jax.random.normal(ks[5], (D, D), jnp.float32) * s
        norm_w = jnp.ones((D,), jnp.float32)
        return {'x': x, 'Wq': Wq, 'Wk': Wk, 'Wv': Wv, 'Wf': Wf, 'Wo': Wo, 'norm_w': norm_w}
    _L0_attn_all = _L0_attn_setup()
    _L0_attn_in = {k: v for k, v in _L0_attn_all.items() if k in ('Wq', 'Wk', 'Wv', 'Wf', 'Wo', 'norm_w')}
    del _L0_attn_all

    def _L0_ffn_setup():
        import jax, jax.numpy as jnp
        import numpy as np
        from functools import partial
        EPS = 1e-08

        @partial(jax.custom_vjp, nondiff_argnums=(2, 3))
        def ste_quantize(x, scale, clamp_min, clamp_max):
            return jnp.clip(jnp.round(x / scale), clamp_min, clamp_max)

        def _ste_fwd(x, scale, clamp_min, clamp_max):
            return (ste_quantize(x, scale, clamp_min, clamp_max), scale)

        def _ste_bwd(clamp_min, clamp_max, scale, g):
            return (g / scale, jnp.zeros_like(scale))
        ste_quantize.defvjp(_ste_fwd, _ste_bwd)
        key = jax.random.key(seed)
        kx, kw = jax.random.split(key)
        x = jax.random.normal(kx, (4, 1024, 512), dtype=jnp.float32)
        weight = 0.006 * jax.random.normal(kw, (512, 512), dtype=jnp.float32)
        return {'x': x, 'weight': weight}
    _L0_ffn_all = _L0_ffn_setup()
    _L0_ffn_in = {k: v for k, v in _L0_ffn_all.items() if k in ('weight',)}
    del _L0_ffn_all
    return {'x': x, 'L0_tok_unigram_table': _L0_tok_in['unigram_table'], 'L0_tok_ngram_table': _L0_tok_in['ngram_table'], 'L0_tok_W': _L0_tok_in['W'], 'L0_tok_b': _L0_tok_in['b'], 'L0_tok_norm_w': _L0_tok_in['norm_w'], 'L0_attn_Wq': _L0_attn_in['Wq'], 'L0_attn_Wk': _L0_attn_in['Wk'], 'L0_attn_Wv': _L0_attn_in['Wv'], 'L0_attn_Wf': _L0_attn_in['Wf'], 'L0_attn_Wo': _L0_attn_in['Wo'], 'L0_attn_norm_w': _L0_attn_in['norm_w'], 'L0_ffn_weight': _L0_ffn_in['weight']}

def reference(x, L0_tok_unigram_table, L0_tok_ngram_table, L0_tok_W, L0_tok_b, L0_tok_norm_w, L0_attn_Wq, L0_attn_Wk, L0_attn_Wv, L0_attn_Wf, L0_attn_Wo, L0_attn_norm_w, L0_ffn_weight):
    import jax
    import jax.numpy as jnp

    def _L0_tok_ref(input_ids, unigram_table, ngram_table, W, b, norm_w):
        import jax, jax.numpy as jnp
        import numpy as np
        VOCAB = 16000
        NGRAM_VOCAB = 25000
        DIM = 512
        MAX_NGRAM = 3
        B, S = (4, 512)
        EPS = 1e-06

        def _hash_ngram(windows):
            h = jnp.zeros(windows.shape[:-1], dtype=windows.dtype)
            for i in range(windows.shape[-1]):
                h = (h * 131 + windows[..., i]) % NGRAM_VOCAB
            return h
        Bsz, Ssz = input_ids.shape
        feats = [unigram_table[input_ids]]
        padded = jnp.pad(input_ids, ((0, 0), (MAX_NGRAM - 1, 0)))
        for n in range(2, MAX_NGRAM + 1):
            idx = jnp.arange(Ssz)[:, None] + (MAX_NGRAM - n) + jnp.arange(n)[None, :]
            windows = padded[:, idx]
            feats.append(ngram_table[_hash_ngram(windows)])
        concat = jnp.concatenate(feats, axis=-1)
        out = concat @ W + b
        var = jnp.mean(out * out, axis=-1, keepdims=True)
        return out * jax.lax.rsqrt(var + EPS) * norm_w

    def _L0_attn_ref(x, Wq, Wk, Wv, Wf, Wo, norm_w):
        import jax, jax.numpy as jnp
        import numpy as np
        D = 512
        E = 128
        H = D // E
        C = 64
        EPS = 1e-06

        def _lightning_scalar_decay(q, k, v, ld):
            b, n, h, e = q.shape
            nc = n // C
            qc = q.reshape(b, nc, C, h, e)
            kc = k.reshape(b, nc, C, h, e)
            vc = v.reshape(b, nc, C, h, e)
            ldc = ld.reshape(b, nc, C, h)
            cum = jnp.cumsum(ldc, axis=2)
            tot = cum[:, :, -1, :]
            Lh = cum.transpose(0, 1, 3, 2)
            decay = jnp.exp(Lh[..., :, None] - Lh[..., None, :])
            mask = jnp.tril(jnp.ones((C, C), bool))
            scores = jnp.einsum('bmihe,bmjhe->bmhij', qc, kc) * decay
            scores = jnp.where(mask, scores, 0.0)
            o_intra = jnp.einsum('bmhij,bmjhe->bmihe', scores, vc)

            def step(S, inp):
                q_c, k_c, v_c, cum_c, tot_c = inp
                o = jnp.einsum('bihe,bhef->bihf', q_c * jnp.exp(cum_c)[..., None], S)
                kd = k_c * jnp.exp(tot_c[:, None, :] - cum_c)[..., None]
                S_new = S * jnp.exp(tot_c)[:, :, None, None] + jnp.einsum('bihe,bihf->bhef', kd, v_c)
                return (S_new, o)
            xs = (qc.transpose(1, 0, 2, 3, 4), kc.transpose(1, 0, 2, 3, 4), vc.transpose(1, 0, 2, 3, 4), cum.transpose(1, 0, 2, 3), tot.transpose(1, 0, 2))
            S0 = jnp.zeros((b, h, e, e), q.dtype)
            S_final, o_inter = jax.lax.scan(step, S0, xs)
            o_inter = o_inter.transpose(1, 0, 2, 3, 4)
            return ((o_intra + o_inter).reshape(b, n, h * e), S_final)
        b, n, d = x.shape
        q = jax.nn.silu(x @ Wq).reshape(b, n, H, E)
        k = jax.nn.silu(x @ Wk).reshape(b, n, H, E)
        v = (x @ Wv).reshape(b, n, H, E)
        ld = jax.nn.log_sigmoid(x @ Wf)
        o, _ = _lightning_scalar_decay(q, k, v, ld)
        o = o * jax.lax.rsqrt(jnp.mean(o * o, axis=-1, keepdims=True) + EPS) * norm_w
        return o @ Wo

    def _L0_ffn_ref(x, weight):
        import jax, jax.numpy as jnp
        import numpy as np
        from functools import partial
        EPS = 1e-08

        @partial(jax.custom_vjp, nondiff_argnums=(2, 3))
        def ste_quantize(x, scale, clamp_min, clamp_max):
            return jnp.clip(jnp.round(x / scale), clamp_min, clamp_max)

        def _ste_fwd(x, scale, clamp_min, clamp_max):
            return (ste_quantize(x, scale, clamp_min, clamp_max), scale)

        def _ste_bwd(clamp_min, clamp_max, scale, g):
            return (g / scale, jnp.zeros_like(scale))
        ste_quantize.defvjp(_ste_fwd, _ste_bwd)
        alpha = jnp.maximum(jnp.mean(jnp.abs(weight)), EPS)
        w_q = ste_quantize(weight, alpha, -1.0, 1.0)
        beta = jnp.maximum(jnp.max(jnp.abs(x), axis=-1, keepdims=True) / 127.0, EPS)
        x_q = ste_quantize(x, beta, -127.0, 127.0)
        y = jnp.einsum('bsi,oi->bso', x_q, w_q)
        return y * alpha * beta
    h = _L0_tok_ref(x, L0_tok_unigram_table, L0_tok_ngram_table, L0_tok_W, L0_tok_b, L0_tok_norm_w)
    h = h + _L0_attn_ref(_layernorm(h, axis=-1), L0_attn_Wq, L0_attn_Wk, L0_attn_Wv, L0_attn_Wf, L0_attn_Wo, L0_attn_norm_w)
    h = h + _L0_ffn_ref(_layernorm(h, axis=-1), L0_ffn_weight)
    return h

_drawn_inputs = setup_inputs


def setup_inputs(seed=0):
    import zlib

    import numpy as np

    out = dict(_drawn_inputs(seed))
    spreads = {'L0_tok_b': (0.0, 0.1), 'L0_tok_norm_w': (1.0, 0.2), 'L0_attn_norm_w': (1.0, 0.2)}
    factors = {}
    for name, (base, spread) in spreads.items():
        noise = np.random.default_rng([zlib.crc32(name.encode()), seed]).standard_normal(out[name].shape)
        drawn = base * np.exp(spread * noise) if base else spread * noise
        out[name] = jnp.asarray(drawn.astype(out[name].dtype))
    for name, factor in factors.items():
        out[name] = (out[name] * factor).astype(out[name].dtype)
    return out
```

```python
import concourse.bass as bass
from concourse import mybir
from contextlib import ExitStack


def lm_tower_kernel(nc, x, uni_table, ngram_table, W_tok, b_tok, norm_tok, Wq, Wk, Wv, Wf, Wo, norm_attn, W_ffn, out):
    f32, f16, bf16, i32 = mybir.dt.float32, mybir.dt.float16, mybir.dt.bfloat16, mybir.dt.int32
    ACT, ALU, AX = mybir.ActivationFunctionType, mybir.AluOpType, mybir.AxisListType

    NB, NS = x.shape
    P = 128
    D = W_ffn.shape[0]
    H = Wf.shape[1]
    KD = D // P
    NG = W_tok.shape[0] // D
    NT = NB * NS // P
    TS = NS // P
    TM = 4
    MT = TM * P
    assert TS == 2 * TM and D == H * P and MT == 512
    VOCAB, NGV = uni_table.shape[0], ngram_table.shape[0]
    HASH_STEPS = 20
    MAGIC = 1.5 * 2.0 ** 23
    RMS_EPS, LN_EPS, Q_EPS = 1e-6, 1e-5, 1e-8
    SW = 2.0 ** 10
    SX = 2.0 ** 8
    SQ = 2.0 ** 10
    SP = 2.0 ** 6
    SO = SP * SQ

    out_t = out.rearrange("b (t p) d -> (b t) p d", p=P)

    ctx = ExitStack()
    with ctx:
        def sb(name, shape, dt=f32):
            return ctx.enter_context(nc.sbuf_tensor(name, shape, dt))

        def pb(name):
            return ctx.enter_context(nc.psum_tensor(name, [P, 512], f32))

        def sem(name):
            return ctx.enter_context(nc.semaphore(name))

        wt = sb("wt", [P, 2, NG * KD, D], f16)
        wq = sb("wq", [P, 2, KD, D], f16)
        wk = sb("wk", [P, 2, KD, D], f16)
        wv = sb("wv", [P, 2, KD, D], f16)
        wo = sb("wo", [P, 2, KD, D], f16)
        wf = sb("wf", [P, KD, H, 2], f16)
        wf32 = sb("wf32", [P, KD, H])
        wffn = sb("wffn", [P, KD, D], bf16)
        bias_b = sb("bias_b", [P, D])
        normt_b = sb("normt_b", [P, D])
        norma = sb("norma", [P, KD])
        ident = sb("ident", [P, P])
        before = sb("before", [P, P], f16)
        upto = sb("upto", [P, P], f16)
        ones16 = sb("ones16", [P, P], f16)
        ones32 = sb("ones32", [P, P])
        neghalf = sb("neghalf", [P, 1])
        one_c = sb("one_c", [P, 1])
        nmagic = sb("nmagic", [P, 1])
        xi = sb("xi", [NT, P + 2], i32)
        idx = sb("idx", [P, NT, NG], i32)
        idx_now = sb("idx_now", [P, 2, TM, NG], i32)
        cat = sb("cat", [P, 4, NG * D])
        catT = sb("catT", [P, 2, NG * KD, P], f16)
        hbuf = sb("hbuf", [P, TS, D])
        junk = sb("junk", [P, D], bf16)
        xn = sb("xn", [P, D])
        xnT = sb("xnT", [P, 2, KD, MT], f16)
        ms = sb("ms", [P, 2]); rms_u = sb("rms_u", [P, 2]); rms_r = sb("rms_r", [P, 2])
        bst = sb("bst", [P, 2, 6]); mv = sb("mv", [P, 2, 2]); ln_u = sb("ln_u", [P, 2]); ln_r = sb("ln_r", [P, 2])
        vs = sb("vs", [P, 2, TM, D], f16)
        qT = sb("qT", [P, 2, H, MT], f16)
        kT = sb("kT", [P, 2, H, MT], f16)
        q32 = sb("q32", [P, 2, MT])
        k32 = sb("k32", [P, H, MT])
        th = sb("th", [P, 2, MT])
        th_flat, q32_flat = th[:, :, :].rearrange("p a t -> p (a t)"), q32[:, :, :].rearrange("p a t -> p (a t)")
        hw = th_flat[0:NT, 0:4 * (P + 2)].rearrange("p (a t) -> p a t", a=4)
        xf = q32_flat[0:NT, 0:P + 2]
        feat = q32_flat[0:NT, 512:512 + NG * P].rearrange("p (a t) -> p a t", a=NG)
        z = sb("z", [P, TM * H]); za = sb("za", [P, TM * H]); ze = sb("ze", [P, TM * H]); zl = sb("zl", [P, TM * H])
        zm = sb("zm", [P, TM * H]); ld = sb("ld", [P, TM * H])
        ldp = sb("ldp", [P, TM, H, 2], f16)
        ct = sb("ct", [P, 3, TM, H])
        ex = sb("ex", [P, 3, TM, H])
        lda = sb("lda", [P, TM, 2 * H, P], f16)
        dec = sb("dec", [P, H, P])
        p32 = sb("p32", [P, H * P])
        pT = sb("pT", [P, 2, H * P], f16)
        kd32 = sb("kd32", [P, H, P])
        kd = sb("kd", [P, 2, H * P], f16)
        st32 = sb("st32", [P, H, P])
        stdec = sb("stdec", [P, H, P])
        st = sb("st", [P, 2, H * P], f16)
        ointer = sb("ointer", [P, H, P])
        o32 = sb("o32", [P, D])
        on = sb("on", [P, D])
        oms = sb("oms", [P, 2]); o_u = sb("o_u", [P, 2]); o_r = sb("o_r", [P, 2])
        oT = sb("oT", [P, 2, KD, P], f16)
        bst2 = sb("bst2", [P, 2, 6]); mv2 = sb("mv2", [P, 2, 2]); ln2_u = sb("ln2_u", [P, 2]); ln2_r = sb("ln2_r", [P, 2])
        xn2 = sb("xn2", [P, D])
        yq = xn2
        amax = sb("amax", [P, 2]); beta = sb("beta", [P, 2]); binv = sb("binv", [P, 2]); ab = sb("ab", [P, 2])
        xqT = sb("xqT", [P, KD, P], bf16)
        obuf = sb("obuf", [P, 2, D])
        wabs = sb("wabs", [P, 1]); alpha = sb("alpha", [P, 1]); ainv = sb("ainv", [P, 1])

        tp = [pb(f"tp{i}") for i in range(3)]
        mma, mmb = pb("mma"), pb("mmb")
        sco = pb("sco")
        dcs = pb("dcs")
        oxb = pb("oxb")
        f_ps = oxb[:, 0:32].rearrange("p (s g) -> p s g", s=TM)
        ct_ps = oxb[:, 32:96]

        x_zero, x_in, small_in, const_set, const_ok, hash_step, feat_tr = map(sem, "x_zero x_in small_in const_set const_ok hash_step feat_tr".split())
        idx_ok, idx_copied, pool_gate, dve_gate, w_hi, w_lo, w_scaled = map(sem, "idx_ok idx_copied pool_gate dve_gate w_hi w_lo w_scaled".split())
        wf_hi, wf_lo, wabs_ok, wabs_mm, alpha_step, fq_step, fq_tr = map(sem, "wf_hi wf_lo wabs_ok wabs_mm alpha_step fq_step fq_tr".split())
        fq_ok, tok_mm, h0_ok, ms_ok, rms_u_ok, rms_ok, h_ok = map(sem, "fq_ok tok_mm h0_ok ms_ok rms_u_ok rms_ok h_ok".split())
        bst_ok, mv_ok, ln_u_ok, ln_ok, xn_ok, xn_tr, xnT_hi = map(sem, "bst_ok mv_ok ln_u_ok ln_ok xn_ok xn_tr xnT_hi".split())
        xnT_lo, v_mm, v_hi, v_lo, qk_mm, th_ok, qk32_ok = map(sem, "xnT_lo v_mm v_hi v_lo qk_mm th_ok qk32_ok".split())
        qk_hi, qk_lo, z_ok, za_ok, ze_ok, zl_ok, zm_ok = map(sem, "qk_hi qk_lo z_ok za_ok ze_ok zl_ok zm_ok".split())
        ld_ok, ldp_hi, ldp_ok, cum_mm, ct_sums, ct_ok, ex_ok = map(sem, "ld_ok ldp_hi ldp_ok cum_mm ct_sums ct_ok ex_ok".split())
        lda_ok, sc_mm, dc_mm, k_tr, dec_exp, dec_ok, p32_ok = map(sem, "lda_ok sc_mm dc_mm k_tr dec_exp dec_ok p32_ok".split())
        p_hi, p_lo, kd32_ok, kd_hi, kd_lo, stdec_ok, st32_ok = map(sem, "p_hi p_lo kd32_ok kd_hi kd_lo stdec_ok st32_ok".split())
        st_hi, st_lo, att_mm, ointer_ok, o32_ok, oms_ok, o_u_ok = map(sem, "st_hi st_lo att_mm ointer_ok o32_ok oms_ok o_u_ok".split())
        o_r_ok, on_ok, on_tr, oT_hi, oT_lo, wo_mm, h2_ok = map(sem, "o_r_ok on_ok on_tr oT_hi oT_lo wo_mm h2_ok".split())
        bst2_ok, mv2_ok, ln2_u_ok, ln2_ok, xn2_ok, amax_ok, beta_ok = map(sem, "bst2_ok mv2_ok ln2_u_ok ln2_ok xn2_ok amax_ok beta_ok".split())
        binv_ok, ab_ok, yq_ok, yq_tr, xqT_ok, ffn_mm, out_ok = map(sem, "binv_ok ab_ok yq_ok yq_tr xqT_ok ffn_mm out_ok".split())
        w_in = [sem(f"w_in{r}") for r in range(H)]
        cat_in = [sem(f"cat_in{r}") for r in range(4)]
        cat_tr = [sem(f"cat_tr{g}") for g in range(NG)]
        cat_hi = [sem(f"cat_hi{g}") for g in range(NG)]
        cat_lo = [sem(f"cat_lo{g}") for g in range(NG)]
        stored = [sem(f"stored{r}") for r in range(2)]

        def tiles(b, c):
            return TS * b + c + 1

        def macros(b, c):
            return 2 * b + c // TM + 1

        def blocks(b, c, j):
            return 4 * H * b + 2 * H * (c // TM) + j + 1

        def states(b, c):
            return (TS - 1) * b + c - c // TS

        def dmas(b, c, ring, each):
            return each * ((TS // ring) * b + c // ring + 1)

        def stage(w):
            return k32[:, w % H, :]

        def weights():
            for k in range(NG * KD):
                yield W_tok, wt, k, False
            for src, dst in ((Wv, wv), (Wq, wq), (Wk, wk)):
                for k in range(KD):
                    yield src, dst, k, False
            for k in range(KD):
                yield Wo, wo, k, True

        WEIGHTS = list(weights())
        NW = len(WEIGHTS)
        CUTS = [NG * KD, NG * KD + 6, NG * KD + 12, NW]

        def split3(mm, act_hi, act_lo, w_hi_, w_lo_, first, last):
            nc.tensor.matmul(mm, act_hi, w_hi_, start=first, stop=False)
            nc.tensor.matmul(mm, act_hi, w_lo_, start=False, stop=False)
            return nc.tensor.matmul(mm, act_lo, w_hi_, start=False, stop=last)

        block = ctx.enter_context(nc.Block())

        @block.sync
        def _(sp):
            sp.wait_ge(x_zero, 1)
            sp.dma_start(xi[:, 2:], x.rearrange("b (t p) -> (b t) p", p=P)).then_inc(x_in, 16)
            for q in range(NB):
                sp.dma_start(xi[q * TS + 1:(q + 1) * TS, 0:2],
                             x[q, :].rearrange("(t p) -> t p", p=P)[0:TS - 1, P - 2:P]).then_inc(x_in, 16)
            sp.dma_start(bias_b[:, :], b_tok.partition_broadcast(P)).then_inc(small_in, 16)
            sp.dma_start(normt_b[:, :], norm_tok.partition_broadcast(P)).then_inc(small_in, 16)
            sp.dma_start(wf32[:, :, :], Wf.rearrange("(k p) h -> p k h", p=P)).then_inc(small_in, 16)
            with nc.allow_non_contiguous_dma(reason="512 numbers, once"):
                sp.dma_start(norma[:, :], norm_attn.rearrange("(k p) -> p k", p=P)).then_inc(small_in, 16)
            for w, (src, _, k, _) in enumerate(WEIGHTS):
                if w >= H:
                    sp.wait_ge(w_hi, w - H + 1)
                    sp.wait_ge(w_lo, w - H + 1)
                sp.dma_start(stage(w), src[k * P:(k + 1) * P, :]).then_inc(w_in[w % H], 16)
            for k in range(KD):
                w = NW + k
                sp.wait_ge(w_hi, w - H + 1)
                sp.wait_ge(w_lo, w - H + 1)
                sp.dma_start(stage(w), W_ffn[k * P:(k + 1) * P, :]).then_inc(w_in[w % H], 16)
            with sp.Fori(0, NB) as b:
                for c in range(TS):
                    sp.wait_ge(out_ok, tiles(b, c))
                    sp.dma_start(out_t[bass.ds(TS * b + c, 1), :, :].rearrange("a p d -> (a p) d"),
                                 obuf[:, c % 2, :]).then_inc(stored[c % 2], 16)
            for r in range(2):
                sp.wait_ge(stored[r], 16 * NT // 2)

        @block.gpsimd
        def _(pool):
            def gate():
                pool.sem_inc(pool_gate, 1)

            pool.memset(xi[:, :], 0).then_inc(x_zero, 1)
            pool.memset(ident[:, :], 0.0).then_inc(const_set, 1)
            pool.memset(before[:, :], 1.0).then_inc(const_set, 1)
            pool.memset(upto[:, :], 1.0).then_inc(const_set, 1)
            pool.memset(ones16[:, :], 1.0).then_inc(const_set, 1)
            pool.memset(ones32[:, :], 1.0).then_inc(const_set, 1)
            pool.memset(neghalf[:, :], -0.5).then_inc(const_set, 1)
            pool.memset(one_c[:, :], 1.0).then_inc(const_set, 1)
            pool.memset(nmagic[:, :], -MAGIC).then_inc(const_set, 1)
            pool.wait_ge(const_set, 8)
            for m, op, mul, step in ((ident, ALU.not_equal, 1, -1), (before, ALU.is_gt, 1, -1), (upto, ALU.is_ge, -1, 1)):
                pool.affine_select(out=m[:, :], in_=m[:, :], compare_op=op, fill=1.0 if m is ident else 0.0, base=0,
                                   pattern=[[step, P]], channel_multiplier=mul).then_inc(const_ok, 1)

            def copy_indices(b, c):
                if not isinstance(b, int) or TS * b + c >= 2 * TM:
                    for r in range(TM):
                        pool.wait_ge(cat_in[r], dmas(b, c + r - 2 * TM, 4, 16 * NG))
                    gate()
                pool.tensor_copy(idx_now[:, c // TM % 2, :, :], idx[:, bass.ds(TS * b + c, TM), :]).then_inc(idx_copied, 1)
                pool.wait_ge(idx_copied, macros(b, c))
                gate()

            def gather(b, c, first=False):
                if not first:
                    pool.wait_ge(cat_tr[NG - 1], tiles(b, c - 4))
                    gate()
                for g, table in enumerate((uni_table, ngram_table, ngram_table)):
                    pool.indirect_dma_start(
                        cat[:, c % 4, g * D:(g + 1) * D], None, table,
                        bass.IndirectOffsetOnAxis(ap=idx_now[:, c // TM % 2, c % TM, g:g + 1], axis=0),
                    ).then_inc(cat_in[c % 4], 16)

            def inv_sqrt(b, c, given, given_ok, u, u_ok, r, r_ok, op0, by0, op1, by1):
                pool.wait_ge(given_ok, tiles(b, c))
                gate()
                pool.tensor_scalar(u, given, by0, by1, op0, op1).then_inc(u_ok, 1)
                pool.wait_ge(u_ok, tiles(b, c))
                pool.tensor_tensor(r, u, neghalf[:, :], ALU.pow).then_inc(r_ok, 1)

            def rms(b, c):
                i = slice(c % 2, c % 2 + 1)
                inv_sqrt(b, c, ms[:, i], ms_ok, rms_u[:, i], rms_u_ok, rms_r[:, i], rms_ok, ALU.mult, 1.0 / D, ALU.add, RMS_EPS)

            def layer(b, c):
                i = slice(c % 2, c % 2 + 1)
                inv_sqrt(b, c, mv[:, c % 2, 1:2], mv_ok, ln_u[:, i], ln_u_ok, ln_r[:, i], ln_ok,
                         ALU.add, LN_EPS, ALU.mult, SX ** -2)

            def layer2(b, c):
                i = slice(c % 2, c % 2 + 1)
                inv_sqrt(b, c, mv2[:, c % 2, 1:2], mv2_ok, ln2_u[:, i], ln2_u_ok, ln2_r[:, i], ln2_ok,
                         ALU.add, LN_EPS, ALU.mult, 1.0)

            def attn_rms(b, c):
                i = slice(c % 2, c % 2 + 1)
                up = (SO / SX) ** 2
                inv_sqrt(b, c, oms[:, i], oms_ok, o_u[:, i], o_u_ok, o_r[:, i], o_r_ok, ALU.mult, up / D, ALU.add, up * RMS_EPS)

            def q_phase(b, c0, prev):
                if prev:
                    rms(b, c0 + 3)
                    layer(b, c0 + 3)
                    layer2(b, c0 - 1)
                pool.wait_ge(ldp_ok, macros(b, c0))
                for t in range(TM):
                    pool.tensor_tensor(
                        lda[:, t, :, :], before[:, :].unsqueeze(1).to_broadcast([P, 2 * H, P]),
                        ldp[:, t, :, :].rearrange("p h g -> p (h g)").unsqueeze(2).to_broadcast([P, 2 * H, P]),
                        ALU.mult).then_inc(lda_ok, 1)

            def a_phase(b, c0, nxt, more):
                if more:
                    copy_indices(b, c0 + 8)
                for t in range(TM):
                    c, n = c0 + t, c0 + t + TM
                    pool.wait_ge(dec_exp, tiles(b, c))
                    gate()
                    pool.affine_select(out=dec[:, :, :], in_=dec[:, :, :], compare_op=ALU.is_ge, fill=0.0, base=0,
                                       pattern=[[0, H], [1, P]], channel_multiplier=-1).then_inc(dec_ok, 1)
                    if nxt and t >= 1:
                        rms(b, n - 1)
                    if c % TS != TS - 1:
                        pool.wait_ge(kd_hi, states(b, c + 1))
                        pool.tensor_tensor(kd[:, 1, :], kd32[:, :, :].rearrange("p h e -> p (h e)"), kd[:, 0, :],
                                           ALU.subtract).then_inc(kd_lo, 1)
                    pool.wait_ge(p_hi, tiles(b, c))
                    pool.tensor_tensor(pT[:, 1, :], p32[:, :], pT[:, 0, :], ALU.subtract).then_inc(p_lo, 1)
                    if nxt and t >= 1:
                        layer(b, n - 1)
                    if 0 < c % TS < TS - 1:
                        pool.wait_ge(st32_ok, states(b, c))
                        pool.tensor_tensor(stdec[:, :, :], st32[:, :, :], ex[:, 1, t, :].unsqueeze(2).to_broadcast([P, H, P]),
                                           ALU.mult).then_inc(stdec_ok, 1)
                    if t >= 1:
                        layer2(b, c - 1)
                    attn_rms(b, c)
                    if c % TS != TS - 1:
                        pool.wait_ge(st_hi, states(b, c + 1))
                        pool.tensor_tensor(st[:, 1, :], st32[:, :, :].rearrange("p h f -> p (h f)"), st[:, 0, :],
                                           ALU.subtract).then_inc(st_lo, 1)
                    if more:
                        gather(b, c + 8)

            pool.wait_ge(idx_ok, 1)
            copy_indices(0, 0)
            for c in range(TM):
                gather(0, c, first=True)
            copy_indices(0, TM)
            for c in range(TM):
                rms(0, c)
                layer(0, c)
                gather(0, c + TM)
            q_phase(0, 0, False)
            with pool.Fori(0, NB - 1) as b:
                a_phase(b, 0, True, True)
                q_phase(b, TM, True)
                a_phase(b, TM, True, True)
                q_phase(b, 2 * TM, True)
            a_phase(NB - 1, 0, True, False)
            q_phase(NB - 1, TM, True)
            a_phase(NB - 1, TM, False, False)
            layer2(NB - 1, TS - 1)

        @block.tensor
        def _(pe):
            def cat_transpose(b, c, g):
                if g == 0:
                    pe.wait_ge(cat_in[c % 4], dmas(b, c, 4, 16 * NG))
                for j in range(KD):
                    k = g * KD + j
                    last = nc.tensor.transpose(tp[g][:, j * P:(j + 1) * P], cat[:, c % 4, k * P:(k + 1) * P], ident[:, :])
                last.then_inc(cat_tr[g], 1)

            def tok_matmul(b, c, g):
                pe.wait_ge(cat_hi[g], tiles(b, c))
                pe.wait_ge(cat_lo[g], tiles(b, c))
                for j in range(KD):
                    k = g * KD + j
                    last = split3(mma[:, :], catT[:, 0, k, :], catT[:, 1, k, :], wt[:, 0, k, :], wt[:, 1, k, :],
                                  k == 0, k == NG * KD - 1)
                if g == NG - 1:
                    last.then_inc(tok_mm, 1)

            def four_transposes(bank, src, done):
                for j in range(KD):
                    last = nc.tensor.transpose(bank[:, j * P:(j + 1) * P], src[:, j * P:(j + 1) * P], ident[:, :])
                last.then_inc(done, 1)

            def xn_transpose(b, c):
                pe.wait_ge(xn_ok, tiles(b, c))
                four_transposes(tp[1], xn, xn_tr)

            def on_transpose(b, c):
                pe.wait_ge(on_ok, tiles(b, c))
                four_transposes(tp[2], on, on_tr)

            def yq_transpose(b, c):
                pe.wait_ge(yq_ok, tiles(b, c))
                four_transposes(tp[2], yq, yq_tr)

            def out_proj(b, c, bank):
                pe.wait_ge(oT_hi, tiles(b, c))
                pe.wait_ge(oT_lo, tiles(b, c))
                for k in range(KD):
                    last = split3(bank[:, :], oT[:, 0, k, :], oT[:, 1, k, :], wo[:, 0, k, :], wo[:, 1, k, :], k == 0, k == KD - 1)
                last.then_inc(wo_mm, 1)

            def ffn(b, c, bank):
                pe.wait_ge(xqT_ok, tiles(b, c))
                for k in range(KD):
                    last = nc.tensor.matmul(bank[:, :], xqT[:, k, :], wffn[:, k, :], start=k == 0, stop=k == KD - 1)
                last.then_inc(ffn_mm, 1)

            def v_proj(b, c):
                t = c % TM
                tok = slice(t * P, (t + 1) * P)
                bank = (mma, mmb)[t % 2]
                pe.wait_ge(xnT_hi, tiles(b, c))
                pe.wait_ge(xnT_lo, tiles(b, c))
                for k in range(KD):
                    hi, lo = xnT[:, 0, k, tok], xnT[:, 1, k, tok]
                    wf_k = wf[:, k, :, :].rearrange("p h g -> p (h g)")
                    nc.tensor.matmul(f_ps[:, t, :], hi, wf_k, start=k == 0, stop=False)
                    nc.tensor.matmul(f_ps[:, t, :], lo, wf_k, start=False, stop=k == KD - 1)
                    last = split3(bank[:, :], hi, lo, wv[:, 0, k, :], wv[:, 1, k, :], k == 0, k == KD - 1)
                last.then_inc(v_mm, 1)

            def qk_proj(b, c0, j):
                bank, w, h = (mma, mmb)[j % 2], (wq, wk)[j // H], j % H
                if j < 2:
                    pe.wait_ge(v_hi, tiles(b, c0 + 2 + j))
                    pe.wait_ge(v_lo, tiles(b, c0 + 2 + j))
                else:
                    pe.wait_ge(th_ok, blocks(b, c0, j - 2))
                    pe.wait_ge(qk32_ok, blocks(b, c0, j - 2))
                for k in range(KD):
                    last = split3(bank[:, :], w[:, 0, k, h * P:(h + 1) * P], w[:, 1, k, h * P:(h + 1) * P],
                                  xnT[:, 0, k, :], xnT[:, 1, k, :], k == 0, k == KD - 1)
                last.then_inc(qk_mm, 1)

            def sums(b, c0):
                pe.wait_ge(ldp_ok, macros(b, c0))
                parts = ldp[:, :, :, :].rearrange("p t h g -> p (t h g)")
                nc.tensor.matmul(ct_ps[:, 0:32], upto[:, :], parts, start=True, stop=True)
                nc.tensor.matmul(ct_ps[:, 32:64], ones16[:, :], parts, start=True, stop=True).then_inc(cum_mm, 1)

            def q_phase(b, c0, prev, nxt):
                p2, p3 = c0 - 2, c0 - 1
                pe.wait_ge(h0_ok, tiles(b, c0 + 3))
                if prev:
                    pe.wait_ge(ointer_ok, states(b, p3))
                v_proj(b, c0)
                if prev:
                    pe.wait_ge(xqT_ok, tiles(b, p2))
                    on_transpose(b, p3)
                    pe.wait_ge(out_ok, tiles(b, c0 - 3))
                v_proj(b, c0 + 1)
                if prev:
                    pe.wait_ge(o32_ok, tiles(b, p3))
                    out_proj(b, p3, sco)
                pe.wait_ge(cat_hi[1], tiles(b, c0 + 3))
                pe.wait_ge(cat_lo[1], tiles(b, c0 + 3))
                xn_transpose(b, c0 + 3)
                pe.wait_ge(v_hi, tiles(b, c0))
                pe.wait_ge(v_lo, tiles(b, c0))
                v_proj(b, c0 + 2)
                if prev:
                    if p3 % TS != TS - 1:
                        pe.wait_ge(st32_ok, states(b, c0))
                    else:
                        pe.wait_ge(dec_exp, tiles(b, p3))
                    ffn(b, p2, dcs)
                pe.wait_ge(v_hi, tiles(b, c0 + 1))
                pe.wait_ge(v_lo, tiles(b, c0 + 1))
                v_proj(b, c0 + 3)
                qk_proj(b, c0, 0)
                qk_proj(b, c0, 1)
                if prev:
                    yq_transpose(b, p3)
                qk_proj(b, c0, 2)
                qk_proj(b, c0, 3)
                qk_proj(b, c0, 4)
                sums(b, c0)
                qk_proj(b, c0, 5)
                if prev:
                    pe.wait_ge(out_ok, tiles(b, p2))
                    ffn(b, p3, dcs)
                qk_proj(b, c0, 6)
                qk_proj(b, c0, 7)
                if nxt:
                    if prev:
                        pe.wait_ge(kd32_ok, tiles(b, p3))
                    else:
                        pe.wait_ge(cat_hi[0], tiles(b, c0 + 3))
                        pe.wait_ge(cat_lo[0], tiles(b, c0 + 3))
                    cat_transpose(b, c0 + TM, 0)
                if prev:
                    pe.wait_ge(h2_ok, tiles(b, p3))
                    pe.wait_ge(out_ok, tiles(b, p3))
                    pe.wait_ge(xqT_ok, tiles(b, p3))

            def scores(b, c):
                tok = slice(c % TM * P, (c % TM + 1) * P)
                for h in range(H):
                    last = split3(sco[:, h * P:(h + 1) * P], kT[:, 0, h, tok], kT[:, 1, h, tok],
                                  qT[:, 0, h, tok], qT[:, 1, h, tok], True, True)
                last.then_inc(sc_mm, 1)

            def decays(b, c):
                for h in range(H):
                    for g in range(2):
                        last = nc.tensor.matmul(dcs[:, h * P:(h + 1) * P], lda[:, c % TM, 2 * h + g, :], upto[:, :],
                                                start=g == 0, stop=g == 1)
                last.then_inc(dc_mm, 1)

            def k_transpose(b, c):
                for h in range(H):
                    last = nc.tensor.transpose(tp[0][:, h * P:(h + 1) * P], k32[:, h, c % TM * P:(c % TM + 1) * P], ident[:, :])
                last.then_inc(k_tr, 1)

            def attend(b, c):
                t = c % TM
                tok = slice(t * P, (t + 1) * P)
                heads = [slice(h * P, (h + 1) * P) for h in range(H)]
                pe.wait_ge(p_hi, tiles(b, c))
                pe.wait_ge(p_lo, tiles(b, c))
                if t == 0:
                    pe.wait_ge(v_lo, tiles(b, c + 3))
                for hd in heads:
                    last = split3(sco[:, hd], pT[:, 0, hd], pT[:, 1, hd], vs[:, 0, t, hd], vs[:, 1, t, hd], True, True)
                if c % TS != 0:
                    pe.wait_ge(st_hi, states(b, c))
                    pe.wait_ge(st_lo, states(b, c))
                    if t == 0:
                        pe.wait_ge(ct_sums, macros(b, c))
                    for h, hd in enumerate(heads):
                        last = split3(oxb[:, hd], qT[:, 0, h, tok], qT[:, 1, h, tok], st[:, 0, hd], st[:, 1, hd], True, True)
                if c % TS != TS - 1:
                    pe.wait_ge(kd_hi, states(b, c + 1))
                    pe.wait_ge(kd_lo, states(b, c + 1))
                    pe.wait_ge(dec_exp, tiles(b, c))
                    for hd in heads:
                        last = split3(dcs[:, hd], kd[:, 0, hd], kd[:, 1, hd], vs[:, 0, t, hd], vs[:, 1, t, hd], True, True)
                last.then_inc(att_mm, 1)

            def a_phase(b, c0, nxt):
                for t in range(TM):
                    c, n = c0 + t, c0 + t + TM
                    if t == 0:
                        pe.wait_ge(qk_hi, blocks(b, c0, 2 * H - 1))
                        pe.wait_ge(qk_lo, blocks(b, c0, 2 * H - 1))
                    else:
                        pe.wait_ge(o32_ok, tiles(b, c - 1))
                    scores(b, c)
                    pe.wait_ge(lda_ok, tiles(b, c))
                    if t >= 1:
                        pe.wait_ge(st32_ok, states(b, c))
                    decays(b, c)
                    if nxt:
                        pe.wait_ge(cat_hi[0], tiles(b, n))
                        pe.wait_ge(cat_lo[0], tiles(b, n))
                    else:
                        pe.wait_ge(kd32_ok, tiles(b, c - 1))
                    k_transpose(b, c)
                    if t >= 1:
                        if t >= 2:
                            pe.wait_ge(xqT_ok, tiles(b, c - 2))
                        elif nxt:
                            pe.wait_ge(cat_hi[2], tiles(b, n - 1))
                            pe.wait_ge(cat_lo[2], tiles(b, n - 1))
                        on_transpose(b, c - 1)
                    if nxt:
                        if t == 1:
                            pe.wait_ge(cat_hi[1], tiles(b, n - 1))
                            pe.wait_ge(cat_lo[1], tiles(b, n - 1))
                        else:
                            pe.wait_ge(xnT_hi, tiles(b, n - 1 if t == 0 else n - 2))
                            pe.wait_ge(xnT_lo, tiles(b, n - 1 if t == 0 else n - 2))
                        cat_transpose(b, n, 1)
                        if t == 0:
                            pe.wait_ge(th_ok, blocks(b, c0, 2 * H - 2))
                            pe.wait_ge(qk32_ok, blocks(b, c0, 2 * H - 2))
                        else:
                            pe.wait_ge(h0_ok, tiles(b, n - 1))
                        tok_matmul(b, n, 0)
                    if t == 1:
                        pe.wait_ge(th_ok, blocks(b, c0, 2 * H - 1))
                        pe.wait_ge(qk32_ok, blocks(b, c0, 2 * H - 1))
                    elif t == 2:
                        pe.wait_ge(h2_ok, tiles(b, c - 2))
                    elif t == 3:
                        pe.wait_ge(out_ok, tiles(b, c - 3))
                    if t >= 1:
                        out_proj(b, c - 1, mmb)
                    if nxt:
                        cat_transpose(b, n, 2)
                    attend(b, c)
                    if t >= 2:
                        pe.wait_ge(h2_ok, tiles(b, c - 1))
                        ffn(b, c - 2, mmb)
                    if nxt:
                        tok_matmul(b, n, 1)
                        if t >= 1:
                            xn_transpose(b, n - 1)
                        if t <= 2:
                            pe.wait_ge(kd32_ok, tiles(b, c))
                            cat_transpose(b, n + 1, 0)
                        tok_matmul(b, n, 2)
                    if t >= 1:
                        yq_transpose(b, c - 1)

            pe.wait_ge(const_ok, 3)
            pe.wait_ge(hash_step, HASH_STEPS)
            for g in range(NG):
                last = nc.tensor.transpose(sco[:, g * NT:(g + 1) * NT], feat[:, g, :], ident[0:NT, 0:NT])
            last.then_inc(feat_tr, 1)
            cat_transpose(0, 0, 0)
            for c in range(TM):
                if c >= 1:
                    pe.wait_ge(cat_hi[1], c)
                    pe.wait_ge(cat_lo[1], c)
                if c >= 2:
                    pe.wait_ge(xnT_hi, c - 1)
                    pe.wait_ge(xnT_lo, c - 1)
                cat_transpose(0, c, 1)
                pe.wait_ge(w_lo, CUTS[0])
                pe.wait_ge(w_hi, CUTS[0])
                if c >= 1:
                    pe.wait_ge(h0_ok, c)
                tok_matmul(0, c, 0)
                if c >= 1:
                    pe.wait_ge(cat_hi[2], c)
                    pe.wait_ge(cat_lo[2], c)
                cat_transpose(0, c, 2)
                tok_matmul(0, c, 1)
                if c >= 1:
                    xn_transpose(0, c - 1)
                if c < TM - 1:
                    cat_transpose(0, c + 1, 0)
                tok_matmul(0, c, 2)
            pe.wait_ge(wabs_ok, 1)
            nc.tensor.matmul(oxb[:, 0:1], ones32[:, :], wabs[:, :], start=True, stop=True).then_inc(wabs_mm, 1)
            for k in range(KD):
                pe.wait_ge(fq_step, 2 * (k + 1))
                if k >= 2:
                    pe.wait_ge(fq_ok, k - 1)
                for j in range(KD):
                    last = nc.tensor.transpose((sco, dcs)[k % 2][:, j * P:(j + 1) * P], stage(NW + k)[:, j * P:(j + 1) * P],
                                               ident[:, :])
                last.then_inc(fq_tr, 1)
            pe.wait_ge(alpha_step, 1)
            pe.wait_ge(w_hi, NW)
            pe.wait_ge(w_lo, NW)
            pe.wait_ge(wf_lo, 1)
            q_phase(0, 0, False, True)
            pe.wait_ge(fq_ok, KD)
            with pe.Fori(0, NB - 1) as b:
                a_phase(b, 0, True)
                q_phase(b, TM, True, True)
                a_phase(b, TM, True)
                q_phase(b, 2 * TM, True, True)
            b = NB - 1
            a_phase(b, 0, True)
            q_phase(b, TM, True, False)
            a_phase(b, TM, False)
            pe.wait_ge(xqT_ok, tiles(b, TS - 2))
            on_transpose(b, TS - 1)
            pe.wait_ge(out_ok, tiles(b, TS - 3))
            out_proj(b, TS - 1, mmb)
            ffn(b, TS - 2, mma)
            yq_transpose(b, TS - 1)
            ffn(b, TS - 1, sco)

        @block.scalar
        def _(act):
            copy = nc.scalar.activation

            def w_split(lo, hi):
                for w in range(lo, hi):
                    _, dst, k, scaled = WEIGHTS[w]
                    if scaled:
                        act.wait_ge(w_scaled, k + 1)
                    else:
                        act.wait_ge(w_in[w % H], 16 * (w // H + 1))
                    copy(dst[:, 0, k, :], stage(w), ACT.Copy, scale=SW).then_inc(w_hi, 1)

            def cat_split(b, c, g):
                act.wait_ge(cat_tr[g], tiles(b, c))
                copy(catT[:, 0, g * KD:(g + 1) * KD, :], tp[g][:, :].rearrange("p (k t) -> p k t", k=KD), ACT.Copy,
                     scale=SW).then_inc(cat_hi[g], 1)

            def mean_square(b, c):
                act.wait_ge(h0_ok, tiles(b, c))
                copy(junk[:, :], hbuf[:, c % TS, :], ACT.Square, accum_out=ms[:, c % 2:c % 2 + 1]).then_inc(ms_ok, 1)

            def xnT_split(b, c):
                act.wait_ge(xn_tr, tiles(b, c))
                copy(xnT[:, 0, :, c % TM * P:(c % TM + 1) * P], tp[1][:, :].rearrange("p (k t) -> p k t", k=KD),
                     ACT.Copy).then_inc(xnT_hi, 1)

            def oT_split(b, c):
                act.wait_ge(on_tr, tiles(b, c))
                copy(oT[:, 0, :, :], tp[2][:, :].rearrange("p (k t) -> p k t", k=KD), ACT.Copy).then_inc(oT_hi, 1)

            def xq_split(b, c):
                act.wait_ge(yq_tr, tiles(b, c))
                copy(xqT[:, :, :], tp[2][:, :].rearrange("p (k t) -> p k t", k=KD), ACT.Identity,
                     bias=nmagic[:, :]).then_inc(xqT_ok, 1)

            def v_split(b, c):
                t = c % TM
                act.wait_ge(v_mm, tiles(b, c))
                copy(vs[:, 0, t, :], (mma, mmb)[t % 2][:, :], ACT.Copy, scale=SQ / (SX * SW)).then_inc(v_hi, 1)

            def qk_tanh(b, c0, j):
                act.wait_ge(qk_mm, blocks(b, c0, j))
                if j >= 2:
                    act.wait_ge(qk32_ok, blocks(b, c0, j - 2))
                copy(th[:, j % 2, :], (mma, mmb)[j % 2][:, :], ACT.Tanh, scale=0.5 / (SX * SW)).then_inc(th_ok, 1)

            def qk_split(b, c0, j):
                dst, src = (qT, q32[:, j % 2, :]) if j < H else (kT, k32[:, j - H, :])
                act.wait_ge(qk32_ok, blocks(b, c0, j))
                copy(dst[:, 0, j % H, :], src, ACT.Copy, scale=SQ / (2 * SX * SW)).then_inc(qk_hi, 1)

            def q_phase(b, c0, prev, nxt):
                if prev:
                    mean_square(b, c0 + 3)
                v_split(b, c0)
                if prev:
                    oT_split(b, c0 - 1)
                v_split(b, c0 + 1)
                xnT_split(b, c0 + 3)
                v_split(b, c0 + 2)
                v_split(b, c0 + 3)
                m = macros(b, c0)
                act.wait_ge(z_ok, m)
                copy(za[:, :], z[:, :], ACT.Abs, scale=1.0 / (SX * SW)).then_inc(za_ok, 1)
                act.wait_ge(za_ok, m)
                copy(ze[:, :], za[:, :], ACT.Exp, scale=-1.0).then_inc(ze_ok, 1)
                act.wait_ge(ze_ok, m)
                copy(zl[:, :], ze[:, :], ACT.Ln, bias=one_c[:, :]).then_inc(zl_ok, 1)
                for j in range(2 * H):
                    qk_tanh(b, c0, j)
                    qk_split(b, c0, j)
                    if j == 3 and prev:
                        xq_split(b, c0 - 1)
                    if j == 5:
                        act.wait_ge(ct_ok, m)
                        copy(ex[:, :, :, :].rearrange("p a t h -> p (a t h)"), ct[:, :, :, :].rearrange("p a t h -> p (a t h)"),
                             ACT.Exp, scale=1.0 / SP).then_inc(ex_ok, 1)
                if nxt:
                    cat_split(b, c0 + TM, 0)

            def a_phase(b, c0, nxt):
                for t in range(TM):
                    c, n = c0 + t, c0 + t + TM
                    act.wait_ge(dc_mm, tiles(b, c))
                    copy(dec[:, :, :].rearrange("p h i -> p (h i)"), dcs[:, :], ACT.Exp, scale=1.0 / SP).then_inc(dec_exp, 1)
                    if nxt and t >= 1:
                        mean_square(b, n - 1)
                    if t >= 1:
                        oT_split(b, c - 1)
                    if nxt:
                        cat_split(b, n, 1)
                    if c % TS != TS - 1:
                        act.wait_ge(kd32_ok, tiles(b, c))
                        copy(kd[:, 0, :], kd32[:, :, :].rearrange("p h e -> p (h e)"), ACT.Copy).then_inc(kd_hi, 1)
                    act.wait_ge(p32_ok, tiles(b, c))
                    copy(pT[:, 0, :], p32[:, :], ACT.Copy).then_inc(p_hi, 1)
                    if nxt:
                        cat_split(b, n, 2)
                    act.wait_ge(att_mm, tiles(b, c))
                    if c % TS != 0:
                        for h in range(H):
                            last = copy(ointer[:, h, :], oxb[:, h * P:(h + 1) * P], ACT.Copy, scale=ex[:, 0, t, h:h + 1])
                        last.then_inc(ointer_ok, 1)
                    if c % TS != TS - 1:
                        act.wait_ge(st32_ok, states(b, c + 1))
                        copy(st[:, 0, :], st32[:, :, :].rearrange("p h f -> p (h f)"), ACT.Copy).then_inc(st_hi, 1)
                    act.wait_ge(o32_ok, tiles(b, c))
                    copy(junk[:, :], o32[:, :], ACT.Square, scale=1.0 / SO, accum_out=oms[:, c % 2:c % 2 + 1]).then_inc(oms_ok, 1)
                    act.wait_ge(o_r_ok, tiles(b, c))
                    copy(on[:, :], o32[:, :], ACT.Copy, scale=o_r[:, c % 2:c % 2 + 1]).then_inc(on_ok, 1)
                    if nxt and t >= 1:
                        xnT_split(b, n - 1)
                    if nxt and t <= 2:
                        cat_split(b, n + 1, 0)
                    if t >= 1:
                        xq_split(b, c - 1)

            w_split(0, CUTS[0])
            cat_split(0, 0, 0)
            for c in range(TM):
                cat_split(0, c, 1)
                cat_split(0, c, 2)
                if c >= 1:
                    xnT_split(0, c - 1)
                if c < TM - 1:
                    cat_split(0, c + 1, 0)
                    w_split(CUTS[c], CUTS[c + 1])
                mean_square(0, c)
            act.wait_ge(small_in, 64)
            copy(wf[:, :, :, 0], wf32[:, :, :], ACT.Copy, scale=SW).then_inc(wf_hi, 1)
            q_phase(0, 0, False, True)
            with act.Fori(0, NB - 1) as b:
                a_phase(b, 0, True)
                q_phase(b, TM, True, True)
                a_phase(b, TM, True)
                q_phase(b, 2 * TM, True, True)
            b = NB - 1
            a_phase(b, 0, True)
            q_phase(b, TM, True, False)
            a_phase(b, TM, False)
            oT_split(b, TS - 1)
            xq_split(b, TS - 1)

        @block.vector
        def _(dve):
            V = nc.vector

            def k_t(bank):
                return bank[:, :].rearrange("p (k t) -> p k t", k=KD)

            def w_split(lo, hi):
                for w in range(lo, hi):
                    _, dst, k, scaled = WEIGHTS[w]
                    dve.wait_ge(w_in[w % H], 16 * (w // H + 1))
                    if scaled:
                        dve.wait_ge(small_in, 64)
                        V.tensor_scalar(stage(w), stage(w), norma[:, k:k + 1], None, ALU.mult).then_inc(w_scaled, 1)
                        dve.wait_ge(w_scaled, k + 1)
                    dve.wait_ge(w_hi, w + 1)
                    V.scalar_tensor_tensor(dst[:, 1, k, :], stage(w), SW, dst[:, 0, k, :], ALU.mult, ALU.subtract).then_inc(w_lo, 1)

            def cat_split(b, c, g):
                dve.wait_ge(cat_hi[g], tiles(b, c))
                gs = slice(g * KD, (g + 1) * KD)
                V.scalar_tensor_tensor(catT[:, 1, gs, :], k_t(tp[g]), SW, catT[:, 0, gs, :], ALU.mult,
                                       ALU.subtract).then_inc(cat_lo[g], 1)

            def tok_out(b, c):
                dve.wait_ge(tok_mm, tiles(b, c))
                V.scalar_tensor_tensor(hbuf[:, c % TS, :], mma[:, :], SW ** -2, bias_b[:, :], ALU.mult, ALU.add).then_inc(h0_ok, 1)

            def stats(b, c, given_ok, st6, st6_ok, out2, out2_ok):
                dve.wait_ge(given_ok, tiles(b, c))
                V.bn_stats(st6[:, c % 2, :], hbuf[:, c % TS, :]).then_inc(st6_ok, 1)
                dve.wait_ge(st6_ok, tiles(b, c))
                dve.sem_inc(dve_gate, 1)
                V.bn_aggr(out2[:, c % 2, :], st6[:, c % 2, :]).then_inc(out2_ok, 1)

            def tok_norm(b, c):
                dve.wait_ge(rms_ok, tiles(b, c))
                V.scalar_tensor_tensor(hbuf[:, c % TS, :], hbuf[:, c % TS, :], rms_r[:, c % 2:c % 2 + 1], normt_b[:, :],
                                       ALU.mult, ALU.mult).then_inc(h_ok, 1)
                stats(b, c, h_ok, bst, bst_ok, mv, mv_ok)

            def tok_xn(b, c):
                dve.wait_ge(ln_ok, tiles(b, c))
                V.tensor_scalar(xn[:, :], hbuf[:, c % TS, :], mv[:, c % 2, 0:1], ln_r[:, c % 2:c % 2 + 1], ALU.subtract,
                                ALU.mult).then_inc(xn_ok, 1)

            def xnT_split(b, c):
                tok = slice(c % TM * P, (c % TM + 1) * P)
                dve.wait_ge(xnT_hi, tiles(b, c))
                V.tensor_tensor(xnT[:, 1, :, tok], k_t(tp[1]), xnT[:, 0, :, tok], ALU.subtract).then_inc(xnT_lo, 1)

            def v_split(b, c):
                t = c % TM
                dve.wait_ge(v_hi, tiles(b, c))
                V.scalar_tensor_tensor(vs[:, 1, t, :], (mma, mmb)[t % 2][:, :], SQ / (SX * SW), vs[:, 0, t, :], ALU.mult,
                                       ALU.subtract).then_inc(v_lo, 1)

            def silu(b, c0, j):
                dst = q32[:, j % 2, :] if j < H else k32[:, j - H, :]
                dve.wait_ge(th_ok, blocks(b, c0, j))
                if 2 <= j < H:
                    dve.wait_ge(qk_hi, blocks(b, c0, j - 2))
                V.scalar_tensor_tensor(dst, th[:, j % 2, :], 1.0, (mma, mmb)[j % 2][:, :], ALU.add, ALU.mult).then_inc(qk32_ok, 1)

            def qk_split(b, c0, j):
                dst, src = (qT, q32[:, j % 2, :]) if j < H else (kT, k32[:, j - H, :])
                dve.wait_ge(qk_hi, blocks(b, c0, j))
                V.scalar_tensor_tensor(dst[:, 1, j % H, :], src, SQ / (2 * SX * SW), dst[:, 0, j % H, :], ALU.mult,
                                       ALU.subtract).then_inc(qk_lo, 1)

            def log_decay_begin(b, c0):
                m = macros(b, c0)
                dve.wait_ge(v_mm, tiles(b, c0 + 3))
                V.tensor_reduce(z[:, :], f_ps.rearrange("p t (h g) -> p (t h) g", g=2), AX.X, ALU.add).then_inc(z_ok, 1)
                dve.wait_ge(z_ok, m)
                V.tensor_scalar(zm[:, :], z[:, :], SP / (SX * SW), 0.0, ALU.mult, ALU.min).then_inc(zm_ok, 1)

            def log_decay_end(b, c0):
                m = macros(b, c0)
                dve.wait_ge(zl_ok, m)
                dve.wait_ge(zm_ok, m)
                V.scalar_tensor_tensor(ld[:, :], zl[:, :], -SP, zm[:, :], ALU.mult, ALU.add).then_inc(ld_ok, 1)
                ld_v = ld[:, :].rearrange("p (t h) -> p t h", t=TM)
                dve.wait_ge(ld_ok, m)
                V.tensor_copy(ldp[:, :, :, 0], ld_v).then_inc(ldp_hi, 1)
                dve.wait_ge(ldp_hi, m)
                V.tensor_tensor(ldp[:, :, :, 1], ld_v, ldp[:, :, :, 0], ALU.subtract).then_inc(ldp_ok, 1)

            def decay_sums(b, c0):
                m = macros(b, c0)
                dve.wait_ge(cum_mm, m)
                V.tensor_reduce(ct[:, 0:2, :, :].rearrange("p a t h -> p (a t h)"),
                                ct_ps.rearrange("p (a g) -> p a g", g=2), AX.X, ALU.add).then_inc(ct_sums, 1)
                dve.wait_ge(ct_sums, m)
                V.tensor_tensor(ct[:, 2, :, :], ct[:, 1, :, :], ct[:, 0, :, :], ALU.subtract).then_inc(ct_ok, 1)

            def oT_split(b, c):
                dve.wait_ge(oT_hi, tiles(b, c))
                V.tensor_tensor(oT[:, 1, :, :], k_t(tp[2]), oT[:, 0, :, :], ALU.subtract).then_inc(oT_lo, 1)

            def attn_residual(b, c, bank):
                dve.wait_ge(wo_mm, tiles(b, c))
                V.scalar_tensor_tensor(hbuf[:, c % TS, :], bank[:, :], 1.0 / (SX * SW), hbuf[:, c % TS, :], ALU.mult,
                                       ALU.add).then_inc(h2_ok, 1)
                stats(b, c, h2_ok, bst2, bst2_ok, mv2, mv2_ok)

            def quantise(b, c):
                i = slice(c % 2, c % 2 + 1)
                dve.wait_ge(ln2_ok, tiles(b, c))
                V.tensor_scalar(xn2[:, :], hbuf[:, c % TS, :], mv2[:, c % 2, 0:1], ln2_r[:, i], ALU.subtract,
                                ALU.mult).then_inc(xn2_ok, 1)
                dve.wait_ge(xn2_ok, tiles(b, c))
                V.tensor_reduce(amax[:, i], xn2[:, :], AX.X, ALU.max, apply_absolute_value=True).then_inc(amax_ok, 1)
                dve.wait_ge(amax_ok, tiles(b, c))
                V.tensor_scalar(beta[:, i], amax[:, i], 1.0 / 127.0, Q_EPS, ALU.mult, ALU.max).then_inc(beta_ok, 1)
                dve.wait_ge(beta_ok, tiles(b, c))
                V.reciprocal(binv[:, i], beta[:, i]).then_inc(binv_ok, 1)
                V.tensor_scalar(ab[:, i], beta[:, i], alpha[:, :], None, ALU.mult).then_inc(ab_ok, 1)
                dve.wait_ge(binv_ok, tiles(b, c))
                V.tensor_scalar(yq[:, :], xn2[:, :], binv[:, i], MAGIC, ALU.mult, ALU.add).then_inc(yq_ok, 1)

            def ffn_residual(b, c, bank):
                dve.wait_ge(ffn_mm, tiles(b, c))
                dve.wait_ge(ab_ok, tiles(b, c))
                if c >= 2:
                    dve.wait_ge(stored[c % 2], dmas(b, c - 2, 2, 16))
                V.scalar_tensor_tensor(obuf[:, c % 2, :], bank[:, :], ab[:, c % 2:c % 2 + 1], hbuf[:, c % TS, :], ALU.mult,
                                       ALU.add).then_inc(out_ok, 1)

            def q_phase(b, c0, prev, nxt):
                if prev:
                    tok_out(b, c0 + 3)
                v_split(b, c0)
                if prev:
                    oT_split(b, c0 - 1)
                    tok_norm(b, c0 + 3)
                v_split(b, c0 + 1)
                if prev:
                    tok_xn(b, c0 + 3)
                    attn_residual(b, c0 - 1, sco)
                xnT_split(b, c0 + 3)
                v_split(b, c0 + 2)
                if prev:
                    ffn_residual(b, c0 - 2, dcs)
                    quantise(b, c0 - 1)
                v_split(b, c0 + 3)
                log_decay_begin(b, c0)
                for j in range(2 * H):
                    silu(b, c0, j)
                    qk_split(b, c0, j)
                    if j == 0:
                        log_decay_end(b, c0)
                    if j == 4:
                        decay_sums(b, c0)
                    if j == 5 and prev:
                        ffn_residual(b, c0 - 1, dcs)
                if nxt:
                    cat_split(b, c0 + TM, 0)
                if c0 == TS:
                    dve.wait_ge(stored[0], dmas(b, c0 - 2, 2, 16))
                    dve.wait_ge(stored[1], dmas(b, c0 - 1, 2, 16))

            def a_phase(b, c0, nxt):
                for t in range(TM):
                    c, n = c0 + t, c0 + t + TM
                    if nxt and t >= 1:
                        tok_out(b, n - 1)
                    dve.wait_ge(k_tr, tiles(b, c))
                    dve.wait_ge(ex_ok, macros(b, c))
                    V.scalar_tensor_tensor(kd32[:, :, :], k_t(tp[0]), SQ / (2 * SX * SW) ,
                                           ex[:, 2, t, :].unsqueeze(2).to_broadcast([P, H, P]), ALU.mult,
                                           ALU.mult).then_inc(kd32_ok, 1)
                    if t >= 1:
                        oT_split(b, c - 1)
                    if nxt:
                        cat_split(b, n, 1)
                    dve.wait_ge(sc_mm, tiles(b, c))
                    dve.wait_ge(dec_ok, tiles(b, c))
                    V.scalar_tensor_tensor(p32[:, :], sco[:, :], SP / SQ ** 2, dec[:, :, :].rearrange("p h i -> p (h i)"),
                                           ALU.mult, ALU.mult).then_inc(p32_ok, 1)
                    if nxt and t >= 1:
                        tok_norm(b, n - 1)
                        tok_xn(b, n - 1)
                    if t >= 1:
                        attn_residual(b, c - 1, mmb)
                    if nxt:
                        cat_split(b, n, 2)
                    dve.wait_ge(att_mm, tiles(b, c))
                    st_v = st32[:, :, :].rearrange("p h f -> p (h f)")
                    if c % TS == 0:
                        V.tensor_scalar(st_v, dcs[:, :], SP / SQ ** 2, None, ALU.mult).then_inc(st32_ok, 1)
                        V.tensor_copy(o32[:, :], sco[:, :]).then_inc(o32_ok, 1)
                    else:
                        if c % TS != TS - 1:
                            dve.wait_ge(stdec_ok, (TS - 2) * b + c)
                            V.scalar_tensor_tensor(st_v, dcs[:, :], SP / SQ ** 2, stdec[:, :, :].rearrange("p h f -> p (h f)"),
                                                   ALU.mult, ALU.add).then_inc(st32_ok, 1)
                        dve.wait_ge(ointer_ok, states(b, c))
                        V.tensor_tensor(o32[:, :], sco[:, :], ointer[:, :, :].rearrange("p h f -> p (h f)"),
                                        ALU.add).then_inc(o32_ok, 1)
                    if t >= 2:
                        ffn_residual(b, c - 2, mmb)
                    if t >= 1:
                        quantise(b, c - 1)
                    if nxt and t >= 1:
                        xnT_split(b, n - 1)
                    if nxt and t <= 2:
                        cat_split(b, n + 1, 0)

            made = [0]

            def step(ins):
                made[0] += 1
                ins.then_inc(hash_step, 1)
                dve.wait_ge(hash_step, made[0])

            def mod_ngv(r, v, q):
                step(V.tensor_scalar(q, v, 1.0 / NGV, MAGIC, ALU.mult, ALU.add))
                step(V.tensor_scalar(q, q, MAGIC, -float(NGV), ALU.subtract, ALU.mult))
                step(V.tensor_tensor(r, q, v, ALU.add))
                step(V.tensor_scalar(q, r, 0.0, float(NGV), ALU.is_lt, ALU.mult))
                step(V.tensor_tensor(r, r, q, ALU.add))

            W2 = P + 2
            dve.wait_ge(x_in, 16 * (NB + 1))
            step(V.tensor_copy(xf[:, :], xi[:, :]))
            step(V.tensor_scalar(feat[:, 0, :], xf[:, 2:], float(VOCAB - 1), 0.0, ALU.min, ALU.max))
            mod_ngv(hw[:, 0, :], xf[:, :], hw[:, 1, :])
            step(V.scalar_tensor_tensor(hw[:, 2, 1:W2], hw[:, 0, 0:W2 - 1], 131.0, xf[:, 1:W2], ALU.mult, ALU.add))
            mod_ngv(hw[:, 3, 1:W2], hw[:, 2, 1:W2], hw[:, 1, 1:W2])
            step(V.tensor_copy(feat[:, 1, :], hw[:, 3, 2:W2]))
            step(V.scalar_tensor_tensor(hw[:, 2, 2:W2], hw[:, 3, 1:W2 - 1], 131.0, xf[:, 2:W2], ALU.mult, ALU.add))
            mod_ngv(feat[:, 2, :], hw[:, 2, 2:W2], hw[:, 1, 2:W2])
            assert made[0] == HASH_STEPS
            dve.wait_ge(feat_tr, 1)
            V.tensor_copy(idx[:, :, :].rearrange("p n g -> p g n"),
                          sco[:, 0:NG * NT].rearrange("p (g n) -> p g n", g=NG)).then_inc(idx_ok, 1)

            w_split(0, CUTS[0])
            dve.wait_ge(small_in, 64)
            cat_split(0, 0, 0)
            for c in range(TM):
                cat_split(0, c, 1)
                cat_split(0, c, 2)
                if c >= 1:
                    xnT_split(0, c - 1)
                if c < TM - 1:
                    cat_split(0, c + 1, 0)
                    w_split(CUTS[c], CUTS[c + 1])
                tok_out(0, c)
                tok_norm(0, c)
                tok_xn(0, c)
            dve.wait_ge(wf_hi, 1)
            V.scalar_tensor_tensor(wf[:, :, :, 1], wf32[:, :, :], SW, wf[:, :, :, 0], ALU.mult, ALU.subtract).then_inc(wf_lo, 1)
            for k in range(KD):
                dve.wait_ge(w_in[(NW + k) % H], 16 * ((NW + k) // H + 1))
            V.tensor_reduce(wabs[:, :], k32[:, :, :].rearrange("p k d -> p (k d)"), AX.X, ALU.add,
                            apply_absolute_value=True).then_inc(wabs_ok, 1)
            dve.wait_ge(wabs_mm, 1)
            V.tensor_scalar(alpha[:, :], oxb[:, 0:1], 1.0 / (D * D), Q_EPS, ALU.mult, ALU.max).then_inc(alpha_step, 1)
            dve.wait_ge(alpha_step, 1)
            V.reciprocal(ainv[:, :], alpha[:, :]).then_inc(alpha_step, 1)
            dve.wait_ge(alpha_step, 2)
            for k in range(KD):
                v = stage(NW + k)
                V.tensor_scalar(v, v, ainv[:, :], MAGIC, ALU.mult, ALU.add).then_inc(fq_step, 1)
                dve.wait_ge(fq_step, 2 * k + 1)
                V.tensor_scalar(v, v, MAGIC, 1.0, ALU.subtract, ALU.min).then_inc(fq_step, 1)
            for k in range(KD):
                dve.wait_ge(fq_tr, k + 1)
                V.tensor_scalar(wffn[:, :, k * P:(k + 1) * P], k_t((sco, dcs)[k % 2]), -1.0, None, ALU.max).then_inc(fq_ok, 1)
            q_phase(0, 0, False, True)
            with dve.Fori(0, NB - 1) as b:
                a_phase(b, 0, True)
                q_phase(b, TM, True, True)
                a_phase(b, TM, True)
                q_phase(b, 2 * TM, True, True)
            b = NB - 1
            a_phase(b, 0, True)
            q_phase(b, TM, True, False)
            a_phase(b, TM, False)
            oT_split(b, TS - 1)
            attn_residual(b, TS - 1, mmb)
            ffn_residual(b, TS - 2, mma)
            quantise(b, TS - 1)
            ffn_residual(b, TS - 1, sco)


_INS = ["x", "L0_tok_unigram_table", "L0_tok_ngram_table", "L0_tok_W", "L0_tok_b", "L0_tok_norm_w", "L0_attn_Wq",
        "L0_attn_Wk", "L0_attn_Wv", "L0_attn_Wf", "L0_attn_Wo", "L0_attn_norm_w", "L0_ffn_weight"]


def kernel(**inputs):
    import numpy as _np
    import concourse.bacc as _bacc
    from concourse import mybir as _mybir
    from concourse.bass_utils import run_bass_kernel_spmd as _run

    nc = _bacc.Bacc("TRN2", target_bir_lowering=False, num_devices=1)
    arrays, args = {}, []
    for name in _INS:
        a = _np.ascontiguousarray(inputs[name])
        arrays[f"in_{name}_dram"] = a
        args.append(nc.dram_tensor(f"in_{name}_dram", a.shape, _mybir.dt.from_np(a.dtype), kind="ExternalInput").ap())
    shape = (*inputs["x"].shape, inputs["L0_ffn_weight"].shape[0])
    args.append(nc.dram_tensor("out_0_dram", shape, _mybir.dt.float32, kind="ExternalOutput").ap())
    lm_tower_kernel(nc, *args)
    r = _run(nc, [arrays], core_ids=[0])
    return r.results[0]["out_0_dram"]
```

```python
import concourse.bass as bass
from concourse import mybir
from contextlib import ExitStack


def lm_tower_kernel(nc, x, uni_table, ngram_table, W_tok, b_tok, norm_tok, Wq, Wk, Wv, Wf, Wo, norm_attn, W_ffn, out):
    f32, f16, bf16, i32 = mybir.dt.float32, mybir.dt.float16, mybir.dt.bfloat16, mybir.dt.int32
    ACT, ALU, AX = mybir.ActivationFunctionType, mybir.AluOpType, mybir.AxisListType

    NB, NS = x.shape
    P = 128
    D = W_ffn.shape[0]
    H = Wf.shape[1]
    KD = D // P
    NG = W_tok.shape[0] // D
    NT = NB * NS // P
    TS = NS // P
    TM = 4
    MT = TM * P
    assert TS == 2 * TM and D == H * P and MT == 512
    VOCAB, NGV = uni_table.shape[0], ngram_table.shape[0]
    HASH_STEPS = 20
    MAGIC = 1.5 * 2.0 ** 23
    RMS_EPS, LN_EPS, Q_EPS = 1e-6, 1e-5, 1e-8
    SW = 2.0 ** 10
    SX = 2.0 ** 8
    SQ = 2.0 ** 10
    SP = 2.0 ** 6
    SO = SP * SQ

    out_t = out.rearrange("b (t p) d -> (b t) p d", p=P)

    ctx = ExitStack()
    with ctx:
        def sb(name, shape, dt=f32):
            return ctx.enter_context(nc.sbuf_tensor(name, shape, dt))

        def pb(name):
            return ctx.enter_context(nc.psum_tensor(name, [P, 512], f32))

        def sem(name):
            return ctx.enter_context(nc.semaphore(name))

        wt = sb("wt", [P, 2, NG * KD, D], f16)
        wq = sb("wq", [P, 2, KD, D], f16)
        wk = sb("wk", [P, 2, KD, D], f16)
        wv = sb("wv", [P, 2, KD, D], f16)
        wo = sb("wo", [P, 2, KD, D], f16)
        wf = sb("wf", [P, KD, H, 2], f16)
        wf32 = sb("wf32", [P, KD, H])
        wffn = sb("wffn", [P, KD, D], bf16)
        bias_b = sb("bias_b", [P, D])
        normt_b = sb("normt_b", [P, D])
        norma = sb("norma", [P, KD])
        ident = sb("ident", [P, P])
        ident16 = sb("ident16", [P, P], bf16)
        before = sb("before", [P, P], f16)
        upto = sb("upto", [P, P], f16)
        ones16 = sb("ones16", [P, P], f16)
        ones32 = sb("ones32", [P, P])
        neghalf = sb("neghalf", [P, 1])
        one_c = sb("one_c", [P, 1])
        xi = sb("xi", [NT, P + 2], i32)
        idx = sb("idx", [P, NT, NG], i32)
        idx_now = sb("idx_now", [P, 2, TM, NG], i32)
        cat = sb("cat", [P, 4, NG * D])
        catT = sb("catT", [P, 2, NG * KD, P], f16)
        hbuf = sb("hbuf", [P, TS, D])
        junk = sb("junk", [P, D], bf16)
        xn = sb("xn", [P, D])
        xnT = sb("xnT", [P, 2, KD, MT], f16)
        ms = sb("ms", [P, 2]); rms_u = sb("rms_u", [P, 2]); rms_r = sb("rms_r", [P, 2])
        bst = sb("bst", [P, 2, 6]); mv = sb("mv", [P, 2, 2]); ln_u = sb("ln_u", [P, 2]); ln_r = sb("ln_r", [P, 2])
        vs = sb("vs", [P, 2, TM, D], f16)
        qT = sb("qT", [P, 2, H, MT], f16)
        kT = sb("kT", [P, 2, H, MT], f16)
        q32 = sb("q32", [P, 2, MT])
        k32 = sb("k32", [P, H, MT])
        th = sb("th", [P, 2, MT])
        th_flat, q32_flat = th[:, :, :].rearrange("p a t -> p (a t)"), q32[:, :, :].rearrange("p a t -> p (a t)")
        hw = th_flat[0:NT, 0:4 * (P + 2)].rearrange("p (a t) -> p a t", a=4)
        xf = q32_flat[0:NT, 0:P + 2]
        feat = q32_flat[0:NT, 512:512 + NG * P].rearrange("p (a t) -> p a t", a=NG)
        z = sb("z", [P, TM * H]); za = sb("za", [P, TM * H]); ze = sb("ze", [P, TM * H]); zl = sb("zl", [P, TM * H])
        zm = sb("zm", [P, TM * H]); ld = sb("ld", [P, TM * H])
        ldp = sb("ldp", [P, TM, H, 2], f16)
        ct = sb("ct", [P, 3, TM, H])
        ex = sb("ex", [P, 3, TM, H])
        lda = sb("lda", [P, TM, 2 * H, P], f16)
        dec = sb("dec", [P, H, P])
        p32 = sb("p32", [P, H * P])
        pT = sb("pT", [P, 2, H * P], f16)
        kd32 = sb("kd32", [P, H, P])
        kd = sb("kd", [P, 2, H * P], f16)
        st32 = sb("st32", [P, H, P])
        stdec = sb("stdec", [P, H, P])
        st = sb("st", [P, 2, H * P], f16)
        ointer = sb("ointer", [P, H, P])
        o32 = sb("o32", [P, D])
        on = sb("on", [P, D])
        oms = sb("oms", [P, 2]); o_u = sb("o_u", [P, 2]); o_r = sb("o_r", [P, 2])
        oT = sb("oT", [P, 2, KD, P], f16)
        bst2 = sb("bst2", [P, 2, 6]); mv2 = sb("mv2", [P, 2, 2]); ln2_u = sb("ln2_u", [P, 2]); ln2_r = sb("ln2_r", [P, 2])
        xn2 = sb("xn2", [P, D])
        yq = sb("yq", [P, D], bf16)
        amax = sb("amax", [P, 2]); beta = sb("beta", [P, 2]); binv = sb("binv", [P, 2]); ab = sb("ab", [P, 2])
        xqT = sb("xqT", [P, KD, P], bf16)
        obuf = sb("obuf", [P, 2, D])
        wabs = sb("wabs", [P, 1]); alpha = sb("alpha", [P, 1]); ainv = sb("ainv", [P, 1])

        tp = [pb(f"tp{i}") for i in range(3)]
        mma, mmb = pb("mma"), pb("mmb")
        sco = pb("sco")
        dcs = pb("dcs")
        oxb = pb("oxb")
        tp2_bf = tp[2][:, 0:D // 2].bitcast(bf16)
        f_ps = oxb[:, 0:32].rearrange("p (s g) -> p s g", s=TM)
        ct_ps = oxb[:, 32:96]

        x_zero, x_in, small_in, const_set, const_ok, hash_step, feat_tr = map(sem, "x_zero x_in small_in const_set const_ok hash_step feat_tr".split())
        idx_ok, idx_copied, pool_gate, dve_gate, w_hi, w_lo, w_scaled = map(sem, "idx_ok idx_copied pool_gate dve_gate w_hi w_lo w_scaled".split())
        wf_hi, wf_lo, wabs_ok, wabs_mm, alpha_step, fq_step, fq_tr = map(sem, "wf_hi wf_lo wabs_ok wabs_mm alpha_step fq_step fq_tr".split())
        fq_ok, tok_mm, h0_ok, ms_ok, rms_u_ok, rms_ok, h_ok = map(sem, "fq_ok tok_mm h0_ok ms_ok rms_u_ok rms_ok h_ok".split())
        bst_ok, mv_ok, ln_u_ok, ln_ok, xn_ok, xn_tr, xnT_hi = map(sem, "bst_ok mv_ok ln_u_ok ln_ok xn_ok xn_tr xnT_hi".split())
        xnT_lo, v_mm, v_hi, v_lo, qk_mm, th_ok, qk32_ok = map(sem, "xnT_lo v_mm v_hi v_lo qk_mm th_ok qk32_ok".split())
        qk_hi, qk_lo, z_ok, za_ok, ze_ok, zl_ok, zm_ok = map(sem, "qk_hi qk_lo z_ok za_ok ze_ok zl_ok zm_ok".split())
        ld_ok, ldp_hi, ldp_ok, cum_mm, ct_sums, ct_ok, ex_ok = map(sem, "ld_ok ldp_hi ldp_ok cum_mm ct_sums ct_ok ex_ok".split())
        lda_ok, sc_mm, dc_mm, k_tr, dec_exp, dec_ok, p32_ok = map(sem, "lda_ok sc_mm dc_mm k_tr dec_exp dec_ok p32_ok".split())
        p_hi, p_lo, kd32_ok, kd_hi, kd_lo, stdec_ok, st32_ok = map(sem, "p_hi p_lo kd32_ok kd_hi kd_lo stdec_ok st32_ok".split())
        st_hi, st_lo, att_mm, ointer_ok, o32_ok, oms_ok, o_u_ok = map(sem, "st_hi st_lo att_mm ointer_ok o32_ok oms_ok o_u_ok".split())
        o_r_ok, on_ok, on_tr, oT_hi, oT_lo, wo_mm, h2_ok = map(sem, "o_r_ok on_ok on_tr oT_hi oT_lo wo_mm h2_ok".split())
        bst2_ok, mv2_ok, ln2_u_ok, ln2_ok, xn2_ok, amax_ok, beta_ok = map(sem, "bst2_ok mv2_ok ln2_u_ok ln2_ok xn2_ok amax_ok beta_ok".split())
        binv_ok, ab_ok, yq_ok, yq_tr, xqT_ok, ffn_mm, out_ok = map(sem, "binv_ok ab_ok yq_ok yq_tr xqT_ok ffn_mm out_ok".split())
        w_in = [sem(f"w_in{r}") for r in range(2 * H)]
        cat_in = [sem(f"cat_in{r}") for r in range(4)]
        cat_tr = [sem(f"cat_tr{g}") for g in range(NG)]
        cat_hi = [sem(f"cat_hi{g}") for g in range(NG)]
        cat_lo = [sem(f"cat_lo{g}") for g in range(NG)]
        first_copied = sem("first_copied")
        round_ok, wo_in, wo_hi, wo_lo = map(sem, "round_ok wo_in wo_hi wo_lo".split())
        stored = [sem(f"stored{r}") for r in range(2)]

        def tiles(b, c):
            return TS * b + c + 1

        def macros(b, c):
            return 2 * b + c // TM + 1

        def blocks(b, c, j):
            return 4 * H * b + 2 * H * (c // TM) + j + 1

        def states(b, c):
            return (TS - 1) * b + c - c // TS

        def dmas(b, c, ring, each):
            return each * ((TS // ring) * b + c // ring + 1)

        NSTG = 2 * H
        vs32 = vs[:, :, :, :].rearrange("p a t d -> p (a t d)").bitcast(f32).rearrange("p (t d) -> p t d", t=H)

        def stage(w):
            return (k32 if w % NSTG < H else vs32)[:, w % H, :]

        wo_stage = [t[:, :, :].rearrange("p h e -> p (h e)") for t in (kd32, st32, stdec, ointer)]

        WEIGHTS = [(W_tok, wt, k) for k in range(NG * KD)]
        WEIGHTS += [(src, dst, k) for src, dst in ((Wv, wv), (Wq, wq), (Wk, wk)) for k in range(KD)]
        NW = len(WEIGHTS)
        assert NW % NSTG == 0
        CUTS = [NG * KD, NG * KD + 4, NG * KD + 8, NW]

        def ffn_bank(nxt):
            return mmb if nxt else mma

        def on_bank(nxt):
            return tp[2] if nxt else tp[1]

        def qk_bank(j):
            return (mma, mmb, sco)[j % 3]

        def v_bank(c):
            return (sco, mmb, mma, mmb)[c % TM]

        def split3(mm, act_hi, act_lo, w_hi_, w_lo_, first, last):
            nc.tensor.matmul(mm, act_hi, w_hi_, start=first, stop=False)
            nc.tensor.matmul(mm, act_hi, w_lo_, start=False, stop=False)
            return nc.tensor.matmul(mm, act_lo, w_hi_, start=False, stop=last)

        block = ctx.enter_context(nc.Block())

        @block.sync
        def _(sp):
            sp.wait_ge(x_zero, 1)
            sp.dma_start(xi[:, 2:], x.rearrange("b (t p) -> (b t) p", p=P)).then_inc(x_in, 16)
            for q in range(0, NB, 2):
                sp.dma_start(xi[q * TS + 1:(q + 1) * TS, 0:2],
                             x[q, :].rearrange("(t p) -> t p", p=P)[0:TS - 1, P - 2:P]).then_inc(x_in, 16)
            sp.dma_start(bias_b[:, :], b_tok.partition_broadcast(P)).then_inc(small_in, 16)
            sp.dma_start(normt_b[:, :], norm_tok.partition_broadcast(P)).then_inc(small_in, 16)
            sp.dma_start(wf32[:, :, :], Wf.rearrange("(k p) h -> p k h", p=P)).then_inc(small_in, 16)
            with nc.allow_non_contiguous_dma(reason="512 numbers, once"):
                sp.dma_start(norma[:, :], norm_attn.rearrange("(k p) -> p k", p=P)).then_inc(small_in, 16)
            for w, (src, _, k) in enumerate(WEIGHTS):
                if w >= NSTG:
                    sp.wait_ge(w_hi, w - NSTG + 1)
                    sp.wait_ge(w_lo, w - NSTG + 1)
                sp.dma_start(stage(w), src[k * P:(k + 1) * P, :]).then_inc(w_in[w % NSTG], 16)
            for k in range(KD):
                w = NW + k
                sp.wait_ge(w_hi, w - NSTG + 1)
                sp.wait_ge(w_lo, w - NSTG + 1)
                sp.dma_start(stage(w), W_ffn[k * P:(k + 1) * P, :]).then_inc(w_in[w % NSTG], 16)
            for k in range(KD):
                sp.dma_start(wo_stage[k], Wo[k * P:(k + 1) * P, :]).then_inc(wo_in, 16)
            with sp.Fori(0, NB) as b:
                for c in range(TS):
                    sp.wait_ge(out_ok, tiles(b, c))
                    sp.dma_start(out_t[bass.ds(TS * b + c, 1), :, :].rearrange("a p d -> (a p) d"),
                                 obuf[:, c % 2, :]).then_inc(stored[c % 2], 16)
            for r in range(2):
                sp.wait_ge(stored[r], 16 * NT // 2)

        @block.gpsimd
        def _(pool):
            def gate():
                pool.sem_inc(pool_gate, 1)

            pool.memset(xi[:, :], 0).then_inc(x_zero, 1)
            pool.memset(ident[:, :], 0.0).then_inc(const_set, 1)
            pool.memset(before[:, :], 1.0).then_inc(const_set, 1)
            pool.memset(upto[:, :], 1.0).then_inc(const_set, 1)
            pool.memset(ones16[:, :], 1.0).then_inc(const_set, 1)
            pool.memset(ones32[:, :], 1.0).then_inc(const_set, 1)
            pool.memset(neghalf[:, :], -0.5).then_inc(const_set, 1)
            pool.memset(one_c[:, :], 1.0).then_inc(const_set, 1)
            pool.memset(ident16[:, :], 0.0).then_inc(const_set, 1)
            pool.wait_ge(const_set, 8)
            for m, op, mul, step in ((ident, ALU.not_equal, 1, -1), (ident16, ALU.not_equal, 1, -1), (before, ALU.is_gt, 1, -1), (upto, ALU.is_ge, -1, 1)):
                pool.affine_select(out=m[:, :], in_=m[:, :], compare_op=op, fill=1.0 if op == ALU.not_equal else 0.0, base=0,
                                   pattern=[[step, P]], channel_multiplier=mul).then_inc(const_ok, 1)

            def copy_indices(b, c):
                if not isinstance(b, int) or TS * b + c >= 2 * TM:
                    for r in range(TM):
                        pool.wait_ge(cat_in[r], dmas(b, c + r - 2 * TM, 4, 16 * NG))
                    gate()
                pool.tensor_copy(idx_now[:, c // TM % 2, :, :], idx[:, bass.ds(TS * b + c, TM), :]).then_inc(idx_copied, 1)
                pool.wait_ge(idx_copied, macros(b, c))
                gate()

            def gather_rows(c, g):
                pool.indirect_dma_start(
                    cat[:, c % 4, g * D:(g + 1) * D], None, (uni_table, ngram_table, ngram_table)[g],
                    bass.IndirectOffsetOnAxis(ap=idx_now[:, c // TM % 2, c % TM, g:g + 1], axis=0),
                ).then_inc(cat_in[c % 4], 16)

            def gather(b, c):
                pool.wait_ge(cat_tr[NG - 1], tiles(b, c - 4))
                gate()
                for g in range(NG):
                    gather_rows(c, g)

            def inv_sqrt(b, c, given, given_ok, u, u_ok, r, r_ok, op0, by0, op1, by1):
                pool.wait_ge(given_ok, tiles(b, c))
                gate()
                pool.tensor_scalar(u, given, by0, by1, op0, op1).then_inc(u_ok, 1)
                pool.wait_ge(u_ok, tiles(b, c))
                pool.tensor_tensor(r, u, neghalf[:, :], ALU.pow).then_inc(r_ok, 1)

            def rms(b, c):
                i = slice(c % 2, c % 2 + 1)
                inv_sqrt(b, c, ms[:, i], ms_ok, rms_u[:, i], rms_u_ok, rms_r[:, i], rms_ok, ALU.mult, 1.0 / D, ALU.add, RMS_EPS)

            def layer(b, c):
                i = slice(c % 2, c % 2 + 1)
                inv_sqrt(b, c, mv[:, c % 2, 1:2], mv_ok, ln_u[:, i], ln_u_ok, ln_r[:, i], ln_ok,
                         ALU.add, LN_EPS, ALU.mult, SX ** -2)

            def layer2(b, c):
                i = slice(c % 2, c % 2 + 1)
                inv_sqrt(b, c, mv2[:, c % 2, 1:2], mv2_ok, ln2_u[:, i], ln2_u_ok, ln2_r[:, i], ln2_ok,
                         ALU.add, LN_EPS, ALU.mult, 1.0)

            def attn_rms(b, c):
                i = slice(c % 2, c % 2 + 1)
                up = (SO / SX) ** 2
                inv_sqrt(b, c, oms[:, i], oms_ok, o_u[:, i], o_u_ok, o_r[:, i], o_r_ok, ALU.mult, up / D, ALU.add, up * RMS_EPS)

            def q_phase(b, c0, prev):
                if prev:
                    rms(b, c0 + 3)
                    layer(b, c0 + 3)
                    layer2(b, c0 - 1)
                pool.wait_ge(ldp_ok, macros(b, c0))
                for t in range(TM):
                    pool.tensor_tensor(
                        lda[:, t, :, :], before[:, :].unsqueeze(1).to_broadcast([P, 2 * H, P]),
                        ldp[:, t, :, :].rearrange("p h g -> p (h g)").unsqueeze(2).to_broadcast([P, 2 * H, P]),
                        ALU.mult).then_inc(lda_ok, 1)

            def a_phase(b, c0, nxt, more):
                if more:
                    copy_indices(b, c0 + 8)
                for t in range(TM):
                    c, n = c0 + t, c0 + t + TM
                    pool.wait_ge(dec_exp, tiles(b, c))
                    gate()
                    pool.affine_select(out=dec[:, :, :], in_=dec[:, :, :], compare_op=ALU.is_ge, fill=0.0, base=0,
                                       pattern=[[0, H], [1, P]], channel_multiplier=-1).then_inc(dec_ok, 1)
                    if nxt and t >= 1:
                        rms(b, n - 1)
                    if c % TS != TS - 1:
                        pool.wait_ge(kd_hi, states(b, c + 1))
                        pool.tensor_tensor(kd[:, 1, :], kd32[:, :, :].rearrange("p h e -> p (h e)"), kd[:, 0, :],
                                           ALU.subtract).then_inc(kd_lo, 1)
                    pool.wait_ge(p_hi, tiles(b, c))
                    pool.tensor_tensor(pT[:, 1, :], p32[:, :], pT[:, 0, :], ALU.subtract).then_inc(p_lo, 1)
                    if nxt and t >= 1:
                        layer(b, n - 1)
                    if 0 < c % TS < TS - 1:
                        pool.wait_ge(st32_ok, states(b, c))
                        pool.tensor_tensor(stdec[:, :, :], st32[:, :, :], ex[:, 1, t, :].unsqueeze(2).to_broadcast([P, H, P]),
                                           ALU.mult).then_inc(stdec_ok, 1)
                    if t >= 1:
                        layer2(b, c - 1)
                    if more:
                        gather(b, c + 8)
                    attn_rms(b, c)
                    if c % TS != TS - 1:
                        pool.wait_ge(st_hi, states(b, c + 1))
                        pool.tensor_tensor(st[:, 1, :], st32[:, :, :].rearrange("p h f -> p (h f)"), st[:, 0, :],
                                           ALU.subtract).then_inc(st_lo, 1)

            pool.wait_ge(idx_ok, 1)
            pool.tensor_copy(idx_now[:, 0, :, 0:1], idx[:, 0:TM, 0:1]).then_inc(first_copied, 1)
            pool.wait_ge(first_copied, 1)
            for c in range(TM):
                gather_rows(c, 0)
            pool.wait_ge(idx_ok, 2)
            pool.tensor_copy(idx_now[:, 0, :, 1:NG], idx[:, 0:TM, 1:NG]).then_inc(idx_copied, 1)
            pool.wait_ge(idx_copied, 1)
            for c in range(TM):
                for g in range(1, NG):
                    gather_rows(c, g)
            copy_indices(0, TM)
            for c in range(TM):
                rms(0, c)
                layer(0, c)
                gather(0, c + TM)
            q_phase(0, 0, False)
            with pool.Fori(0, NB - 1) as b:
                a_phase(b, 0, True, True)
                q_phase(b, TM, True)
                a_phase(b, TM, True, True)
                q_phase(b, 2 * TM, True)
            a_phase(NB - 1, 0, True, False)
            q_phase(NB - 1, TM, True)
            a_phase(NB - 1, TM, False, False)
            layer2(NB - 1, TS - 1)

        @block.tensor
        def _(pe):
            def cat_transpose(b, c, g):
                if g == 0:
                    pe.wait_ge(cat_in[c % 4], dmas(b, c, 4, 16 * NG))
                for j in range(KD):
                    k = g * KD + j
                    last = nc.tensor.transpose(tp[g][:, j * P:(j + 1) * P], cat[:, c % 4, k * P:(k + 1) * P], ident[:, :])
                last.then_inc(cat_tr[g], 1)

            def tok_matmul(b, c, g):
                pe.wait_ge(cat_hi[g], tiles(b, c))
                pe.wait_ge(cat_lo[g], tiles(b, c))
                for j in range(KD):
                    k = g * KD + j
                    last = split3(mma[:, :], catT[:, 0, k, :], catT[:, 1, k, :], wt[:, 0, k, :], wt[:, 1, k, :],
                                  k == 0, k == NG * KD - 1)
                if g == NG - 1:
                    last.then_inc(tok_mm, 1)

            def four_transposes(bank, src, done):
                for j in range(KD):
                    last = nc.tensor.transpose(bank[:, j * P:(j + 1) * P], src[:, j * P:(j + 1) * P], ident[:, :])
                last.then_inc(done, 1)

            def xn_transpose(b, c):
                pe.wait_ge(xn_ok, tiles(b, c))
                four_transposes(tp[1], xn, xn_tr)

            def on_transpose(b, c, nxt=True):
                pe.wait_ge(on_ok, tiles(b, c))
                four_transposes(on_bank(nxt), on, on_tr)

            def yq_transpose(b, c):
                pe.wait_ge(yq_ok, tiles(b, c))
                for j in range(KD):
                    last = nc.tensor.transpose(tp2_bf[:, j * P:(j + 1) * P], yq[:, j * P:(j + 1) * P], ident16[:, :])
                last.then_inc(yq_tr, 1)

            def out_proj(b, c, bank):
                pe.wait_ge(oT_hi, tiles(b, c))
                pe.wait_ge(oT_lo, tiles(b, c))
                for k in range(KD):
                    last = split3(bank[:, :], oT[:, 0, k, :], oT[:, 1, k, :], wo[:, 0, k, :], wo[:, 1, k, :], k == 0, k == KD - 1)
                last.then_inc(wo_mm, 1)

            def ffn(b, c, bank):
                pe.wait_ge(xqT_ok, tiles(b, c))
                for k in range(KD):
                    last = nc.tensor.matmul(bank[:, :], xqT[:, k, :], wffn[:, k, :], start=k == 0, stop=k == KD - 1)
                last.then_inc(ffn_mm, 1)

            def v_proj(b, c):
                t = c % TM
                tok = slice(t * P, (t + 1) * P)
                bank = v_bank(c)
                pe.wait_ge(xnT_hi, tiles(b, c))
                pe.wait_ge(xnT_lo, tiles(b, c))
                for k in range(KD):
                    hi, lo = xnT[:, 0, k, tok], xnT[:, 1, k, tok]
                    wf_k = wf[:, k, :, :].rearrange("p h g -> p (h g)")
                    nc.tensor.matmul(f_ps[:, t, :], hi, wf_k, start=k == 0, stop=False)
                    nc.tensor.matmul(f_ps[:, t, :], lo, wf_k, start=False, stop=k == KD - 1)
                    last = split3(bank[:, :], hi, lo, wv[:, 0, k, :], wv[:, 1, k, :], k == 0, k == KD - 1)
                last.then_inc(v_mm, 1)

            def qk_proj(b, c0, j):
                bank, w, h = qk_bank(j), (wq, wk)[j // H], j % H
                if j < 2:
                    pe.wait_ge(v_hi, tiles(b, c0 + 2 + j))
                    pe.wait_ge(v_lo, tiles(b, c0 + 2 + j))
                elif j >= 3:
                    pe.wait_ge(th_ok, blocks(b, c0, j - 3))
                    pe.wait_ge(qk32_ok, blocks(b, c0, j - 3))
                for k in range(KD):
                    last = split3(bank[:, :], w[:, 0, k, h * P:(h + 1) * P], w[:, 1, k, h * P:(h + 1) * P],
                                  xnT[:, 0, k, :], xnT[:, 1, k, :], k == 0, k == KD - 1)
                last.then_inc(qk_mm, 1)

            def sums(b, c0):
                pe.wait_ge(ldp_ok, macros(b, c0))
                parts = ldp[:, :, :, :].rearrange("p t h g -> p (t h g)")
                nc.tensor.matmul(ct_ps[:, 0:32], upto[:, :], parts, start=True, stop=True)
                nc.tensor.matmul(ct_ps[:, 32:64], ones16[:, :], parts, start=True, stop=True).then_inc(cum_mm, 1)

            def fq_transposes(lo, hi):
                for k in range(lo, hi):
                    pe.wait_ge(fq_step, 2 * (k + 1))
                    if k >= 2:
                        pe.wait_ge(fq_ok, k - 1)
                    for j in range(KD):
                        last = nc.tensor.transpose((tp[2], dcs)[k % 2][:, j * P:(j + 1) * P],
                                                   stage(NW + k)[:, j * P:(j + 1) * P], ident[:, :])
                    last.then_inc(fq_tr, 1)

            def q_phase(b, c0, prev, nxt):
                p2, p3 = c0 - 2, c0 - 1
                if prev:
                    pe.wait_ge(ointer_ok, states(b, p3))
                    pe.wait_ge(o32_ok, tiles(b, p3))
                v_proj(b, c0)
                if prev:
                    pe.wait_ge(xqT_ok, tiles(b, p2))
                    on_transpose(b, p3)
                    pe.wait_ge(out_ok, tiles(b, c0 - 3))
                v_proj(b, c0 + 1)
                if prev:
                    if p3 % TS != TS - 1:
                        pe.wait_ge(st32_ok, states(b, c0))
                    else:
                        pe.wait_ge(dec_exp, tiles(b, p3))
                    out_proj(b, p3, dcs)
                pe.wait_ge(cat_hi[1], tiles(b, c0 + 3))
                pe.wait_ge(cat_lo[1], tiles(b, c0 + 3))
                xn_transpose(b, c0 + 3)
                pe.wait_ge(h0_ok, tiles(b, c0 + 3))
                v_proj(b, c0 + 2)
                if prev:
                    pe.wait_ge(h2_ok, tiles(b, p3))
                    ffn(b, p2, dcs)
                pe.wait_ge(v_hi, tiles(b, c0 + 1))
                pe.wait_ge(v_lo, tiles(b, c0 + 1))
                v_proj(b, c0 + 3)
                qk_proj(b, c0, 0)
                qk_proj(b, c0, 1)
                if prev:
                    yq_transpose(b, p3)
                else:
                    fq_transposes(0, 2)
                qk_proj(b, c0, 2)
                qk_proj(b, c0, 3)
                if not prev:
                    fq_transposes(2, KD)
                qk_proj(b, c0, 4)
                if nxt:
                    if prev:
                        pe.wait_ge(kd32_ok, tiles(b, p3))
                    else:
                        pe.wait_ge(cat_hi[0], tiles(b, c0 + 3))
                        pe.wait_ge(cat_lo[0], tiles(b, c0 + 3))
                    cat_transpose(b, c0 + TM, 0)
                sums(b, c0)
                qk_proj(b, c0, 5)
                if prev:
                    pe.wait_ge(out_ok, tiles(b, p2))
                    ffn(b, p3, dcs)
                qk_proj(b, c0, 6)
                qk_proj(b, c0, 7)
                pe.wait_ge(th_ok, blocks(b, c0, 5))
                pe.wait_ge(qk32_ok, blocks(b, c0, 5))
                if prev:
                    pe.wait_ge(out_ok, tiles(b, p3))
                    pe.wait_ge(xqT_ok, tiles(b, p3))

            def scores(b, c):
                tok = slice(c % TM * P, (c % TM + 1) * P)
                for h in range(H):
                    last = split3(sco[:, h * P:(h + 1) * P], kT[:, 0, h, tok], kT[:, 1, h, tok],
                                  qT[:, 0, h, tok], qT[:, 1, h, tok], True, True)
                last.then_inc(sc_mm, 1)

            def decays(b, c):
                for h in range(H):
                    for g in range(2):
                        last = nc.tensor.matmul(dcs[:, h * P:(h + 1) * P], lda[:, c % TM, 2 * h + g, :], upto[:, :],
                                                start=g == 0, stop=g == 1)
                last.then_inc(dc_mm, 1)

            def k_transpose(b, c):
                for h in range(H):
                    last = nc.tensor.transpose(tp[0][:, h * P:(h + 1) * P], k32[:, h, c % TM * P:(c % TM + 1) * P], ident[:, :])
                last.then_inc(k_tr, 1)

            def attend(b, c):
                t = c % TM
                tok = slice(t * P, (t + 1) * P)
                heads = [slice(h * P, (h + 1) * P) for h in range(H)]
                if t == 0:
                    pe.wait_ge(v_lo, tiles(b, c + 3))
                if c % TS != 0:
                    pe.wait_ge(st_hi, states(b, c))
                    pe.wait_ge(st_lo, states(b, c))
                    if t == 0:
                        pe.wait_ge(ct_sums, macros(b, c))
                    for h, hd in enumerate(heads):
                        split3(oxb[:, hd], qT[:, 0, h, tok], qT[:, 1, h, tok], st[:, 0, hd], st[:, 1, hd], True, True)
                if c % TS != TS - 1:
                    pe.wait_ge(kd_hi, states(b, c + 1))
                    pe.wait_ge(kd_lo, states(b, c + 1))
                    pe.wait_ge(dec_exp, tiles(b, c))
                    for hd in heads:
                        split3(dcs[:, hd], kd[:, 0, hd], kd[:, 1, hd], vs[:, 0, t, hd], vs[:, 1, t, hd], True, True)
                pe.wait_ge(p_hi, tiles(b, c))
                pe.wait_ge(p_lo, tiles(b, c))
                for hd in heads:
                    last = split3(sco[:, hd], pT[:, 0, hd], pT[:, 1, hd], vs[:, 0, t, hd], vs[:, 1, t, hd], True, True)
                last.then_inc(att_mm, 1)

            def tile_scores(b, c, nxt, first):
                pe.wait_ge(lda_ok, tiles(b, c))
                if not first:
                    pe.wait_ge(st32_ok, states(b, c))
                decays(b, c)
                if first:
                    pe.wait_ge(qk_hi, blocks(b, c, 2 * H - 1))
                    pe.wait_ge(qk_lo, blocks(b, c, 2 * H - 1))
                else:
                    pe.wait_ge(o32_ok, tiles(b, c - 1))
                scores(b, c)
                if nxt:
                    pe.wait_ge(cat_hi[0], tiles(b, c + TM))
                    pe.wait_ge(cat_lo[0], tiles(b, c + TM))
                else:
                    pe.wait_ge(kd32_ok, tiles(b, c - 1))
                k_transpose(b, c)

            def a_phase(b, c0, nxt):
                c, n = c0, c0 + TM
                if nxt:
                    pe.wait_ge(xnT_hi, tiles(b, n - 1))
                    pe.wait_ge(xnT_lo, tiles(b, n - 1))
                    cat_transpose(b, n, 1)
                    pe.wait_ge(th_ok, blocks(b, c0, 2 * H - 2))
                    pe.wait_ge(qk32_ok, blocks(b, c0, 2 * H - 2))
                    tok_matmul(b, n, 0)
                tile_scores(b, c, nxt, True)
                if nxt:
                    cat_transpose(b, n, 2)
                    tok_matmul(b, n, 1)
                attend(b, c)
                if nxt:
                    pe.wait_ge(kd32_ok, tiles(b, c))
                    cat_transpose(b, n + 1, 0)
                    tok_matmul(b, n, 2)
                for t in range(1, TM):
                    c, n = c0 + t, c0 + t + TM
                    tile_scores(b, c, nxt, False)
                    if t >= 2 and nxt:
                        pe.wait_ge(xqT_ok, tiles(b, c - 2))
                    elif nxt:
                        pe.wait_ge(cat_hi[2], tiles(b, n - 1))
                        pe.wait_ge(cat_lo[2], tiles(b, n - 1))
                    elif t >= 2:
                        yq_transpose(b, c - 2)
                    on_transpose(b, c - 1, nxt)
                    if nxt:
                        if t == 1:
                            pe.wait_ge(cat_hi[1], tiles(b, n - 1))
                            pe.wait_ge(cat_lo[1], tiles(b, n - 1))
                        else:
                            pe.wait_ge(xnT_hi, tiles(b, n - 2))
                            pe.wait_ge(xnT_lo, tiles(b, n - 2))
                        cat_transpose(b, n, 1)
                        pe.wait_ge(h0_ok, tiles(b, n - 1))
                        tok_matmul(b, n, 0)
                    if t == 1:
                        pe.wait_ge(th_ok, blocks(b, c0, 2 * H - 1))
                        pe.wait_ge(qk32_ok, blocks(b, c0, 2 * H - 1))
                    elif t == 2 or not nxt:
                        pe.wait_ge(h2_ok, tiles(b, c - 2))
                    elif t == 3:
                        pe.wait_ge(out_ok, tiles(b, c - 3))
                    out_proj(b, c - 1, mmb)
                    if nxt:
                        cat_transpose(b, n, 2)
                    attend(b, c)
                    if t >= 2:
                        if nxt:
                            pe.wait_ge(h2_ok, tiles(b, c - 1))
                        elif t == 2:
                            pe.wait_ge(th_ok, blocks(b, c0, 2 * H - 2))
                            pe.wait_ge(qk32_ok, blocks(b, c0, 2 * H - 2))
                        else:
                            pe.wait_ge(out_ok, tiles(b, c - 3))
                        ffn(b, c - 2, ffn_bank(nxt))
                    if nxt:
                        tok_matmul(b, n, 1)
                        xn_transpose(b, n - 1)
                        if t <= 2:
                            pe.wait_ge(kd32_ok, tiles(b, c))
                            cat_transpose(b, n + 1, 0)
                        tok_matmul(b, n, 2)
                        yq_transpose(b, c - 1)

            pe.wait_ge(const_ok, 4)
            pe.wait_ge(hash_step, 2)
            nc.tensor.transpose(sco[:, 0:NT], feat[:, 0, :], ident[0:NT, 0:NT]).then_inc(feat_tr, 1)
            pe.wait_ge(hash_step, HASH_STEPS)
            for g in range(1, NG):
                last = nc.tensor.transpose(dcs[:, g * NT:(g + 1) * NT], feat[:, g, :], ident[0:NT, 0:NT])
            last.then_inc(feat_tr, 1)
            cat_transpose(0, 0, 0)
            for c in range(TM):
                if c >= 1:
                    pe.wait_ge(cat_hi[1], c)
                    pe.wait_ge(cat_lo[1], c)
                if c >= 2:
                    pe.wait_ge(xnT_hi, c - 1)
                    pe.wait_ge(xnT_lo, c - 1)
                cat_transpose(0, c, 1)
                if c >= 1:
                    pe.wait_ge(h0_ok, c)
                else:
                    pe.wait_ge(w_lo, KD)
                tok_matmul(0, c, 0)
                if c >= 1:
                    pe.wait_ge(cat_hi[2], c)
                    pe.wait_ge(cat_lo[2], c)
                cat_transpose(0, c, 2)
                if c == 0:
                    pe.wait_ge(w_lo, 2 * KD)
                tok_matmul(0, c, 1)
                if c >= 1:
                    xn_transpose(0, c - 1)
                if c < TM - 1:
                    cat_transpose(0, c + 1, 0)
                if c == 0:
                    pe.wait_ge(w_lo, 3 * KD)
                tok_matmul(0, c, 2)
            pe.wait_ge(wabs_ok, 1)
            nc.tensor.matmul(dcs[:, 0:1], ones32[:, :], wabs[:, :], start=True, stop=True).then_inc(wabs_mm, 1)
            pe.wait_ge(w_hi, NW)
            pe.wait_ge(w_lo, NW)
            pe.wait_ge(wf_lo, 1)
            q_phase(0, 0, False, True)
            pe.wait_ge(fq_ok, KD)
            pe.wait_ge(wo_hi, KD)
            pe.wait_ge(wo_lo, KD)
            with pe.Fori(0, NB - 1) as b:
                a_phase(b, 0, True)
                q_phase(b, TM, True, True)
                a_phase(b, TM, True)
                q_phase(b, 2 * TM, True, True)
            b = NB - 1
            a_phase(b, 0, True)
            q_phase(b, TM, True, False)
            a_phase(b, TM, False)
            yq_transpose(b, TS - 2)
            on_transpose(b, TS - 1, False)
            pe.wait_ge(h2_ok, tiles(b, TS - 2))
            out_proj(b, TS - 1, mmb)
            pe.wait_ge(out_ok, tiles(b, TS - 3))
            ffn(b, TS - 2, mma)
            yq_transpose(b, TS - 1)
            ffn(b, TS - 1, sco)

        @block.scalar
        def _(act):
            copy = nc.scalar.activation

            def w_split(lo, hi):
                for w in range(lo, hi):
                    _, dst, k = WEIGHTS[w]
                    act.wait_ge(w_in[w % NSTG], 16 * (w // NSTG + 1))
                    copy(dst[:, 0, k, :], stage(w), ACT.Copy, scale=SW).then_inc(w_hi, 1)

            def cat_split(b, c, g):
                act.wait_ge(cat_tr[g], tiles(b, c))
                copy(catT[:, 0, g * KD:(g + 1) * KD, :], tp[g][:, :].rearrange("p (k t) -> p k t", k=KD), ACT.Copy,
                     scale=SW).then_inc(cat_hi[g], 1)

            def mean_square(b, c):
                act.wait_ge(h0_ok, tiles(b, c))
                copy(junk[:, :], hbuf[:, c % TS, :], ACT.Square, accum_out=ms[:, c % 2:c % 2 + 1]).then_inc(ms_ok, 1)

            def xnT_split(b, c):
                act.wait_ge(xn_tr, tiles(b, c))
                copy(xnT[:, 0, :, c % TM * P:(c % TM + 1) * P], tp[1][:, :].rearrange("p (k t) -> p k t", k=KD),
                     ACT.Copy).then_inc(xnT_hi, 1)

            def oT_split(b, c, nxt=True):
                act.wait_ge(on_tr, tiles(b, c))
                copy(oT[:, 0, :, :], on_bank(nxt)[:, :].rearrange("p (k t) -> p k t", k=KD), ACT.Copy).then_inc(oT_hi, 1)

            def xq_split(b, c):
                act.wait_ge(yq_tr, tiles(b, c))
                copy(xqT[:, :, :], tp2_bf.rearrange("p (k t) -> p k t", k=KD), ACT.Copy).then_inc(xqT_ok, 1)

            def v_split(b, c):
                t = c % TM
                act.wait_ge(v_mm, tiles(b, c))
                copy(vs[:, 0, t, :], v_bank(c)[:, :], ACT.Copy, scale=SQ / (SX * SW)).then_inc(v_hi, 1)

            def qk_tanh(b, c0, j):
                act.wait_ge(qk_mm, blocks(b, c0, j))
                if j >= 2:
                    act.wait_ge(qk32_ok, blocks(b, c0, j - 2))
                copy(th[:, j % 2, :], qk_bank(j)[:, :], ACT.Tanh, scale=0.5 / (SX * SW)).then_inc(th_ok, 1)

            def qk_split(b, c0, j):
                dst, src = (qT, q32[:, j % 2, :]) if j < H else (kT, k32[:, j - H, :])
                act.wait_ge(qk32_ok, blocks(b, c0, j))
                copy(dst[:, 0, j % H, :], src, ACT.Copy, scale=SQ / (2 * SX * SW)).then_inc(qk_hi, 1)

            def q_phase(b, c0, prev, nxt):
                if prev:
                    mean_square(b, c0 + 3)
                v_split(b, c0)
                if prev:
                    oT_split(b, c0 - 1)
                v_split(b, c0 + 1)
                xnT_split(b, c0 + 3)
                v_split(b, c0 + 2)
                v_split(b, c0 + 3)
                if not prev:
                    for k in range(KD):
                        act.wait_ge(w_scaled, k + 1)
                        copy(wo[:, 0, k, :], wo_stage[k], ACT.Copy, scale=SW).then_inc(wo_hi, 1)
                m = macros(b, c0)
                for j in range(2 * H):
                    qk_tanh(b, c0, j)
                    qk_split(b, c0, j)
                    if j == 1:
                        act.wait_ge(z_ok, m)
                        copy(za[:, :], z[:, :], ACT.Abs, scale=1.0 / (SX * SW)).then_inc(za_ok, 1)
                        act.wait_ge(za_ok, m)
                        copy(ze[:, :], za[:, :], ACT.Exp, scale=-1.0).then_inc(ze_ok, 1)
                        act.wait_ge(ze_ok, m)
                        copy(zl[:, :], ze[:, :], ACT.Ln, bias=one_c[:, :]).then_inc(zl_ok, 1)
                    if j == 3 and prev:
                        xq_split(b, c0 - 1)
                    if j == 5:
                        act.wait_ge(ct_ok, m)
                        copy(ex[:, :, :, :].rearrange("p a t h -> p (a t h)"), ct[:, :, :, :].rearrange("p a t h -> p (a t h)"),
                             ACT.Exp, scale=1.0 / SP).then_inc(ex_ok, 1)
                        if nxt:
                            cat_split(b, c0 + TM, 0)

            def a_phase(b, c0, nxt):
                for t in range(TM):
                    c, n = c0 + t, c0 + t + TM
                    if nxt and t == 0:
                        cat_split(b, n, 1)
                    act.wait_ge(dc_mm, tiles(b, c))
                    copy(dec[:, :, :].rearrange("p h i -> p (h i)"), dcs[:, :], ACT.Exp, scale=1.0 / SP).then_inc(dec_exp, 1)
                    if nxt and t >= 1:
                        mean_square(b, n - 1)
                    if t >= 1:
                        oT_split(b, c - 1, nxt)
                    if t >= 2 and not nxt:
                        xq_split(b, c - 2)
                    if nxt and t >= 1:
                        cat_split(b, n, 1)
                    if c % TS != TS - 1:
                        act.wait_ge(kd32_ok, tiles(b, c))
                        copy(kd[:, 0, :], kd32[:, :, :].rearrange("p h e -> p (h e)"), ACT.Copy).then_inc(kd_hi, 1)
                    act.wait_ge(p32_ok, tiles(b, c))
                    copy(pT[:, 0, :], p32[:, :], ACT.Copy).then_inc(p_hi, 1)
                    if nxt:
                        cat_split(b, n, 2)
                    act.wait_ge(att_mm, tiles(b, c))
                    if c % TS != 0:
                        for h in range(H):
                            last = copy(ointer[:, h, :], oxb[:, h * P:(h + 1) * P], ACT.Copy, scale=ex[:, 0, t, h:h + 1])
                        last.then_inc(ointer_ok, 1)
                    if c % TS != TS - 1:
                        act.wait_ge(st32_ok, states(b, c + 1))
                        copy(st[:, 0, :], st32[:, :, :].rearrange("p h f -> p (h f)"), ACT.Copy).then_inc(st_hi, 1)
                    if nxt and t == 0:
                        cat_split(b, n + 1, 0)
                    act.wait_ge(o32_ok, tiles(b, c))
                    copy(junk[:, :], o32[:, :], ACT.Square, scale=1.0 / SO, accum_out=oms[:, c % 2:c % 2 + 1]).then_inc(oms_ok, 1)
                    act.wait_ge(o_r_ok, tiles(b, c))
                    copy(on[:, :], o32[:, :], ACT.Copy, scale=o_r[:, c % 2:c % 2 + 1]).then_inc(on_ok, 1)
                    if nxt and t >= 1:
                        xnT_split(b, n - 1)
                    if nxt and 1 <= t <= 2:
                        cat_split(b, n + 1, 0)
                    if nxt and t >= 1:
                        xq_split(b, c - 1)

            act.wait_ge(x_zero, 1)
            for q in range(1, NB, 2):
                act.dma_start(xi[q * TS + 1:(q + 1) * TS, 0:2],
                              x[q, :].rearrange("(t p) -> t p", p=P)[0:TS - 1, P - 2:P]).then_inc(x_in, 16)
            w_split(0, KD)
            cat_split(0, 0, 0)
            w_split(KD, 2 * KD)
            cat_split(0, 0, 1)
            w_split(2 * KD, 3 * KD)
            cat_split(0, 0, 2)
            cat_split(0, 1, 0)
            act.wait_ge(small_in, 64)
            copy(wf[:, :, :, 0], wf32[:, :, :], ACT.Copy, scale=SW).then_inc(wf_hi, 1)
            for c in range(1, TM):
                mean_square(0, c - 1)
                cat_split(0, c, 1)
                cat_split(0, c, 2)
                w_split(CUTS[c - 1], CUTS[c])
                xnT_split(0, c - 1)
                if c < TM - 1:
                    cat_split(0, c + 1, 0)
            mean_square(0, TM - 1)
            q_phase(0, 0, False, True)
            with act.Fori(0, NB - 1) as b:
                a_phase(b, 0, True)
                q_phase(b, TM, True, True)
                a_phase(b, TM, True)
                q_phase(b, 2 * TM, True, True)
            b = NB - 1
            a_phase(b, 0, True)
            q_phase(b, TM, True, False)
            a_phase(b, TM, False)
            xq_split(b, TS - 2)
            oT_split(b, TS - 1, False)
            xq_split(b, TS - 1)

        @block.vector
        def _(dve):
            V = nc.vector

            def k_t(bank):
                return bank[:, :].rearrange("p (k t) -> p k t", k=KD)

            def w_split(lo, hi):
                for w in range(lo, hi):
                    _, dst, k = WEIGHTS[w]
                    dve.wait_ge(w_in[w % NSTG], 16 * (w // NSTG + 1))
                    dve.wait_ge(w_hi, w + 1)
                    V.scalar_tensor_tensor(dst[:, 1, k, :], stage(w), SW, dst[:, 0, k, :], ALU.mult, ALU.subtract).then_inc(w_lo, 1)

            def cat_split(b, c, g):
                dve.wait_ge(cat_hi[g], tiles(b, c))
                gs = slice(g * KD, (g + 1) * KD)
                V.scalar_tensor_tensor(catT[:, 1, gs, :], k_t(tp[g]), SW, catT[:, 0, gs, :], ALU.mult,
                                       ALU.subtract).then_inc(cat_lo[g], 1)

            def tok_out(b, c):
                dve.wait_ge(tok_mm, tiles(b, c))
                V.scalar_tensor_tensor(hbuf[:, c % TS, :], mma[:, :], SW ** -2, bias_b[:, :], ALU.mult, ALU.add).then_inc(h0_ok, 1)

            def stats(b, c, given_ok, st6, st6_ok, out2, out2_ok):
                dve.wait_ge(given_ok, tiles(b, c))
                V.bn_stats(st6[:, c % 2, :], hbuf[:, c % TS, :]).then_inc(st6_ok, 1)
                dve.wait_ge(st6_ok, tiles(b, c))
                dve.sem_inc(dve_gate, 1)
                V.bn_aggr(out2[:, c % 2, :], st6[:, c % 2, :]).then_inc(out2_ok, 1)

            def tok_norm(b, c):
                dve.wait_ge(rms_ok, tiles(b, c))
                V.scalar_tensor_tensor(hbuf[:, c % TS, :], hbuf[:, c % TS, :], rms_r[:, c % 2:c % 2 + 1], normt_b[:, :],
                                       ALU.mult, ALU.mult).then_inc(h_ok, 1)
                stats(b, c, h_ok, bst, bst_ok, mv, mv_ok)

            def tok_xn(b, c):
                dve.wait_ge(ln_ok, tiles(b, c))
                V.tensor_scalar(xn[:, :], hbuf[:, c % TS, :], mv[:, c % 2, 0:1], ln_r[:, c % 2:c % 2 + 1], ALU.subtract,
                                ALU.mult).then_inc(xn_ok, 1)

            def xnT_split(b, c):
                tok = slice(c % TM * P, (c % TM + 1) * P)
                dve.wait_ge(xnT_hi, tiles(b, c))
                V.tensor_tensor(xnT[:, 1, :, tok], k_t(tp[1]), xnT[:, 0, :, tok], ALU.subtract).then_inc(xnT_lo, 1)

            def v_split(b, c):
                t = c % TM
                dve.wait_ge(v_hi, tiles(b, c))
                V.scalar_tensor_tensor(vs[:, 1, t, :], v_bank(c)[:, :], SQ / (SX * SW), vs[:, 0, t, :], ALU.mult,
                                       ALU.subtract).then_inc(v_lo, 1)

            def silu(b, c0, j):
                dst = q32[:, j % 2, :] if j < H else k32[:, j - H, :]
                dve.wait_ge(th_ok, blocks(b, c0, j))
                if 2 <= j < H:
                    dve.wait_ge(qk_hi, blocks(b, c0, j - 2))
                V.scalar_tensor_tensor(dst, th[:, j % 2, :], 1.0, qk_bank(j)[:, :], ALU.add, ALU.mult).then_inc(qk32_ok, 1)

            def qk_split(b, c0, j):
                dst, src = (qT, q32[:, j % 2, :]) if j < H else (kT, k32[:, j - H, :])
                dve.wait_ge(qk_hi, blocks(b, c0, j))
                V.scalar_tensor_tensor(dst[:, 1, j % H, :], src, SQ / (2 * SX * SW), dst[:, 0, j % H, :], ALU.mult,
                                       ALU.subtract).then_inc(qk_lo, 1)

            def log_decay_begin(b, c0):
                m = macros(b, c0)
                dve.wait_ge(v_mm, tiles(b, c0 + 3))
                V.tensor_reduce(z[:, :], f_ps.rearrange("p t (h g) -> p (t h) g", g=2), AX.X, ALU.add).then_inc(z_ok, 1)
                dve.wait_ge(z_ok, m)
                V.tensor_scalar(zm[:, :], z[:, :], SP / (SX * SW), 0.0, ALU.mult, ALU.min).then_inc(zm_ok, 1)

            def log_decay_end(b, c0):
                m = macros(b, c0)
                dve.wait_ge(zl_ok, m)
                dve.wait_ge(zm_ok, m)
                V.scalar_tensor_tensor(ld[:, :], zl[:, :], -SP, zm[:, :], ALU.mult, ALU.add).then_inc(ld_ok, 1)
                ld_v = ld[:, :].rearrange("p (t h) -> p t h", t=TM)
                dve.wait_ge(ld_ok, m)
                V.tensor_copy(ldp[:, :, :, 0], ld_v).then_inc(ldp_hi, 1)
                dve.wait_ge(ldp_hi, m)
                V.tensor_tensor(ldp[:, :, :, 1], ld_v, ldp[:, :, :, 0], ALU.subtract).then_inc(ldp_ok, 1)

            def decay_sums(b, c0):
                m = macros(b, c0)
                dve.wait_ge(cum_mm, m)
                V.tensor_reduce(ct[:, 0:2, :, :].rearrange("p a t h -> p (a t h)"),
                                ct_ps.rearrange("p (a g) -> p a g", g=2), AX.X, ALU.add).then_inc(ct_sums, 1)
                dve.wait_ge(ct_sums, m)
                V.tensor_tensor(ct[:, 2, :, :], ct[:, 1, :, :], ct[:, 0, :, :], ALU.subtract).then_inc(ct_ok, 1)

            def oT_split(b, c, nxt=True):
                dve.wait_ge(oT_hi, tiles(b, c))
                V.tensor_tensor(oT[:, 1, :, :], k_t(on_bank(nxt)), oT[:, 0, :, :], ALU.subtract).then_inc(oT_lo, 1)

            def attn_residual(b, c, bank):
                dve.wait_ge(wo_mm, tiles(b, c))
                V.scalar_tensor_tensor(hbuf[:, c % TS, :], bank[:, :], 1.0 / (SX * SW), hbuf[:, c % TS, :], ALU.mult,
                                       ALU.add).then_inc(h2_ok, 1)
                stats(b, c, h2_ok, bst2, bst2_ok, mv2, mv2_ok)

            def quantise(b, c):
                i = slice(c % 2, c % 2 + 1)
                dve.wait_ge(ln2_ok, tiles(b, c))
                V.tensor_scalar(xn2[:, :], hbuf[:, c % TS, :], mv2[:, c % 2, 0:1], ln2_r[:, i], ALU.subtract,
                                ALU.mult).then_inc(xn2_ok, 1)
                dve.wait_ge(xn2_ok, tiles(b, c))
                V.tensor_reduce(amax[:, i], xn2[:, :], AX.X, ALU.max, apply_absolute_value=True).then_inc(amax_ok, 1)
                dve.wait_ge(amax_ok, tiles(b, c))
                V.tensor_scalar(beta[:, i], amax[:, i], 1.0 / 127.0, Q_EPS, ALU.mult, ALU.max).then_inc(beta_ok, 1)
                dve.wait_ge(beta_ok, tiles(b, c))
                V.reciprocal(binv[:, i], beta[:, i]).then_inc(binv_ok, 1)
                V.tensor_scalar(ab[:, i], beta[:, i], alpha[:, :], None, ALU.mult).then_inc(ab_ok, 1)
                dve.wait_ge(binv_ok, tiles(b, c))
                V.tensor_scalar(xn2[:, :], xn2[:, :], binv[:, i], MAGIC, ALU.mult, ALU.add).then_inc(round_ok, 1)
                dve.wait_ge(round_ok, tiles(b, c))
                V.tensor_scalar(yq[:, :], xn2[:, :], MAGIC, None, ALU.subtract).then_inc(yq_ok, 1)

            def ffn_residual(b, c, bank):
                dve.wait_ge(ffn_mm, tiles(b, c))
                dve.wait_ge(ab_ok, tiles(b, c))
                if c >= 2:
                    dve.wait_ge(stored[c % 2], dmas(b, c - 2, 2, 16))
                V.scalar_tensor_tensor(obuf[:, c % 2, :], bank[:, :], ab[:, c % 2:c % 2 + 1], hbuf[:, c % TS, :], ALU.mult,
                                       ALU.add).then_inc(out_ok, 1)

            def ffn_weights():
                dve.wait_ge(wabs_mm, 1)
                V.tensor_scalar(alpha[:, :], dcs[:, 0:1], 1.0 / (D * D), Q_EPS, ALU.mult, ALU.max).then_inc(alpha_step, 1)
                dve.wait_ge(alpha_step, 1)
                V.reciprocal(ainv[:, :], alpha[:, :]).then_inc(alpha_step, 1)
                dve.wait_ge(alpha_step, 2)
                for k in range(KD):
                    v = stage(NW + k)
                    V.tensor_scalar(v, v, ainv[:, :], MAGIC, ALU.mult, ALU.add).then_inc(fq_step, 1)
                    dve.wait_ge(fq_step, 2 * k + 1)
                    V.tensor_scalar(v, v, MAGIC, 1.0, ALU.subtract, ALU.min).then_inc(fq_step, 1)

            def ternary(lo, hi):
                for k in range(lo, hi):
                    dve.wait_ge(fq_tr, k + 1)
                    V.tensor_scalar(wffn[:, :, k * P:(k + 1) * P], k_t((tp[2], dcs)[k % 2]), -1.0, None,
                                    ALU.max).then_inc(fq_ok, 1)

            def wo_split():
                dve.wait_ge(wo_in, 16 * KD)
                for k in range(KD):
                    V.tensor_scalar(wo_stage[k], wo_stage[k], norma[:, k:k + 1], None, ALU.mult).then_inc(w_scaled, 1)
                for k in range(KD):
                    dve.wait_ge(wo_hi, k + 1)
                    V.scalar_tensor_tensor(wo[:, 1, k, :], wo_stage[k], SW, wo[:, 0, k, :], ALU.mult, ALU.subtract).then_inc(wo_lo, 1)

            def q_phase(b, c0, prev, nxt):
                if prev:
                    tok_out(b, c0 + 3)
                v_split(b, c0)
                if prev:
                    oT_split(b, c0 - 1)
                    tok_norm(b, c0 + 3)
                v_split(b, c0 + 1)
                if prev:
                    tok_xn(b, c0 + 3)
                    attn_residual(b, c0 - 1, dcs)
                xnT_split(b, c0 + 3)
                if not prev:
                    ffn_weights()
                v_split(b, c0 + 2)
                if prev:
                    ffn_residual(b, c0 - 2, dcs)
                    quantise(b, c0 - 1)
                v_split(b, c0 + 3)
                if not prev:
                    wo_split()
                log_decay_begin(b, c0)
                for j in range(2 * H):
                    silu(b, c0, j)
                    qk_split(b, c0, j)
                    if j == 1 and not prev:
                        ternary(0, 2)
                    if j == 3 and not prev:
                        ternary(2, KD)
                    if j == 2:
                        log_decay_end(b, c0)
                    if j == 4:
                        decay_sums(b, c0)
                    if j == 5 and nxt:
                        cat_split(b, c0 + TM, 0)
                    if j == 5 and prev:
                        ffn_residual(b, c0 - 1, dcs)
                if c0 == TS:
                    dve.wait_ge(stored[0], dmas(b, c0 - 2, 2, 16))
                    dve.wait_ge(stored[1], dmas(b, c0 - 1, 2, 16))

            def a_phase(b, c0, nxt):
                for t in range(TM):
                    c, n = c0 + t, c0 + t + TM
                    if nxt and t == 0:
                        cat_split(b, n, 1)
                    if nxt and t >= 1:
                        tok_out(b, n - 1)
                    dve.wait_ge(k_tr, tiles(b, c))
                    dve.wait_ge(ex_ok, macros(b, c))
                    V.scalar_tensor_tensor(kd32[:, :, :], k_t(tp[0]), SQ / (2 * SX * SW) ,
                                           ex[:, 2, t, :].unsqueeze(2).to_broadcast([P, H, P]), ALU.mult,
                                           ALU.mult).then_inc(kd32_ok, 1)
                    if t >= 1:
                        oT_split(b, c - 1, nxt)
                    if nxt and t >= 1:
                        cat_split(b, n, 1)
                    dve.wait_ge(sc_mm, tiles(b, c))
                    dve.wait_ge(dec_ok, tiles(b, c))
                    V.scalar_tensor_tensor(p32[:, :], sco[:, :], SP / SQ ** 2, dec[:, :, :].rearrange("p h i -> p (h i)"),
                                           ALU.mult, ALU.mult).then_inc(p32_ok, 1)
                    if nxt and t >= 1:
                        tok_norm(b, n - 1)
                        tok_xn(b, n - 1)
                    if t >= 1:
                        attn_residual(b, c - 1, mmb)
                    if nxt:
                        cat_split(b, n, 2)
                    dve.wait_ge(att_mm, tiles(b, c))
                    st_v = st32[:, :, :].rearrange("p h f -> p (h f)")
                    if c % TS == 0:
                        V.tensor_scalar(st_v, dcs[:, :], SP / SQ ** 2, None, ALU.mult).then_inc(st32_ok, 1)
                        V.tensor_copy(o32[:, :], sco[:, :]).then_inc(o32_ok, 1)
                    else:
                        if c % TS != TS - 1:
                            dve.wait_ge(stdec_ok, (TS - 2) * b + c)
                            V.scalar_tensor_tensor(st_v, dcs[:, :], SP / SQ ** 2, stdec[:, :, :].rearrange("p h f -> p (h f)"),
                                                   ALU.mult, ALU.add).then_inc(st32_ok, 1)
                        dve.wait_ge(ointer_ok, states(b, c))
                        V.tensor_tensor(o32[:, :], sco[:, :], ointer[:, :, :].rearrange("p h f -> p (h f)"),
                                        ALU.add).then_inc(o32_ok, 1)
                    if t >= 2:
                        ffn_residual(b, c - 2, ffn_bank(nxt))
                    if t >= 1:
                        quantise(b, c - 1)
                    if nxt and t >= 1:
                        xnT_split(b, n - 1)
                    if nxt and t <= 2:
                        cat_split(b, n + 1, 0)

            made = [0]

            def step(ins):
                made[0] += 1
                ins.then_inc(hash_step, 1)
                dve.wait_ge(hash_step, made[0])

            def mod_ngv(r, v, q):
                step(V.tensor_scalar(q, v, 1.0 / NGV, MAGIC, ALU.mult, ALU.add))
                step(V.tensor_scalar(q, q, MAGIC, -float(NGV), ALU.subtract, ALU.mult))
                step(V.tensor_tensor(r, q, v, ALU.add))
                step(V.tensor_scalar(q, r, 0.0, float(NGV), ALU.is_lt, ALU.mult))
                step(V.tensor_tensor(r, r, q, ALU.add))

            W2 = P + 2
            dve.wait_ge(x_in, 16 * (NB + 1))
            step(V.tensor_copy(xf[:, :], xi[:, :]))
            step(V.tensor_scalar(feat[:, 0, :], xf[:, 2:], float(VOCAB - 1), 0.0, ALU.min, ALU.max))
            mod_ngv(hw[:, 0, :], xf[:, :], hw[:, 1, :])
            dve.wait_ge(feat_tr, 1)
            V.tensor_copy(idx[:, :, 0], sco[:, 0:NT]).then_inc(idx_ok, 1)
            step(V.scalar_tensor_tensor(hw[:, 2, 1:W2], hw[:, 0, 0:W2 - 1], 131.0, xf[:, 1:W2], ALU.mult, ALU.add))
            mod_ngv(hw[:, 3, 1:W2], hw[:, 2, 1:W2], hw[:, 1, 1:W2])
            step(V.tensor_copy(feat[:, 1, :], hw[:, 3, 2:W2]))
            step(V.scalar_tensor_tensor(hw[:, 2, 2:W2], hw[:, 3, 1:W2 - 1], 131.0, xf[:, 2:W2], ALU.mult, ALU.add))
            mod_ngv(feat[:, 2, :], hw[:, 2, 2:W2], hw[:, 1, 2:W2])
            assert made[0] == HASH_STEPS
            dve.wait_ge(feat_tr, 2)
            V.tensor_copy(idx[:, :, 1:NG].rearrange("p n g -> p g n"),
                          dcs[:, NT:NG * NT].rearrange("p (g n) -> p g n", g=NG - 1)).then_inc(idx_ok, 1)

            w_split(0, KD)
            cat_split(0, 0, 0)
            w_split(KD, 2 * KD)
            cat_split(0, 0, 1)
            w_split(2 * KD, 3 * KD)
            cat_split(0, 0, 2)
            cat_split(0, 1, 0)
            dve.wait_ge(small_in, 64)
            dve.wait_ge(wf_hi, 1)
            V.scalar_tensor_tensor(wf[:, :, :, 1], wf32[:, :, :], SW, wf[:, :, :, 0], ALU.mult, ALU.subtract).then_inc(wf_lo, 1)
            for c in range(1, TM):
                tok_out(0, c - 1)
                cat_split(0, c, 1)
                tok_norm(0, c - 1)
                cat_split(0, c, 2)
                tok_xn(0, c - 1)
                w_split(CUTS[c - 1], CUTS[c])
                xnT_split(0, c - 1)
                if c < TM - 1:
                    cat_split(0, c + 1, 0)
            for k in range(KD):
                dve.wait_ge(w_in[k], 16 * (NW // NSTG + 1))
            V.tensor_reduce(wabs[:, :], k32[:, :, :].rearrange("p k d -> p (k d)"), AX.X, ALU.add,
                            apply_absolute_value=True).then_inc(wabs_ok, 1)
            tok_out(0, TM - 1)
            tok_norm(0, TM - 1)
            tok_xn(0, TM - 1)
            q_phase(0, 0, False, True)
            with dve.Fori(0, NB - 1) as b:
                a_phase(b, 0, True)
                q_phase(b, TM, True, True)
                a_phase(b, TM, True)
                q_phase(b, 2 * TM, True, True)
            b = NB - 1
            a_phase(b, 0, True)
            q_phase(b, TM, True, False)
            a_phase(b, TM, False)
            oT_split(b, TS - 1, False)
            attn_residual(b, TS - 1, mmb)
            ffn_residual(b, TS - 2, mma)
            quantise(b, TS - 1)
            ffn_residual(b, TS - 1, sco)


_INS = ["x", "L0_tok_unigram_table", "L0_tok_ngram_table", "L0_tok_W", "L0_tok_b", "L0_tok_norm_w", "L0_attn_Wq",
        "L0_attn_Wk", "L0_attn_Wv", "L0_attn_Wf", "L0_attn_Wo", "L0_attn_norm_w", "L0_ffn_weight"]


def kernel(**inputs):
    import numpy as _np
    import concourse.bacc as _bacc
    from concourse import mybir as _mybir
    from concourse.bass_utils import run_bass_kernel_spmd as _run

    nc = _bacc.Bacc("TRN2", target_bir_lowering=False, num_devices=1)
    arrays, args = {}, []
    for name in _INS:
        a = _np.ascontiguousarray(inputs[name])
        arrays[f"in_{name}_dram"] = a
        args.append(nc.dram_tensor(f"in_{name}_dram", a.shape, _mybir.dt.from_np(a.dtype), kind="ExternalInput").ap())
    shape = (*inputs["x"].shape, inputs["L0_ffn_weight"].shape[0])
    args.append(nc.dram_tensor("out_0_dram", shape, _mybir.dt.float32, kind="ExternalOutput").ap())
    lm_tower_kernel(nc, *args)
    r = _run(nc, [arrays], core_ids=[0])
    return r.results[0]["out_0_dram"]
```

```python
import concourse.bass as bass
from concourse import mybir
from contextlib import ExitStack


def lm_tower_kernel(nc, x, uni_table, ngram_table, W_tok, b_tok, norm_tok, Wq, Wk, Wv, Wf, Wo, norm_attn, W_ffn, out):
    f32, f16, bf16, i32 = mybir.dt.float32, mybir.dt.float16, mybir.dt.bfloat16, mybir.dt.int32
    ACT, ALU, AX = mybir.ActivationFunctionType, mybir.AluOpType, mybir.AxisListType

    NB, NS = x.shape
    P = 128
    D = W_ffn.shape[0]
    H = Wf.shape[1]
    KD = D // P
    NG = W_tok.shape[0] // D
    NT = NB * NS // P
    TS = NS // P
    TM = 4
    MT = TM * P
    assert TS == 2 * TM and D == H * P and MT == 512
    VOCAB, NGV = uni_table.shape[0], ngram_table.shape[0]
    HASH_STEPS = 20
    MAGIC = 1.5 * 2.0 ** 23
    RMS_EPS, LN_EPS, Q_EPS = 1e-6, 1e-5, 1e-8
    SW = 2.0 ** 10
    SX = 2.0 ** 8
    SQ = 2.0 ** 10
    SP = 2.0 ** 6
    SO = SP * SQ

    out_t = out.rearrange("b (t p) d -> (b t) p d", p=P)

    ctx = ExitStack()
    with ctx:
        def sb(name, shape, dt=f32):
            return ctx.enter_context(nc.sbuf_tensor(name, shape, dt))

        def pb(name):
            return ctx.enter_context(nc.psum_tensor(name, [P, 512], f32))

        def sem(name):
            return ctx.enter_context(nc.semaphore(name))

        wt = sb("wt", [P, 2, NG * KD, D], f16)
        wq = sb("wq", [P, 2, KD, D], f16)
        wk = sb("wk", [P, 2, KD, D], f16)
        wv = sb("wv", [P, 2, KD, D], f16)
        wo = sb("wo", [P, 2, KD, D], f16)
        wf = sb("wf", [P, KD, H, 2], f16)
        wf32 = sb("wf32", [P, KD, H])
        wffn = sb("wffn", [P, KD, D], bf16)
        bias_b = sb("bias_b", [P, D])
        normt_b = sb("normt_b", [P, D])
        norma = sb("norma", [P, KD])
        ident = sb("ident", [P, P])
        before = sb("before", [P, P], f16)
        upto = sb("upto", [P, P], f16)
        ones16 = sb("ones16", [P, P], f16)
        ones32 = sb("ones32", [P, P])
        neghalf = sb("neghalf", [P, 1])
        one_c = sb("one_c", [P, 1])
        xi = sb("xi", [NT, P + 2], i32)
        idx = sb("idx", [P, NT, NG], i32)
        idx_now = sb("idx_now", [P, 2, TM, NG], i32)
        cat = sb("cat", [P, 2, NG * D])
        cs = sb("cs", [P, NG, 2, D], f16)
        catT = sb("catT", [P, NG, 2, KD, P], f16)
        hbuf = sb("hbuf", [P, TS, D])
        junk = sb("junk", [P, D], bf16)
        xn = sb("xn", [P, D])
        xns = sb("xns", [P, 2, D], f16)
        xnT = sb("xnT", [P, 2, KD, MT], f16)
        ms = sb("ms", [P, 2]); rms_u = sb("rms_u", [P, 2]); rms_r = sb("rms_r", [P, 2])
        bst = sb("bst", [P, 2, 6]); mv = sb("mv", [P, 2, 2]); ln_u = sb("ln_u", [P, 2]); ln_r = sb("ln_r", [P, 2])
        vs = sb("vs", [P, 2, TM, D], f16)
        qT = sb("qT", [P, 2, H, MT], f16)
        kT = sb("kT", [P, 2, H, MT], f16)
        qk32 = sb("qk32", [P, 2, MT])
        ktok = sb("ktok", [P, 2, TM, H, P], f16)
        th = sb("th", [P, 2, MT])
        th_flat, qk32_flat = th[:, :, :].rearrange("p a t -> p (a t)"), qk32[:, :, :].rearrange("p a t -> p (a t)")
        hw = th_flat[0:NT, 0:4 * (P + 2)].rearrange("p (a t) -> p a t", a=4)
        xf = qk32_flat[0:NT, 0:P + 2]
        feat = qk32_flat[0:NT, 512:512 + NG * P].rearrange("p (a t) -> p a t", a=NG)
        z = sb("z", [P, TM * H]); za = sb("za", [P, TM * H]); ze = sb("ze", [P, TM * H]); zl = sb("zl", [P, TM * H])
        zm = sb("zm", [P, TM * H]); ld = sb("ld", [P, TM * H])
        ldp = sb("ldp", [P, TM, H, 2], f16)
        ct = sb("ct", [P, 3, TM, H])
        ex = sb("ex", [P, 3, TM, H])
        lda = sb("lda", [P, TM, 2 * H, P], f16)
        dec = sb("dec", [P, H, P])
        p32 = sb("p32", [P, H * P])
        pT = sb("pT", [P, 2, H * P], f16)
        ksum = sb("ksum", [P, H, P])
        kd32 = sb("kd32", [P, H, P])
        kd = sb("kd", [P, 2, H * P], f16)
        st32 = sb("st32", [P, H, P])
        stdec = sb("stdec", [P, H, P])
        st = sb("st", [P, 2, H * P], f16)
        ointer = sb("ointer", [P, H, P])
        o32 = sb("o32", [P, D])
        on = sb("on", [P, D])
        oms = sb("oms", [P, 2]); o_u = sb("o_u", [P, 2]); o_r = sb("o_r", [P, 2])
        oT = sb("oT", [P, 2, KD, P], f16)
        bst2 = sb("bst2", [P, 2, 6]); mv2 = sb("mv2", [P, 2, 2]); ln2_u = sb("ln2_u", [P, 2]); ln2_r = sb("ln2_r", [P, 2])
        xn2 = sb("xn2", [P, D])
        yq = sb("yq", [P, D], bf16)
        amax = sb("amax", [P, 2]); beta = sb("beta", [P, 2]); binv = sb("binv", [P, 2]); ab = sb("ab", [P, 2])
        xqT = sb("xqT", [P, KD, P], bf16)
        obuf = sb("obuf", [P, 2, D])
        wabs = sb("wabs", [P, 1]); alpha = sb("alpha", [P, 1]); ainv = sb("ainv", [P, 1])

        on_ps = pb("on_ps")
        fq_ps = pb("fq_ps")
        mma, mmb = pb("mma"), pb("mmb")
        sco = pb("sco")
        dcs = pb("dcs")
        oxb = pb("oxb")
        f_ps = oxb[:, 0:32].rearrange("p (s g) -> p s g", s=TM)
        ct_ps = oxb[:, 32:96]

        x_zero, x_in, small_in, const_set, const_ok, hash_step, feat_tr = map(sem, "x_zero x_in small_in const_set const_ok hash_step feat_tr".split())
        idx_ok, idx_copied, pool_gate, dve_gate, w_hi, w_lo, w_scaled = map(sem, "idx_ok idx_copied pool_gate dve_gate w_hi w_lo w_scaled".split())
        wf_hi, wf_lo, wabs_ok, wabs_mm, alpha_step, fq_step, fq_tr = map(sem, "wf_hi wf_lo wabs_ok wabs_mm alpha_step fq_step fq_tr".split())
        fq_ok, sp_gate, h0_ok, ms_ok, rms_u_ok, rms_ok, h_ok = map(sem, "fq_ok sp_gate h0_ok ms_ok rms_u_ok rms_ok h_ok".split())
        bst_ok, mv_ok, ln_u_ok, ln_ok, xn_ok, xnT_ok, xns_hi = map(sem, "bst_ok mv_ok ln_u_ok ln_ok xn_ok xnT_ok xns_hi".split())
        xns_lo, v_mm, v_hi, v_lo, qk_mm, th_ok, qk32_ok = map(sem, "xns_lo v_mm v_hi v_lo qk_mm th_ok qk32_ok".split())
        qk_hi, qk_lo, z_ok, za_ok, ze_ok, zl_ok, zm_ok = map(sem, "qk_hi qk_lo z_ok za_ok ze_ok zl_ok zm_ok".split())
        ld_ok, ldp_hi, ldp_ok, cum_mm, ct_sums, ct_ok, ex_ok = map(sem, "ld_ok ldp_hi ldp_ok cum_mm ct_sums ct_ok ex_ok".split())
        lda_ok, sc_mm, dc_mm, ktok_ok, dec_exp, dec_ok, p32_ok = map(sem, "lda_ok sc_mm dc_mm ktok_ok dec_exp dec_ok p32_ok".split())
        p_hi, p_lo, k_sum, kd32_ok, kd_hi, kd_lo, stdec_ok, st32_ok = map(sem, "p_hi p_lo k_sum kd32_ok kd_hi kd_lo stdec_ok st32_ok".split())
        st_hi, st_lo, att_mm, ointer_ok, o32_ok, oms_ok, o_u_ok = map(sem, "st_hi st_lo att_mm ointer_ok o32_ok oms_ok o_u_ok".split())
        o_r_ok, on_ok, on_tr, oT_hi, oT_lo, wo_mm, h2_ok = map(sem, "o_r_ok on_ok on_tr oT_hi oT_lo wo_mm h2_ok".split())
        bst2_ok, mv2_ok, ln2_u_ok, ln2_ok, xn2_ok, amax_ok, beta_ok = map(sem, "bst2_ok mv2_ok ln2_u_ok ln2_ok xn2_ok amax_ok beta_ok".split())
        binv_ok, ab_ok, yq_ok, xqT_ok, ffn_mm, out_ok = map(sem, "binv_ok ab_ok yq_ok xqT_ok ffn_mm out_ok".split())
        w_in = [sem(f"w_in{r}") for r in range(2 * H)]
        cat_in = [sem(f"cat_in{r}") for r in range(2)]
        cat_hi = [sem(f"cat_hi{g}") for g in range(NG)]
        cat_lo = [sem(f"cat_lo{g}") for g in range(NG)]
        catT_ok = [sem(f"catT_ok{g}") for g in range(NG)]
        tok_mm = [sem(f"tok_mm{g}") for g in range(NG)]
        first_copied = sem("first_copied")
        round_ok, wo_in, wo_hi, wo_lo = map(sem, "round_ok wo_in wo_hi wo_lo".split())
        stored = [sem(f"stored{r}") for r in range(2)]

        def tiles(b, c):
            return TS * b + c + 1

        def macros(b, c):
            return 2 * b + c // TM + 1

        def blocks(b, c, j):
            return 4 * H * b + 2 * H * (c // TM) + j + 1

        def states(b, c):
            return (TS - 1) * b + c - c // TS

        def dmas(b, c, ring, each):
            return each * ((TS // ring) * b + c // ring + 1)

        NSTG = 2 * H
        vs32 = vs[:, :, :, :].rearrange("p a t d -> p (a t d)").bitcast(f32).rearrange("p (t d) -> p t d", t=H)

        ktok32 = ktok[:, :, :, :, :].rearrange("p a t h e -> p (a t h e)").bitcast(f32).rearrange("p (t d) -> p t d", t=H)

        def stage(w):
            return (ktok32 if w % NSTG < H else vs32)[:, w % H, :]

        wo_stage = [t[:, :, :].rearrange("p h e -> p (h e)") for t in (kd32, st32, stdec, ointer)]

        WEIGHTS = [(W_tok, wt, k) for k in range(NG * KD)]
        WEIGHTS += [(src, dst, k) for src, dst in ((Wv, wv), (Wq, wq), (Wk, wk)) for k in range(KD)]
        NW = len(WEIGHTS)
        assert NW % NSTG == 0
        CUTS = [NG * KD, NG * KD + 4, NG * KD + 8, NW]

        def ffn_bank(nxt):
            return mmb if nxt else mma

        def qk_bank(j):
            return (mma, mmb, sco)[j % 3]

        def v_bank(c):
            return (sco, mmb, mma, mmb)[c % TM]

        def split3(mm, act_hi, act_lo, w_hi_, w_lo_, first, last):
            nc.tensor.matmul(mm, act_hi, w_hi_, start=first, stop=False)
            nc.tensor.matmul(mm, act_hi, w_lo_, start=False, stop=False)
            return nc.tensor.matmul(mm, act_lo, w_hi_, start=False, stop=last)

        block = ctx.enter_context(nc.Block())

        @block.sync
        def _(sp):
            sp.wait_ge(x_zero, 1)
            sp.dma_start(xi[:, 2:], x.rearrange("b (t p) -> (b t) p", p=P)).then_inc(x_in, 16)
            for q in range(0, NB, 2):
                sp.dma_start(xi[q * TS + 1:(q + 1) * TS, 0:2],
                             x[q, :].rearrange("(t p) -> t p", p=P)[0:TS - 1, P - 2:P]).then_inc(x_in, 16)
            sp.dma_start(bias_b[:, :], b_tok.partition_broadcast(P)).then_inc(small_in, 16)
            sp.dma_start(normt_b[:, :], norm_tok.partition_broadcast(P)).then_inc(small_in, 16)
            sp.dma_start(wf32[:, :, :], Wf.rearrange("(k p) h -> p k h", p=P)).then_inc(small_in, 16)
            with nc.allow_non_contiguous_dma(reason="512 numbers, once"):
                sp.dma_start(norma[:, :], norm_attn.rearrange("(k p) -> p k", p=P)).then_inc(small_in, 16)

            def load_weights(lo, hi):
                for w in range(lo, hi):
                    if w >= NSTG:
                        sp.wait_ge(w_hi, w - NSTG + 1)
                        sp.wait_ge(w_lo, w - NSTG + 1)
                    src, k = (WEIGHTS[w][0], WEIGHTS[w][2]) if w < NW else (W_ffn, w - NW)
                    sp.dma_start(stage(w), src[k * P:(k + 1) * P, :]).then_inc(w_in[w % NSTG], 16)

            def gate():
                sp.sem_inc(sp_gate, 1)

            def cat_transpose(b, c, g):
                sp.wait_ge(cat_lo[g], tiles(b, c))
                gate()
                if not isinstance(b, int) or TS * b + c >= 1:
                    sp.wait_ge(tok_mm[g], tiles(b, c - 1))
                    gate()
                sp.dma_start_transpose(catT[:, g, :, :, :].rearrange("p a k t -> p (a k) t"),
                                       cs[:, g, :, :].rearrange("p a d -> p (a d)")).then_inc(catT_ok[g], 16)

            def xn_transpose(b, c):
                sp.wait_ge(xns_lo, tiles(b, c))
                gate()
                if not isinstance(b, int) or TS * b + c >= TM:
                    sp.wait_ge(qk_mm, macros(b, c - TM) * 2 * H)
                    gate()
                sp.dma_start_transpose(xnT[:, :, :, c % TM * P:(c % TM + 1) * P].rearrange("p a k t -> p (a k) t"),
                                       xns[:, :, :].rearrange("p a d -> p (a d)")).then_inc(xnT_ok, 16)

            def k_transpose(b, c0, h):
                sp.wait_ge(qk_lo, blocks(b, c0, h))
                gate()
                if not isinstance(b, int) or TS * b + c0 >= 1:
                    sp.wait_ge(kd32_ok, tiles(b, c0 - 1))
                    gate()
                elif h == 0:
                    sp.wait_ge(fq_tr, KD)
                for a in range(2):
                    sp.dma_start_transpose(ktok[:, a, :, h, :], kT[:, a, h, :]).then_inc(ktok_ok, 16)

            def yq_transpose(b, c):
                sp.wait_ge(yq_ok, tiles(b, c))
                gate()
                if not isinstance(b, int) or TS * b + c >= 1:
                    sp.wait_ge(ffn_mm, tiles(b, c - 1))
                    gate()
                sp.dma_start_transpose(xqT[:, :, :], yq[:, :]).then_inc(xqT_ok, 16)

            def store(b, c):
                sp.wait_ge(out_ok, tiles(b, c))
                sp.dma_start(out_t[bass.ds(TS * b + c, 1), :, :].rearrange("a p d -> (a p) d"),
                             obuf[:, c % 2, :]).then_inc(stored[c % 2], 16)

            def q_phase(b, c0, prev, nxt):
                xn_transpose(b, c0 + 3)
                if prev:
                    store(b, c0 - 2)
                    yq_transpose(b, c0 - 1)
                for h in range(H - 1):
                    k_transpose(b, c0, h)
                if nxt:
                    cat_transpose(b, c0 + TM, 0)
                k_transpose(b, c0, H - 1)
                if nxt:
                    cat_transpose(b, c0 + TM, 1)
                if prev:
                    store(b, c0 - 1)

            def a_phase(b, c0, nxt):
                for t in range(TM):
                    c, n = c0 + t, c0 + t + TM
                    if nxt and t >= 1:
                        cat_transpose(b, n, 1)
                    if nxt:
                        cat_transpose(b, n, 2)
                    if nxt and t < TM - 1:
                        cat_transpose(b, n + 1, 0)
                    if nxt and t >= 1:
                        xn_transpose(b, n - 1)
                    if t >= 1:
                        yq_transpose(b, c - 1)
                    if t >= 2:
                        store(b, c - 2)

            load_weights(0, NSTG + 2 * KD)
            cat_transpose(0, 0, 0)
            cat_transpose(0, 0, 1)
            load_weights(NSTG + 2 * KD, NSTG + 3 * KD)
            cat_transpose(0, 0, 2)
            cat_transpose(0, 1, 0)
            for c in range(1, TM):
                cat_transpose(0, c, 1)
                cat_transpose(0, c, 2)
                if c < TM - 1:
                    cat_transpose(0, c + 1, 0)
                if c <= 2:
                    load_weights(CUTS[c] + KD, CUTS[c] + 2 * KD)
                xn_transpose(0, c - 1)
            for k in range(KD):
                sp.dma_start(wo_stage[k], Wo[k * P:(k + 1) * P, :]).then_inc(wo_in, 16)
            q_phase(0, 0, False, True)
            with sp.Fori(0, NB - 1) as b:
                a_phase(b, 0, True)
                q_phase(b, TM, True, True)
                a_phase(b, TM, True)
                q_phase(b, 2 * TM, True, True)
            b = NB - 1
            a_phase(b, 0, True)
            q_phase(b, TM, True, False)
            a_phase(b, TM, False)
            store(b, TS - 2)
            yq_transpose(b, TS - 1)
            store(b, TS - 1)
            for r in range(2):
                sp.wait_ge(stored[r], 16 * NT // 2)

        @block.gpsimd
        def _(pool):
            def gate():
                pool.sem_inc(pool_gate, 1)

            pool.memset(xi[:, :], 0).then_inc(x_zero, 1)
            pool.memset(ident[:, :], 0.0).then_inc(const_set, 1)
            pool.memset(before[:, :], 1.0).then_inc(const_set, 1)
            pool.memset(upto[:, :], 1.0).then_inc(const_set, 1)
            pool.memset(ones16[:, :], 1.0).then_inc(const_set, 1)
            pool.memset(ones32[:, :], 1.0).then_inc(const_set, 1)
            pool.memset(neghalf[:, :], -0.5).then_inc(const_set, 1)
            pool.memset(one_c[:, :], 1.0).then_inc(const_set, 1)
            pool.wait_ge(const_set, 7)
            for m, op, mul, step in ((ident, ALU.not_equal, 1, -1), (before, ALU.is_gt, 1, -1), (upto, ALU.is_ge, -1, 1)):
                pool.affine_select(out=m[:, :], in_=m[:, :], compare_op=op, fill=1.0 if op == ALU.not_equal else 0.0, base=0,
                                   pattern=[[step, P]], channel_multiplier=mul).then_inc(const_ok, 1)

            def copy_indices(b, c):
                if not isinstance(b, int) or TS * b + c >= 2 * TM:
                    for r in range(2):
                        pool.wait_ge(cat_in[r], dmas(b, c + r - TM - 2, 2, 16 * NG))
                    gate()
                pool.tensor_copy(idx_now[:, c // TM % 2, :, :], idx[:, bass.ds(TS * b + c, TM), :]).then_inc(idx_copied, 1)
                pool.wait_ge(idx_copied, macros(b, c))
                gate()

            def gather_rows(c, g):
                pool.indirect_dma_start(
                    cat[:, c % 2, g * D:(g + 1) * D], None, (uni_table, ngram_table, ngram_table)[g],
                    bass.IndirectOffsetOnAxis(ap=idx_now[:, c // TM % 2, c % TM, g:g + 1], axis=0),
                ).then_inc(cat_in[c % 2], 16)

            def gather(b, c, lo=0, hi=NG):
                pool.wait_ge(cat_lo[NG - 1], tiles(b, c - 2))
                gate()
                for g in range(lo, hi):
                    gather_rows(c, g)

            def inv_sqrt(b, c, given, given_ok, u, u_ok, r, r_ok, op0, by0, op1, by1):
                pool.wait_ge(given_ok, tiles(b, c))
                gate()
                pool.tensor_scalar(u, given, by0, by1, op0, op1).then_inc(u_ok, 1)
                pool.wait_ge(u_ok, tiles(b, c))
                pool.tensor_tensor(r, u, neghalf[:, :], ALU.pow).then_inc(r_ok, 1)

            def rms(b, c):
                i = slice(c % 2, c % 2 + 1)
                inv_sqrt(b, c, ms[:, i], ms_ok, rms_u[:, i], rms_u_ok, rms_r[:, i], rms_ok, ALU.mult, 1.0 / D, ALU.add, RMS_EPS)

            def layer(b, c):
                i = slice(c % 2, c % 2 + 1)
                inv_sqrt(b, c, mv[:, c % 2, 1:2], mv_ok, ln_u[:, i], ln_u_ok, ln_r[:, i], ln_ok,
                         ALU.add, LN_EPS, ALU.mult, SX ** -2)

            def layer2(b, c):
                i = slice(c % 2, c % 2 + 1)
                inv_sqrt(b, c, mv2[:, c % 2, 1:2], mv2_ok, ln2_u[:, i], ln2_u_ok, ln2_r[:, i], ln2_ok,
                         ALU.add, LN_EPS, ALU.mult, 1.0)

            def attn_rms(b, c):
                i = slice(c % 2, c % 2 + 1)
                up = (SO / SX) ** 2
                inv_sqrt(b, c, oms[:, i], oms_ok, o_u[:, i], o_u_ok, o_r[:, i], o_r_ok, ALU.mult, up / D, ALU.add, up * RMS_EPS)

            def q_phase(b, c0, prev):
                if prev:
                    rms(b, c0 + 3)
                    layer(b, c0 + 3)
                    layer2(b, c0 - 1)
                pool.wait_ge(ldp_ok, macros(b, c0))
                for t in range(TM):
                    pool.tensor_tensor(
                        lda[:, t, :, :], before[:, :].unsqueeze(1).to_broadcast([P, 2 * H, P]),
                        ldp[:, t, :, :].rearrange("p h g -> p (h g)").unsqueeze(2).to_broadcast([P, 2 * H, P]),
                        ALU.mult).then_inc(lda_ok, 1)

            def a_phase(b, c0, nxt, more):
                if more:
                    copy_indices(b, c0 + 8)
                for t in range(TM):
                    c, n = c0 + t, c0 + t + TM
                    pool.wait_ge(dec_exp, tiles(b, c))
                    gate()
                    pool.affine_select(out=dec[:, :, :], in_=dec[:, :, :], compare_op=ALU.is_ge, fill=0.0, base=0,
                                       pattern=[[0, H], [1, P]], channel_multiplier=-1).then_inc(dec_ok, 1)
                    if nxt and t >= 1:
                        rms(b, n - 1)
                    if c % TS != TS - 1:
                        pool.wait_ge(kd_hi, states(b, c + 1))
                        pool.tensor_tensor(kd[:, 1, :], kd32[:, :, :].rearrange("p h e -> p (h e)"), kd[:, 0, :],
                                           ALU.subtract).then_inc(kd_lo, 1)
                    pool.wait_ge(p_hi, tiles(b, c))
                    pool.tensor_tensor(pT[:, 1, :], p32[:, :], pT[:, 0, :], ALU.subtract).then_inc(p_lo, 1)
                    if more or nxt and t < 2:
                        gather(b, c + 6, 0, 1)
                    if nxt and t >= 1:
                        layer(b, n - 1)
                    if 0 < c % TS < TS - 1:
                        pool.wait_ge(st32_ok, states(b, c))
                        pool.tensor_tensor(stdec[:, :, :], st32[:, :, :], ex[:, 1, t, :].unsqueeze(2).to_broadcast([P, H, P]),
                                           ALU.mult).then_inc(stdec_ok, 1)
                    if t >= 1:
                        layer2(b, c - 1)
                    if more or nxt and t < 2:
                        gather(b, c + 6, 1, NG)
                    attn_rms(b, c)
                    if c % TS != TS - 1:
                        pool.wait_ge(st_hi, states(b, c + 1))
                        pool.tensor_tensor(st[:, 1, :], st32[:, :, :].rearrange("p h f -> p (h f)"), st[:, 0, :],
                                           ALU.subtract).then_inc(st_lo, 1)

            pool.wait_ge(idx_ok, 1)
            pool.tensor_copy(idx_now[:, 0, :, 0:1], idx[:, 0:TM, 0:1]).then_inc(first_copied, 1)
            pool.wait_ge(first_copied, 1)
            for c in range(2):
                gather_rows(c, 0)
            pool.wait_ge(idx_ok, 2)
            pool.tensor_copy(idx_now[:, 0, :, 1:NG], idx[:, 0:TM, 1:NG]).then_inc(idx_copied, 1)
            pool.wait_ge(idx_copied, 1)
            for c in range(2):
                for g in range(1, NG):
                    gather_rows(c, g)
            copy_indices(0, TM)
            for c in range(TM):
                gather(0, c + 2)
                rms(0, c)
                layer(0, c)
            q_phase(0, 0, False)
            with pool.Fori(0, NB - 1) as b:
                a_phase(b, 0, True, True)
                q_phase(b, TM, True)
                a_phase(b, TM, True, True)
                q_phase(b, 2 * TM, True)
            a_phase(NB - 1, 0, True, False)
            q_phase(NB - 1, TM, True)
            a_phase(NB - 1, TM, False, False)
            layer2(NB - 1, TS - 1)

        @block.tensor
        def _(pe):
            def tok_matmul(b, c, g):
                pe.wait_ge(catT_ok[g], 16 * tiles(b, c))
                for j in range(KD):
                    k = g * KD + j
                    last = split3(mma[:, :], catT[:, g, 0, j, :], catT[:, g, 1, j, :], wt[:, 0, k, :], wt[:, 1, k, :],
                                  k == 0, k == NG * KD - 1)
                last.then_inc(tok_mm[g], 1)

            def on_transpose(b, c):
                pe.wait_ge(on_ok, tiles(b, c))
                for j in range(KD):
                    last = nc.tensor.transpose(on_ps[:, j * P:(j + 1) * P], on[:, j * P:(j + 1) * P], ident[:, :])
                last.then_inc(on_tr, 1)

            def out_proj(b, c, bank):
                pe.wait_ge(oT_hi, tiles(b, c))
                pe.wait_ge(oT_lo, tiles(b, c))
                for k in range(KD):
                    last = split3(bank[:, :], oT[:, 0, k, :], oT[:, 1, k, :], wo[:, 0, k, :], wo[:, 1, k, :], k == 0, k == KD - 1)
                last.then_inc(wo_mm, 1)

            def ffn(b, c, bank):
                pe.wait_ge(xqT_ok, 16 * tiles(b, c))
                for k in range(KD):
                    last = nc.tensor.matmul(bank[:, :], xqT[:, k, :], wffn[:, k, :], start=k == 0, stop=k == KD - 1)
                last.then_inc(ffn_mm, 1)

            def v_proj(b, c):
                t = c % TM
                tok = slice(t * P, (t + 1) * P)
                bank = v_bank(c)
                pe.wait_ge(xnT_ok, 16 * tiles(b, c))
                for k in range(KD):
                    hi, lo = xnT[:, 0, k, tok], xnT[:, 1, k, tok]
                    wf_k = wf[:, k, :, :].rearrange("p h g -> p (h g)")
                    nc.tensor.matmul(f_ps[:, t, :], hi, wf_k, start=k == 0, stop=False)
                    nc.tensor.matmul(f_ps[:, t, :], lo, wf_k, start=False, stop=k == KD - 1)
                    last = split3(bank[:, :], hi, lo, wv[:, 0, k, :], wv[:, 1, k, :], k == 0, k == KD - 1)
                last.then_inc(v_mm, 1)

            def qk_proj(b, c0, j):
                bank, w, h = qk_bank(j), (wk, wq)[j // H], j % H
                if j < 2:
                    pe.wait_ge(v_hi, tiles(b, c0 + 2 + j))
                    pe.wait_ge(v_lo, tiles(b, c0 + 2 + j))
                elif j >= 3:
                    pe.wait_ge(th_ok, blocks(b, c0, j - 3))
                    pe.wait_ge(qk32_ok, blocks(b, c0, j - 3))
                for k in range(KD):
                    last = split3(bank[:, :], w[:, 0, k, h * P:(h + 1) * P], w[:, 1, k, h * P:(h + 1) * P],
                                  xnT[:, 0, k, :], xnT[:, 1, k, :], k == 0, k == KD - 1)
                last.then_inc(qk_mm, 1)

            def sums(b, c0):
                pe.wait_ge(ldp_ok, macros(b, c0))
                parts = ldp[:, :, :, :].rearrange("p t h g -> p (t h g)")
                nc.tensor.matmul(ct_ps[:, 0:32], upto[:, :], parts, start=True, stop=True)
                nc.tensor.matmul(ct_ps[:, 32:64], ones16[:, :], parts, start=True, stop=True).then_inc(cum_mm, 1)

            def fq_transposes(lo, hi):
                for k in range(lo, hi):
                    pe.wait_ge(fq_step, 2 * (k + 1))
                    if k >= 2:
                        pe.wait_ge(fq_ok, k - 1)
                    for j in range(KD):
                        last = nc.tensor.transpose((fq_ps, dcs)[k % 2][:, j * P:(j + 1) * P],
                                                   stage(NW + k)[:, j * P:(j + 1) * P], ident[:, :])
                    last.then_inc(fq_tr, 1)

            def q_phase(b, c0, prev, nxt):
                p2, p3 = c0 - 2, c0 - 1
                if prev:
                    pe.wait_ge(ointer_ok, states(b, p3))
                    pe.wait_ge(o32_ok, tiles(b, p3))
                v_proj(b, c0)
                if prev:
                    on_transpose(b, p3)
                    pe.wait_ge(out_ok, tiles(b, c0 - 3))
                v_proj(b, c0 + 1)
                if prev:
                    if p3 % TS != TS - 1:
                        pe.wait_ge(st32_ok, states(b, c0))
                    else:
                        pe.wait_ge(dec_exp, tiles(b, p3))
                    out_proj(b, p3, dcs)
                pe.wait_ge(h0_ok, tiles(b, c0 + 3))
                v_proj(b, c0 + 2)
                if prev:
                    pe.wait_ge(h2_ok, tiles(b, p3))
                    ffn(b, p2, dcs)
                pe.wait_ge(v_hi, tiles(b, c0 + 1))
                pe.wait_ge(v_lo, tiles(b, c0 + 1))
                v_proj(b, c0 + 3)
                qk_proj(b, c0, 0)
                qk_proj(b, c0, 1)
                if not prev:
                    fq_transposes(0, 2)
                qk_proj(b, c0, 2)
                qk_proj(b, c0, 3)
                if not prev:
                    fq_transposes(2, KD)
                qk_proj(b, c0, 4)
                qk_proj(b, c0, 5)
                sums(b, c0)
                if prev:
                    pe.wait_ge(out_ok, tiles(b, p2))
                    ffn(b, p3, dcs)
                qk_proj(b, c0, 6)
                qk_proj(b, c0, 7)
                pe.wait_ge(th_ok, blocks(b, c0, 5))
                pe.wait_ge(qk32_ok, blocks(b, c0, 5))
                if prev:
                    pe.wait_ge(out_ok, tiles(b, p3))

            def scores(b, c):
                tok = slice(c % TM * P, (c % TM + 1) * P)
                for h in range(H):
                    last = split3(sco[:, h * P:(h + 1) * P], kT[:, 0, h, tok], kT[:, 1, h, tok],
                                  qT[:, 0, h, tok], qT[:, 1, h, tok], True, True)
                last.then_inc(sc_mm, 1)

            def decays(b, c):
                for h in range(H):
                    for g in range(2):
                        last = nc.tensor.matmul(dcs[:, h * P:(h + 1) * P], lda[:, c % TM, 2 * h + g, :], upto[:, :],
                                                start=g == 0, stop=g == 1)
                last.then_inc(dc_mm, 1)

            def attend(b, c):
                t = c % TM
                tok = slice(t * P, (t + 1) * P)
                heads = [slice(h * P, (h + 1) * P) for h in range(H)]
                if t == 0:
                    pe.wait_ge(v_lo, tiles(b, c + 3))
                if c % TS != 0:
                    pe.wait_ge(st_hi, states(b, c))
                    pe.wait_ge(st_lo, states(b, c))
                    if t == 0:
                        pe.wait_ge(ct_sums, macros(b, c))
                    for h, hd in enumerate(heads):
                        split3(oxb[:, hd], qT[:, 0, h, tok], qT[:, 1, h, tok], st[:, 0, hd], st[:, 1, hd], True, True)
                if c % TS != TS - 1:
                    pe.wait_ge(kd_hi, states(b, c + 1))
                    pe.wait_ge(kd_lo, states(b, c + 1))
                    pe.wait_ge(dec_exp, tiles(b, c))
                    for hd in heads:
                        split3(dcs[:, hd], kd[:, 0, hd], kd[:, 1, hd], vs[:, 0, t, hd], vs[:, 1, t, hd], True, True)
                pe.wait_ge(p_hi, tiles(b, c))
                pe.wait_ge(p_lo, tiles(b, c))
                for hd in heads:
                    last = split3(sco[:, hd], pT[:, 0, hd], pT[:, 1, hd], vs[:, 0, t, hd], vs[:, 1, t, hd], True, True)
                last.then_inc(att_mm, 1)

            def tile_scores(b, c, nxt, first):
                pe.wait_ge(lda_ok, tiles(b, c))
                if not first:
                    pe.wait_ge(st32_ok, states(b, c))
                decays(b, c)
                if first:
                    if nxt:
                        pe.wait_ge(th_ok, blocks(b, c, 2 * H - 2))
                        pe.wait_ge(qk32_ok, blocks(b, c, 2 * H - 2))
                        tok_matmul(b, c + TM, 0)
                    pe.wait_ge(qk_hi, blocks(b, c, 2 * H - 1))
                    pe.wait_ge(qk_lo, blocks(b, c, 2 * H - 1))
                else:
                    pe.wait_ge(o32_ok, tiles(b, c - 1))
                scores(b, c)

            def a_phase(b, c0, nxt):
                c, n = c0, c0 + TM
                tile_scores(b, c, nxt, True)
                if nxt:
                    tok_matmul(b, n, 1)
                attend(b, c)
                if nxt:
                    tok_matmul(b, n, 2)
                for t in range(1, TM):
                    c, n = c0 + t, c0 + t + TM
                    tile_scores(b, c, nxt, False)
                    on_transpose(b, c - 1)
                    if nxt:
                        pe.wait_ge(h0_ok, tiles(b, n - 1))
                        tok_matmul(b, n, 0)
                    if t == 1:
                        pe.wait_ge(th_ok, blocks(b, c0, 2 * H - 1))
                        pe.wait_ge(qk32_ok, blocks(b, c0, 2 * H - 1))
                    elif t == 2 or not nxt:
                        pe.wait_ge(h2_ok, tiles(b, c - 2))
                    elif t == 3:
                        pe.wait_ge(out_ok, tiles(b, c - 3))
                    out_proj(b, c - 1, mmb)
                    attend(b, c)
                    if nxt and t == TM - 1:
                        tok_matmul(b, n, 1)
                        tok_matmul(b, n, 2)
                    if t >= 2:
                        if nxt:
                            pe.wait_ge(h2_ok, tiles(b, c - 1))
                        elif t == 2:
                            pe.wait_ge(th_ok, blocks(b, c0, 2 * H - 2))
                            pe.wait_ge(qk32_ok, blocks(b, c0, 2 * H - 2))
                        else:
                            pe.wait_ge(out_ok, tiles(b, c - 3))
                        ffn(b, c - 2, ffn_bank(nxt))
                    if nxt and t < TM - 1:
                        tok_matmul(b, n, 1)
                        tok_matmul(b, n, 2)

            pe.wait_ge(const_ok, 3)
            pe.wait_ge(hash_step, 2)
            nc.tensor.transpose(sco[:, 0:NT], feat[:, 0, :], ident[0:NT, 0:NT]).then_inc(feat_tr, 1)
            pe.wait_ge(hash_step, HASH_STEPS)
            for g in range(1, NG):
                last = nc.tensor.transpose(dcs[:, g * NT:(g + 1) * NT], feat[:, g, :], ident[0:NT, 0:NT])
            last.then_inc(feat_tr, 1)
            for c in range(TM):
                if c >= 1:
                    pe.wait_ge(h0_ok, c)
                else:
                    pe.wait_ge(w_lo, KD)
                tok_matmul(0, c, 0)
                if c == 0:
                    pe.wait_ge(w_lo, 2 * KD)
                tok_matmul(0, c, 1)
                if c == 0:
                    pe.wait_ge(w_lo, 3 * KD)
                tok_matmul(0, c, 2)
            pe.wait_ge(wabs_ok, 1)
            nc.tensor.matmul(dcs[:, 0:1], ones32[:, :], wabs[:, :], start=True, stop=True).then_inc(wabs_mm, 1)
            pe.wait_ge(w_hi, NW)
            pe.wait_ge(w_lo, NW)
            pe.wait_ge(wf_lo, 1)
            q_phase(0, 0, False, True)
            pe.wait_ge(fq_ok, KD)
            pe.wait_ge(wo_hi, KD)
            pe.wait_ge(wo_lo, KD)
            with pe.Fori(0, NB - 1) as b:
                a_phase(b, 0, True)
                q_phase(b, TM, True, True)
                a_phase(b, TM, True)
                q_phase(b, 2 * TM, True, True)
            b = NB - 1
            a_phase(b, 0, True)
            q_phase(b, TM, True, False)
            a_phase(b, TM, False)
            on_transpose(b, TS - 1)
            pe.wait_ge(h2_ok, tiles(b, TS - 2))
            out_proj(b, TS - 1, mmb)
            pe.wait_ge(out_ok, tiles(b, TS - 3))
            ffn(b, TS - 2, mma)
            ffn(b, TS - 1, sco)

        @block.scalar
        def _(act):
            copy = nc.scalar.activation

            def w_split(lo, hi):
                for w in range(lo, hi):
                    _, dst, k = WEIGHTS[w]
                    act.wait_ge(w_in[w % NSTG], 16 * (w // NSTG + 1))
                    copy(dst[:, 0, k, :], stage(w), ACT.Copy, scale=SW).then_inc(w_hi, 1)

            def cat_split(b, c, g):
                if g == 0:
                    act.wait_ge(cat_in[c % 2], dmas(b, c, 2, 16 * NG))
                if not isinstance(b, int) or TS * b + c >= 1:
                    act.wait_ge(catT_ok[g], 16 * tiles(b, c - 1))
                copy(cs[:, g, 0, :], cat[:, c % 2, g * D:(g + 1) * D], ACT.Copy, scale=SW).then_inc(cat_hi[g], 1)

            def mean_square(b, c):
                act.wait_ge(h0_ok, tiles(b, c))
                copy(junk[:, :], hbuf[:, c % TS, :], ACT.Square, accum_out=ms[:, c % 2:c % 2 + 1]).then_inc(ms_ok, 1)

            def xn_split(b, c):
                act.wait_ge(xn_ok, tiles(b, c))
                if not isinstance(b, int) or TS * b + c >= 1:
                    act.wait_ge(xnT_ok, 16 * tiles(b, c - 1))
                copy(xns[:, 0, :], xn[:, :], ACT.Copy).then_inc(xns_hi, 1)

            def oT_split(b, c):
                act.wait_ge(on_tr, tiles(b, c))
                copy(oT[:, 0, :, :], on_ps[:, :].rearrange("p (k t) -> p k t", k=KD), ACT.Copy).then_inc(oT_hi, 1)

            def v_split(b, c):
                t = c % TM
                act.wait_ge(v_mm, tiles(b, c))
                copy(vs[:, 0, t, :], v_bank(c)[:, :], ACT.Copy, scale=SQ / (SX * SW)).then_inc(v_hi, 1)

            def qk_tanh(b, c0, j):
                act.wait_ge(qk_mm, blocks(b, c0, j))
                if j >= 2:
                    act.wait_ge(qk32_ok, blocks(b, c0, j - 2))
                copy(th[:, j % 2, :], qk_bank(j)[:, :], ACT.Tanh, scale=0.5 / (SX * SW)).then_inc(th_ok, 1)

            def qk_split(b, c0, j):
                dst, src = (kT, qT)[j // H], qk32[:, j % 2, :]
                act.wait_ge(qk32_ok, blocks(b, c0, j))
                copy(dst[:, 0, j % H, :], src, ACT.Copy, scale=SQ / (2 * SX * SW)).then_inc(qk_hi, 1)

            def q_phase(b, c0, prev, nxt):
                v_split(b, c0)
                if prev:
                    oT_split(b, c0 - 1)
                xn_split(b, c0 + 3)
                v_split(b, c0 + 1)
                v_split(b, c0 + 2)
                v_split(b, c0 + 3)
                if not prev:
                    for k in range(KD):
                        act.wait_ge(w_scaled, k + 1)
                        copy(wo[:, 0, k, :], wo_stage[k], ACT.Copy, scale=SW).then_inc(wo_hi, 1)
                m = macros(b, c0)
                for j in range(2 * H):
                    qk_tanh(b, c0, j)
                    if nxt and j in (3, 4):
                        cat_split(b, c0 + TM, j - 3)
                    qk_split(b, c0, j)
                    if j == 1:
                        act.wait_ge(z_ok, m)
                        copy(za[:, :], z[:, :], ACT.Abs, scale=1.0 / (SX * SW)).then_inc(za_ok, 1)
                        act.wait_ge(za_ok, m)
                        copy(ze[:, :], za[:, :], ACT.Exp, scale=-1.0).then_inc(ze_ok, 1)
                        act.wait_ge(ze_ok, m)
                        copy(zl[:, :], ze[:, :], ACT.Ln, bias=one_c[:, :]).then_inc(zl_ok, 1)
                    if j == 6:
                        act.wait_ge(ct_ok, m)
                        copy(ex[:, :, :, :].rearrange("p a t h -> p (a t h)"), ct[:, :, :, :].rearrange("p a t h -> p (a t h)"),
                             ACT.Exp, scale=1.0 / SP).then_inc(ex_ok, 1)

            def a_phase(b, c0, nxt):
                for t in range(TM):
                    c, n = c0 + t, c0 + t + TM
                    act.wait_ge(dc_mm, tiles(b, c))
                    copy(dec[:, :, :].rearrange("p h i -> p (h i)"), dcs[:, :], ACT.Exp, scale=1.0 / SP).then_inc(dec_exp, 1)
                    if nxt and t >= 1:
                        mean_square(b, n - 1)
                    if t >= 1:
                        oT_split(b, c - 1)
                    if nxt:
                        cat_split(b, n, 1 if t >= 1 else 2)
                    if c % TS != TS - 1:
                        act.wait_ge(kd32_ok, tiles(b, c))
                        copy(kd[:, 0, :], kd32[:, :, :].rearrange("p h e -> p (h e)"), ACT.Copy).then_inc(kd_hi, 1)
                    act.wait_ge(p32_ok, tiles(b, c))
                    copy(pT[:, 0, :], p32[:, :], ACT.Copy).then_inc(p_hi, 1)
                    if nxt and t >= 1:
                        cat_split(b, n, 2)
                    if nxt and t < TM - 1:
                        cat_split(b, n + 1, 0)
                    act.wait_ge(att_mm, tiles(b, c))
                    if c % TS != 0:
                        for h in range(H):
                            last = copy(ointer[:, h, :], oxb[:, h * P:(h + 1) * P], ACT.Copy, scale=ex[:, 0, t, h:h + 1])
                        last.then_inc(ointer_ok, 1)
                    if nxt and t >= 1:
                        xn_split(b, n - 1)
                    if c % TS != TS - 1:
                        act.wait_ge(st32_ok, states(b, c + 1))
                        copy(st[:, 0, :], st32[:, :, :].rearrange("p h f -> p (h f)"), ACT.Copy).then_inc(st_hi, 1)
                    act.wait_ge(o32_ok, tiles(b, c))
                    copy(junk[:, :], o32[:, :], ACT.Square, scale=1.0 / SO, accum_out=oms[:, c % 2:c % 2 + 1]).then_inc(oms_ok, 1)
                    act.wait_ge(o_r_ok, tiles(b, c))
                    copy(on[:, :], o32[:, :], ACT.Copy, scale=o_r[:, c % 2:c % 2 + 1]).then_inc(on_ok, 1)
                    if nxt and t == TM - 1:
                        mean_square(b, n)

            act.wait_ge(x_zero, 1)
            for q in range(1, NB, 2):
                act.dma_start(xi[q * TS + 1:(q + 1) * TS, 0:2],
                              x[q, :].rearrange("(t p) -> t p", p=P)[0:TS - 1, P - 2:P]).then_inc(x_in, 16)
            w_split(0, 2 * KD)
            cat_split(0, 0, 0)
            cat_split(0, 0, 1)
            w_split(2 * KD, 3 * KD)
            cat_split(0, 0, 2)
            cat_split(0, 1, 0)
            act.wait_ge(small_in, 64)
            copy(wf[:, :, :, 0], wf32[:, :, :], ACT.Copy, scale=SW).then_inc(wf_hi, 1)
            for c in range(1, TM):
                cat_split(0, c, 1)
                mean_square(0, c - 1)
                cat_split(0, c, 2)
                if c < TM - 1:
                    cat_split(0, c + 1, 0)
                w_split(CUTS[c - 1], CUTS[c])
                xn_split(0, c - 1)
            mean_square(0, TM - 1)
            q_phase(0, 0, False, True)
            with act.Fori(0, NB - 1) as b:
                a_phase(b, 0, True)
                q_phase(b, TM, True, True)
                a_phase(b, TM, True)
                q_phase(b, 2 * TM, True, True)
            b = NB - 1
            a_phase(b, 0, True)
            q_phase(b, TM, True, False)
            a_phase(b, TM, False)
            oT_split(b, TS - 1)

        @block.vector
        def _(dve):
            V = nc.vector

            def k_t(bank):
                return bank[:, :].rearrange("p (k t) -> p k t", k=KD)

            def w_split(lo, hi):
                for w in range(lo, hi):
                    _, dst, k = WEIGHTS[w]
                    dve.wait_ge(w_in[w % NSTG], 16 * (w // NSTG + 1))
                    dve.wait_ge(w_hi, w + 1)
                    V.scalar_tensor_tensor(dst[:, 1, k, :], stage(w), SW, dst[:, 0, k, :], ALU.mult, ALU.subtract).then_inc(w_lo, 1)

            def cat_split(b, c, g):
                dve.wait_ge(cat_hi[g], tiles(b, c))
                V.scalar_tensor_tensor(cs[:, g, 1, :], cat[:, c % 2, g * D:(g + 1) * D], SW, cs[:, g, 0, :], ALU.mult,
                                       ALU.subtract).then_inc(cat_lo[g], 1)

            def tok_out(b, c):
                dve.wait_ge(tok_mm[NG - 1], tiles(b, c))
                V.scalar_tensor_tensor(hbuf[:, c % TS, :], mma[:, :], SW ** -2, bias_b[:, :], ALU.mult, ALU.add).then_inc(h0_ok, 1)

            def stats(b, c, given_ok, st6, st6_ok, out2, out2_ok):
                dve.wait_ge(given_ok, tiles(b, c))
                V.bn_stats(st6[:, c % 2, :], hbuf[:, c % TS, :]).then_inc(st6_ok, 1)
                dve.wait_ge(st6_ok, tiles(b, c))
                dve.sem_inc(dve_gate, 1)
                V.bn_aggr(out2[:, c % 2, :], st6[:, c % 2, :]).then_inc(out2_ok, 1)

            def tok_norm(b, c):
                dve.wait_ge(rms_ok, tiles(b, c))
                V.scalar_tensor_tensor(hbuf[:, c % TS, :], hbuf[:, c % TS, :], rms_r[:, c % 2:c % 2 + 1], normt_b[:, :],
                                       ALU.mult, ALU.mult).then_inc(h_ok, 1)
                stats(b, c, h_ok, bst, bst_ok, mv, mv_ok)

            def tok_xn(b, c):
                dve.wait_ge(ln_ok, tiles(b, c))
                V.tensor_scalar(xn[:, :], hbuf[:, c % TS, :], mv[:, c % 2, 0:1], ln_r[:, c % 2:c % 2 + 1], ALU.subtract,
                                ALU.mult).then_inc(xn_ok, 1)

            def xn_split(b, c):
                dve.wait_ge(xns_hi, tiles(b, c))
                V.tensor_tensor(xns[:, 1, :], xn[:, :], xns[:, 0, :], ALU.subtract).then_inc(xns_lo, 1)

            def v_split(b, c):
                t = c % TM
                dve.wait_ge(v_hi, tiles(b, c))
                V.scalar_tensor_tensor(vs[:, 1, t, :], v_bank(c)[:, :], SQ / (SX * SW), vs[:, 0, t, :], ALU.mult,
                                       ALU.subtract).then_inc(v_lo, 1)

            def silu(b, c0, j):
                dst = qk32[:, j % 2, :]
                dve.wait_ge(th_ok, blocks(b, c0, j))
                if j >= 2:
                    dve.wait_ge(qk_hi, blocks(b, c0, j - 2))
                V.scalar_tensor_tensor(dst, th[:, j % 2, :], 1.0, qk_bank(j)[:, :], ALU.add, ALU.mult).then_inc(qk32_ok, 1)

            def qk_split(b, c0, j):
                dst, src = (kT, qT)[j // H], qk32[:, j % 2, :]
                dve.wait_ge(qk_hi, blocks(b, c0, j))
                V.scalar_tensor_tensor(dst[:, 1, j % H, :], src, SQ / (2 * SX * SW), dst[:, 0, j % H, :], ALU.mult,
                                       ALU.subtract).then_inc(qk_lo, 1)

            def log_decay_begin(b, c0):
                m = macros(b, c0)
                dve.wait_ge(v_mm, tiles(b, c0 + 3))
                V.tensor_reduce(z[:, :], f_ps.rearrange("p t (h g) -> p (t h) g", g=2), AX.X, ALU.add).then_inc(z_ok, 1)
                dve.wait_ge(z_ok, m)
                V.tensor_scalar(zm[:, :], z[:, :], SP / (SX * SW), 0.0, ALU.mult, ALU.min).then_inc(zm_ok, 1)

            def log_decay_end(b, c0):
                m = macros(b, c0)
                dve.wait_ge(zl_ok, m)
                dve.wait_ge(zm_ok, m)
                V.scalar_tensor_tensor(ld[:, :], zl[:, :], -SP, zm[:, :], ALU.mult, ALU.add).then_inc(ld_ok, 1)
                ld_v = ld[:, :].rearrange("p (t h) -> p t h", t=TM)
                dve.wait_ge(ld_ok, m)
                V.tensor_copy(ldp[:, :, :, 0], ld_v).then_inc(ldp_hi, 1)
                dve.wait_ge(ldp_hi, m)
                V.tensor_tensor(ldp[:, :, :, 1], ld_v, ldp[:, :, :, 0], ALU.subtract).then_inc(ldp_ok, 1)

            def decay_sums(b, c0):
                m = macros(b, c0)
                dve.wait_ge(cum_mm, m)
                V.tensor_reduce(ct[:, 0:2, :, :].rearrange("p a t h -> p (a t h)"),
                                ct_ps.rearrange("p (a g) -> p a g", g=2), AX.X, ALU.add).then_inc(ct_sums, 1)
                dve.wait_ge(ct_sums, m)
                V.tensor_tensor(ct[:, 2, :, :], ct[:, 1, :, :], ct[:, 0, :, :], ALU.subtract).then_inc(ct_ok, 1)

            def oT_split(b, c):
                dve.wait_ge(oT_hi, tiles(b, c))
                V.tensor_tensor(oT[:, 1, :, :], k_t(on_ps), oT[:, 0, :, :], ALU.subtract).then_inc(oT_lo, 1)

            def attn_residual(b, c, bank):
                dve.wait_ge(wo_mm, tiles(b, c))
                V.scalar_tensor_tensor(hbuf[:, c % TS, :], bank[:, :], 1.0 / (SX * SW), hbuf[:, c % TS, :], ALU.mult,
                                       ALU.add).then_inc(h2_ok, 1)
                stats(b, c, h2_ok, bst2, bst2_ok, mv2, mv2_ok)

            def quantise_begin(b, c):
                i = slice(c % 2, c % 2 + 1)
                dve.wait_ge(ln2_ok, tiles(b, c))
                V.tensor_scalar(xn2[:, :], hbuf[:, c % TS, :], mv2[:, c % 2, 0:1], ln2_r[:, i], ALU.subtract,
                                ALU.mult).then_inc(xn2_ok, 1)
                dve.wait_ge(xn2_ok, tiles(b, c))
                V.tensor_reduce(amax[:, i], xn2[:, :], AX.X, ALU.max, apply_absolute_value=True).then_inc(amax_ok, 1)
                dve.wait_ge(amax_ok, tiles(b, c))
                V.tensor_scalar(beta[:, i], amax[:, i], 1.0 / 127.0, Q_EPS, ALU.mult, ALU.max).then_inc(beta_ok, 1)
                dve.wait_ge(beta_ok, tiles(b, c))
                V.reciprocal(binv[:, i], beta[:, i]).then_inc(binv_ok, 1)
                V.tensor_scalar(ab[:, i], beta[:, i], alpha[:, :], None, ALU.mult).then_inc(ab_ok, 1)

            def quantise_end(b, c):
                i = slice(c % 2, c % 2 + 1)
                dve.wait_ge(binv_ok, tiles(b, c))
                V.tensor_scalar(xn2[:, :], xn2[:, :], binv[:, i], MAGIC, ALU.mult, ALU.add).then_inc(round_ok, 1)
                dve.wait_ge(round_ok, tiles(b, c))
                if not isinstance(b, int) or TS * b + c >= 1:
                    dve.wait_ge(xqT_ok, 16 * tiles(b, c - 1))
                V.tensor_scalar(yq[:, :], xn2[:, :], MAGIC, None, ALU.subtract).then_inc(yq_ok, 1)

            def ffn_residual(b, c, bank):
                dve.wait_ge(ffn_mm, tiles(b, c))
                dve.wait_ge(ab_ok, tiles(b, c))
                if c >= 2:
                    dve.wait_ge(stored[c % 2], dmas(b, c - 2, 2, 16))
                V.scalar_tensor_tensor(obuf[:, c % 2, :], bank[:, :], ab[:, c % 2:c % 2 + 1], hbuf[:, c % TS, :], ALU.mult,
                                       ALU.add).then_inc(out_ok, 1)

            def ffn_weights():
                dve.wait_ge(wabs_mm, 1)
                V.tensor_scalar(alpha[:, :], dcs[:, 0:1], 1.0 / (D * D), Q_EPS, ALU.mult, ALU.max).then_inc(alpha_step, 1)
                dve.wait_ge(alpha_step, 1)
                V.reciprocal(ainv[:, :], alpha[:, :]).then_inc(alpha_step, 1)
                dve.wait_ge(alpha_step, 2)
                for k in range(KD):
                    v = stage(NW + k)
                    V.tensor_scalar(v, v, ainv[:, :], MAGIC, ALU.mult, ALU.add).then_inc(fq_step, 1)
                    dve.wait_ge(fq_step, 2 * k + 1)
                    V.tensor_scalar(v, v, MAGIC, 1.0, ALU.subtract, ALU.min).then_inc(fq_step, 1)

            def ternary(lo, hi):
                for k in range(lo, hi):
                    dve.wait_ge(fq_tr, k + 1)
                    V.tensor_scalar(wffn[:, :, k * P:(k + 1) * P], k_t((fq_ps, dcs)[k % 2]), -1.0, None,
                                    ALU.max).then_inc(fq_ok, 1)

            def add_k(b, c):
                t = c % TM
                if t >= 1:
                    dve.wait_ge(kd32_ok, tiles(b, c - 1))
                V.tensor_tensor(ksum[:, :, :], ktok[:, 0, t, :, :], ktok[:, 1, t, :, :], ALU.add).then_inc(k_sum, 1)

            def wo_split():
                dve.wait_ge(wo_in, 16 * KD)
                for k in range(KD):
                    V.tensor_scalar(wo_stage[k], wo_stage[k], norma[:, k:k + 1], None, ALU.mult).then_inc(w_scaled, 1)
                for k in range(KD):
                    dve.wait_ge(wo_hi, k + 1)
                    V.scalar_tensor_tensor(wo[:, 1, k, :], wo_stage[k], SW, wo[:, 0, k, :], ALU.mult, ALU.subtract).then_inc(wo_lo, 1)

            def q_phase(b, c0, prev, nxt):
                if prev:
                    tok_norm(b, c0 + 3)
                v_split(b, c0)
                if prev:
                    oT_split(b, c0 - 1)
                    tok_xn(b, c0 + 3)
                xn_split(b, c0 + 3)
                v_split(b, c0 + 1)
                if prev:
                    attn_residual(b, c0 - 1, dcs)
                if not prev:
                    ffn_weights()
                v_split(b, c0 + 2)
                if prev:
                    ffn_residual(b, c0 - 2, dcs)
                    quantise_begin(b, c0 - 1)
                    quantise_end(b, c0 - 1)
                v_split(b, c0 + 3)
                if not prev:
                    wo_split()
                log_decay_begin(b, c0)
                for j in range(2 * H):
                    silu(b, c0, j)
                    if nxt and j in (3, 4):
                        cat_split(b, c0 + TM, j - 3)
                    if j == 5 and prev:
                        ffn_residual(b, c0 - 1, dcs)
                    qk_split(b, c0, j)
                    if j == 1 and not prev:
                        ternary(0, 2)
                    if j == 3 and not prev:
                        ternary(2, KD)
                    if j == 2:
                        log_decay_end(b, c0)
                    if j == 5:
                        decay_sums(b, c0)
                if c0 == TS:
                    dve.wait_ge(stored[0], dmas(b, c0 - 2, 2, 16))
                    dve.wait_ge(stored[1], dmas(b, c0 - 1, 2, 16))

            def a_phase(b, c0, nxt):
                for t in range(TM):
                    c, n = c0 + t, c0 + t + TM
                    if t == 0:
                        dve.wait_ge(ktok_ok, 32 * H * macros(b, c))
                        add_k(b, c)
                    dve.wait_ge(k_sum, tiles(b, c))
                    dve.wait_ge(ex_ok, macros(b, c))
                    V.tensor_tensor(kd32[:, :, :], ksum[:, :, :], ex[:, 2, t, :].unsqueeze(2).to_broadcast([P, H, P]),
                                    ALU.mult).then_inc(kd32_ok, 1)
                    if t >= 1:
                        oT_split(b, c - 1)
                    if nxt:
                        cat_split(b, n, 1 if t >= 1 else 2)
                    dve.wait_ge(sc_mm, tiles(b, c))
                    dve.wait_ge(dec_ok, tiles(b, c))
                    V.scalar_tensor_tensor(p32[:, :], sco[:, :], SP / SQ ** 2, dec[:, :, :].rearrange("p h i -> p (h i)"),
                                           ALU.mult, ALU.mult).then_inc(p32_ok, 1)
                    if t < TM - 1:
                        add_k(b, c + 1)
                    if nxt and t >= 1:
                        cat_split(b, n, 2)
                    if nxt and t >= 1:
                        tok_norm(b, n - 1)
                    if t >= 1:
                        attn_residual(b, c - 1, mmb)
                    if nxt and t < TM - 1:
                        cat_split(b, n + 1, 0)
                    if nxt and t >= 1:
                        tok_xn(b, n - 1)
                    dve.wait_ge(att_mm, tiles(b, c))
                    st_v = st32[:, :, :].rearrange("p h f -> p (h f)")
                    if c % TS == 0:
                        V.tensor_scalar(st_v, dcs[:, :], SP / SQ ** 2, None, ALU.mult).then_inc(st32_ok, 1)
                        V.tensor_copy(o32[:, :], sco[:, :]).then_inc(o32_ok, 1)
                    else:
                        if c % TS != TS - 1:
                            dve.wait_ge(stdec_ok, (TS - 2) * b + c)
                            V.scalar_tensor_tensor(st_v, dcs[:, :], SP / SQ ** 2, stdec[:, :, :].rearrange("p h f -> p (h f)"),
                                                   ALU.mult, ALU.add).then_inc(st32_ok, 1)
                        dve.wait_ge(ointer_ok, states(b, c))
                        V.tensor_tensor(o32[:, :], sco[:, :], ointer[:, :, :].rearrange("p h f -> p (h f)"),
                                        ALU.add).then_inc(o32_ok, 1)
                    if nxt and t >= 1:
                        xn_split(b, n - 1)
                    if t >= 1:
                        quantise_begin(b, c - 1)
                    if nxt:
                        tok_out(b, n)
                    if t >= 1:
                        quantise_end(b, c - 1)
                    if t >= 2:
                        ffn_residual(b, c - 2, ffn_bank(nxt))

            made = [0]

            def step(ins):
                made[0] += 1
                ins.then_inc(hash_step, 1)
                dve.wait_ge(hash_step, made[0])

            def mod_ngv(r, v, q):
                step(V.tensor_scalar(q, v, 1.0 / NGV, MAGIC, ALU.mult, ALU.add))
                step(V.tensor_scalar(q, q, MAGIC, -float(NGV), ALU.subtract, ALU.mult))
                step(V.tensor_tensor(r, q, v, ALU.add))
                step(V.tensor_scalar(q, r, 0.0, float(NGV), ALU.is_lt, ALU.mult))
                step(V.tensor_tensor(r, r, q, ALU.add))

            W2 = P + 2
            dve.wait_ge(x_in, 16 * (NB + 1))
            step(V.tensor_copy(xf[:, :], xi[:, :]))
            step(V.tensor_scalar(feat[:, 0, :], xf[:, 2:], float(VOCAB - 1), 0.0, ALU.min, ALU.max))
            mod_ngv(hw[:, 0, :], xf[:, :], hw[:, 1, :])
            dve.wait_ge(feat_tr, 1)
            V.tensor_copy(idx[:, :, 0], sco[:, 0:NT]).then_inc(idx_ok, 1)
            step(V.scalar_tensor_tensor(hw[:, 2, 1:W2], hw[:, 0, 0:W2 - 1], 131.0, xf[:, 1:W2], ALU.mult, ALU.add))
            mod_ngv(hw[:, 3, 1:W2], hw[:, 2, 1:W2], hw[:, 1, 1:W2])
            step(V.tensor_copy(feat[:, 1, :], hw[:, 3, 2:W2]))
            step(V.scalar_tensor_tensor(hw[:, 2, 2:W2], hw[:, 3, 1:W2 - 1], 131.0, xf[:, 2:W2], ALU.mult, ALU.add))
            mod_ngv(feat[:, 2, :], hw[:, 2, 2:W2], hw[:, 1, 2:W2])
            assert made[0] == HASH_STEPS
            dve.wait_ge(feat_tr, 2)
            V.tensor_copy(idx[:, :, 1:NG].rearrange("p n g -> p g n"),
                          dcs[:, NT:NG * NT].rearrange("p (g n) -> p g n", g=NG - 1)).then_inc(idx_ok, 1)

            w_split(0, 2 * KD)
            cat_split(0, 0, 0)
            cat_split(0, 0, 1)
            w_split(2 * KD, 3 * KD)
            cat_split(0, 0, 2)
            cat_split(0, 1, 0)
            dve.wait_ge(small_in, 64)
            dve.wait_ge(wf_hi, 1)
            V.scalar_tensor_tensor(wf[:, :, :, 1], wf32[:, :, :], SW, wf[:, :, :, 0], ALU.mult, ALU.subtract).then_inc(wf_lo, 1)
            for c in range(1, TM):
                cat_split(0, c, 1)
                tok_out(0, c - 1)
                tok_norm(0, c - 1)
                cat_split(0, c, 2)
                tok_xn(0, c - 1)
                if c < TM - 1:
                    cat_split(0, c + 1, 0)
                w_split(CUTS[c - 1], CUTS[c])
                xn_split(0, c - 1)
            for k in range(KD):
                dve.wait_ge(w_in[k], 16 * (NW // NSTG + 1))
            V.tensor_reduce(wabs[:, :], ktok32[:, :, :].rearrange("p k d -> p (k d)"), AX.X, ALU.add,
                            apply_absolute_value=True).then_inc(wabs_ok, 1)
            tok_out(0, TM - 1)
            tok_norm(0, TM - 1)
            tok_xn(0, TM - 1)
            q_phase(0, 0, False, True)
            with dve.Fori(0, NB - 1) as b:
                a_phase(b, 0, True)
                q_phase(b, TM, True, True)
                a_phase(b, TM, True)
                q_phase(b, 2 * TM, True, True)
            b = NB - 1
            a_phase(b, 0, True)
            q_phase(b, TM, True, False)
            a_phase(b, TM, False)
            oT_split(b, TS - 1)
            attn_residual(b, TS - 1, mmb)
            ffn_residual(b, TS - 2, mma)
            quantise_begin(b, TS - 1)
            quantise_end(b, TS - 1)
            ffn_residual(b, TS - 1, sco)


_INS = ["x", "L0_tok_unigram_table", "L0_tok_ngram_table", "L0_tok_W", "L0_tok_b", "L0_tok_norm_w", "L0_attn_Wq",
        "L0_attn_Wk", "L0_attn_Wv", "L0_attn_Wf", "L0_attn_Wo", "L0_attn_norm_w", "L0_ffn_weight"]


def kernel(**inputs):
    import numpy as _np
    import concourse.bacc as _bacc
    from concourse import mybir as _mybir
    from concourse.bass_utils import run_bass_kernel_spmd as _run

    nc = _bacc.Bacc("TRN2", target_bir_lowering=False, num_devices=1)
    arrays, args = {}, []
    for name in _INS:
        a = _np.ascontiguousarray(inputs[name])
        arrays[f"in_{name}_dram"] = a
        args.append(nc.dram_tensor(f"in_{name}_dram", a.shape, _mybir.dt.from_np(a.dtype), kind="ExternalInput").ap())
    shape = (*inputs["x"].shape, inputs["L0_ffn_weight"].shape[0])
    args.append(nc.dram_tensor("out_0_dram", shape, _mybir.dt.float32, kind="ExternalOutput").ap())
    lm_tower_kernel(nc, *args)
    r = _run(nc, [arrays], core_ids=[0])
    return r.results[0]["out_0_dram"]
```
